# Optimizing a Trainium2 kernel written in Bass

```python
import numpy as np
import jax
import jax.numpy as jnp

def _softmax(x, axis=-1):
    return jax.nn.softmax(x, axis=axis)

def _gelu(x):
    return jax.nn.gelu(x, approximate=True)

def _silu(x):
    return jax.nn.silu(x)

def _sigmoid(x):
    return jax.nn.sigmoid(x)

def _layernorm(x, axis=-1, eps=1e-05):
    m = jnp.mean(x, axis=axis, keepdims=True)
    v = jnp.var(x, axis=axis, keepdims=True)
    return (x - m) / jnp.sqrt(v + eps)

def _scatter_add(tgt, idx, src, axis=0):
    return tgt.at[idx].add(src)

def _segment_sum(src, seg, n):
    return jax.ops.segment_sum(src, seg, n)
kernel_name = 'mk_macaron_d4_jaxref_r8_9ecdd6'

def setup_inputs(seed: int=0):
    np.random.seed(seed)
    _w = jnp.asarray

    def _L0_attn_setup():
        import jax, jax.numpy as jnp
        import numpy as np
        import math
        EMB = 128
        HEADS = 16
        B, S = (2, 256)
        key = jax.random.key(seed)
        k_x, k_wq, k_bq, k_wu, k_bu = jax.random.split(key, 5)
        lim = 1.0 / math.sqrt(EMB)
        x = jax.random.normal(k_x, (B, S, EMB), dtype=jnp.float32)
        wq = jax.random.uniform(k_wq, (EMB, EMB), jnp.float32, -lim, lim)
        bq = jax.random.uniform(k_bq, (EMB,), jnp.float32, -lim, lim)
        wu = jax.random.uniform(k_wu, (EMB, EMB), jnp.float32, -lim, lim)
        bu = jax.random.uniform(k_bu, (EMB,), jnp.float32, -lim, lim)
        return {'x': x, 'wq': wq, 'bq': bq, 'wu': wu, 'bu': bu}
    _L0_attn_in = _L0_attn_setup()

    def _L0_ffn_setup():
        import jax, jax.numpy as jnp
        import numpy as np
        B, L, M = (4, 256, 128)
        G, E = (8, 8)
        CAP_FACTOR = 2.0

        def _ffn_size(m, widening=8.0):
            f = int(widening * m) * 2 // 3
            return f + (8 - f) % 8
        H = _ffn_size(M)

        def _gating_top2(logits, C):
            Gd, Sd, Ed = logits.shape
            raw = jax.nn.softmax(logits, axis=-1)
            idx1 = jnp.argmax(raw, axis=-1)
            m1 = jax.nn.one_hot(idx1, Ed, dtype=logits.dtype)
            gate1 = jnp.sum(raw * m1, axis=-1)
            rest = raw * (1.0 - m1)
            idx2 = jnp.argmax(rest, axis=-1)
            m2 = jax.nn.one_hot(idx2, Ed, dtype=logits.dtype)
            gate2 = jnp.sum(rest * m2, axis=-1)
            p1 = jnp.cumsum(m1, axis=-2) - m1
            m1 = m1 * (p1 < C).astype(m1.dtype)
            p1 = jnp.sum(p1 * m1, axis=-1)
            m1_flat = jnp.sum(m1, axis=-1)
            m1_count = jnp.sum(m1, axis=-2)
            p2 = jnp.cumsum(m2, axis=-2) - m2 + m1_count[:, None, :]
            m2 = m2 * (p2 < C).astype(m2.dtype)
            p2 = jnp.sum(p2 * m2, axis=-1)
            m2_flat = jnp.sum(m2, axis=-1)
            gate1 = gate1 * m1_flat
            gate2 = gate2 * m2_flat
            c1 = (gate1[..., None] * jax.nn.one_hot(idx1, Ed, dtype=jnp.float32))[..., None] * jax.nn.one_hot(p1.astype(jnp.int32), C, dtype=jnp.float32)[:, :, None, :]
            c2 = (gate2[..., None] * jax.nn.one_hot(idx2, Ed, dtype=jnp.float32))[..., None] * jax.nn.one_hot(p2.astype(jnp.int32), C, dtype=jnp.float32)[:, :, None, :]
            combine = (c1 + c2).astype(logits.dtype)
            dispatch = (combine != 0).astype(logits.dtype)
            return (dispatch, combine)
        key = jax.random.key(seed)
        k0, k1, k2, k3, k4 = jax.random.split(key, 5)
        return {'inputs': jax.random.normal(k0, (B, L, M), jnp.float32), 'router_w': jax.random.normal(k1, (M, E), jnp.float32) * 0.02, 'w0_kernel': jax.random.normal(k2, (E, M, H), jnp.float32) * 0.02, 'w1_kernel': jax.random.normal(k3, (E, M, H), jnp.float32) * 0.02, 'wo_kernel': jax.random.normal(k4, (E, H, M), jnp.float32) * 0.02}
    _L0_ffn_in = _L0_ffn_setup()

    def _L1_attn_setup():
        import jax, jax.numpy as jnp
        import numpy as np
        D = 128
        B = 4
        S = 512
        LN_EPS = 1e-05

        def _layer_norm(x, gamma, beta):
            mu = jnp.mean(x, axis=-1, keepdims=True)
            var = jnp.mean(jnp.square(x - mu), axis=-1, keepdims=True)
            return (x - mu) * jax.lax.rsqrt(var + LN_EPS) * gamma + beta
        key = jax.random.key(seed)
        ks = jax.random.split(key, 5)
        scale = 1.0 / np.sqrt(D)
        return {'hidden_states': jax.random.normal(ks[0], (B, S, D), dtype=jnp.float32), 'attention_mask': jnp.ones((B, S), dtype=jnp.int32), 'Wk': jax.random.normal(ks[1], (D, D), dtype=jnp.float32) * scale, 'bk': jnp.zeros((D,), dtype=jnp.float32), 'Wka': jax.random.normal(ks[2], (D, D), dtype=jnp.float32) * scale, 'bka': jnp.zeros((D,), dtype=jnp.float32), 'Wv': jax.random.normal(ks[3], (D, D), dtype=jnp.float32) * scale, 'bv': jnp.zeros((D,), dtype=jnp.float32), 'gamma': jnp.ones((D,), dtype=jnp.float32), 'beta': jnp.zeros((D,), dtype=jnp.float32)}
    _L1_attn_in = _L1_attn_setup()

    def _L1_ffn_setup():
        import jax, jax.numpy as jnp
        import numpy as np
        D_IN, D_HID = (128, 512)

        def _ternary(key, shape):
            return jax.random.randint(key, shape, -1, 2).astype(jnp.float32)

        def _tlin(x, w, s):
            return jnp.einsum('bsi,oi->bso', x, w) * s
        key = jax.random.key(seed)
        ks = jax.random.split(key, 12)
        inv = lambda fan: 1.0 / np.sqrt(fan).astype(np.float32)
        return {'x': jax.random.normal(ks[0], (4, 256, D_IN), dtype=jnp.float32), 'w1_w': _ternary(ks[1], (D_HID, D_IN)), 'w1_s': jax.random.uniform(ks[2], (D_HID,), dtype=jnp.float32) * inv(D_IN), 'w2_w': _ternary(ks[3], (D_HID, D_IN)), 'w2_s': jax.random.uniform(ks[4], (D_HID,), dtype=jnp.float32) * inv(D_IN), 'h1_w': _ternary(ks[5], (D_HID, D_HID)), 'h1_s': jax.random.uniform(ks[6], (D_HID,), dtype=jnp.float32) * inv(D_HID), 'h2_w': _ternary(ks[7], (D_HID, D_HID)), 'h2_s': jax.random.uniform(ks[8], (D_HID,), dtype=jnp.float32) * inv(D_HID), 'w3_w': _ternary(ks[9], (D_IN, D_HID)), 'w3_s': jax.random.uniform(ks[10], (D_IN,), dtype=jnp.float32) * inv(D_HID)}
    _L1_ffn_in = _L1_ffn_setup()

    def _L2_attn_setup():
        import jax, jax.numpy as jnp
        import numpy as np
        EMBED_DIM = 128
        NUM_HEADS = 16
        BATCH = 4
        SEQ = 512
        key = jax.random.key(seed)
        ks = jax.random.split(key, 5)
        scale = 0.02
        E = EMBED_DIM
        x = jax.random.normal(ks[0], (BATCH, SEQ, E), dtype=jnp.float32)
        Wq = jax.random.normal(ks[1], (E, E), dtype=jnp.float32) * scale
        Wk = jax.random.normal(ks[2], (E, E), dtype=jnp.float32) * scale
        Wv = jax.random.normal(ks[3], (E, E), dtype=jnp.float32) * scale
        Wo = jax.random.normal(ks[4], (E, E), dtype=jnp.float32) * scale
        z = jnp.zeros((E,), dtype=jnp.float32)
        return {'x': x, 'Wq': Wq, 'bq': z, 'Wk': Wk, 'bk': z, 'Wv': Wv, 'bv': z, 'Wo': Wo, 'bo': z}
    _L2_attn_in = _L2_attn_setup()

    def _L2_ffn_setup():
        import jax, jax.numpy as jnp
        import numpy as np
        B, S, H = (4, 256, 128)
        E = 8
        GS = 2
        NG = E // GS
        F = int(H * 4 * (2.0 / 3.0))
        key = jax.random.key(seed)
        ks = jax.random.split(key, 7)
        sc_h = 1.0 / np.sqrt(H)
        sc_f = 1.0 / np.sqrt(F)
        return {'x': jax.random.normal(ks[0], (B, S, H), dtype=jnp.float32), 'Wr': jax.random.normal(ks[1], (H, E), dtype=jnp.float32) * sc_h, 'br': jnp.zeros((E,), dtype=jnp.float32), 'W_up': jax.random.normal(ks[2], (NG, H, F), dtype=jnp.float32) * sc_h, 'b_up': jax.random.normal(ks[3], (NG, F), dtype=jnp.float32) * 0.01, 'W_down': jax.random.normal(ks[4], (E, F, H), dtype=jnp.float32) * sc_f, 'b_down': jax.random.normal(ks[5], (E, H), dtype=jnp.float32) * 0.01}
    _L2_ffn_in = _L2_ffn_setup()

    def _L3_attn_setup():
        import jax, jax.numpy as jnp
        import numpy as np
        HIDDEN = 128
        HEADS = 16
        HEAD_DIM = HIDDEN // HEADS
        BLOCK = 128
        B, S = (1, 512)

        def _ring_attention(q, k, v, block, scale):
            b, h, s, d = q.shape
            nb = s // block
            kb = jnp.moveaxis(k.reshape(b, h, nb, block, d), 2, 0)
            vb = jnp.moveaxis(v.reshape(b, h, nb, block, d), 2, 0)

            def step(carry, kv):
                num, den = carry
                k_blk, v_blk = kv
                s_blk = jnp.einsum('bhqd,bhkd->bhqk', q, k_blk) * scale
                m = jnp.max(s_blk, axis=-1, keepdims=True)
                e = jnp.exp(s_blk - m)
                num = num + jnp.einsum('bhqk,bhkd->bhqd', e, v_blk)
                den = den + jnp.sum(e, axis=-1, keepdims=True)
                return ((num, den), None)
            init = (jnp.zeros_like(q), jnp.zeros((b, h, s, 1), dtype=q.dtype))
            (num, den), _ = jax.lax.scan(step, init, (kb, vb))
            return num / den
        key = jax.random.key(seed)
        k0, k1, k2, k3, k4 = jax.random.split(key, 5)
        w_scale = 0.02
        return {'hidden_states': jax.random.normal(k0, (B, S, HIDDEN), dtype=jnp.float32), 'w_q': jax.random.normal(k1, (HIDDEN, HIDDEN), dtype=jnp.float32) * w_scale, 'w_k': jax.random.normal(k2, (HIDDEN, HIDDEN), dtype=jnp.float32) * w_scale, 'w_v': jax.random.normal(k3, (HIDDEN, HIDDEN), dtype=jnp.float32) * w_scale, 'w_o': jax.random.normal(k4, (HIDDEN, HIDDEN), dtype=jnp.float32) * w_scale}
    _L3_attn_in = _L3_attn_setup()

    def _L3_ffn_setup():
        import jax, jax.numpy as jnp
        import numpy as np
        B, S, D, E = (4, 256, 128, 8)
        key = jax.random.key(seed)
        ks = jax.random.split(key, 5)
        s = 0.02
        return {'hidden_states': jax.random.normal(ks[0], (B, S, D), dtype=jnp.float32), 'Wr': jax.random.normal(ks[1], (D, E), dtype=jnp.float32) * s, 'br': jnp.zeros((E,), dtype=jnp.float32), 'W1': jax.random.normal(ks[2], (E, D, 4 * D), dtype=jnp.float32) * s, 'b1': jnp.zeros((E, 4 * D), dtype=jnp.float32), 'W2': jax.random.normal(ks[3], (E, 4 * D, 2 * D), dtype=jnp.float32) * s, 'b2': jnp.zeros((E, 2 * D), dtype=jnp.float32), 'W3': jax.random.normal(ks[4], (E, 2 * D, D), dtype=jnp.float32) * s, 'b3': jnp.zeros((E, D), dtype=jnp.float32)}
    _L3_ffn_in = _L3_ffn_setup()
    _d = {'L0_attn_x': _L0_attn_in['x'], 'L0_attn_wq': _L0_attn_in['wq'], 'L0_attn_bq': _L0_attn_in['bq'], 'L0_attn_wu': _L0_attn_in['wu'], 'L0_attn_bu': _L0_attn_in['bu'], 'L0_ffn_router_w': _L0_ffn_in['router_w'], 'L0_ffn_w0_kernel': _L0_ffn_in['w0_kernel'], 'L0_ffn_w1_kernel': _L0_ffn_in['w1_kernel'], 'L0_ffn_wo_kernel': _L0_ffn_in['wo_kernel'], 'L1_attn_attention_mask': _L1_attn_in['attention_mask'], 'L1_attn_Wk': _L1_attn_in['Wk'], 'L1_attn_bk': _L1_attn_in['bk'], 'L1_attn_Wka': _L1_attn_in['Wka'], 'L1_attn_bka': _L1_attn_in['bka'], 'L1_attn_Wv': _L1_attn_in['Wv'], 'L1_attn_bv': _L1_attn_in['bv'], 'L1_attn_gamma': _L1_attn_in['gamma'], 'L1_attn_beta': _L1_attn_in['beta'], 'L1_ffn_w1_w': _L1_ffn_in['w1_w'], 'L1_ffn_w1_s': _L1_ffn_in['w1_s'], 'L1_ffn_w2_w': _L1_ffn_in['w2_w'], 'L1_ffn_w2_s': _L1_ffn_in['w2_s'], 'L1_ffn_h1_w': _L1_ffn_in['h1_w'], 'L1_ffn_h1_s': _L1_ffn_in['h1_s'], 'L1_ffn_h2_w': _L1_ffn_in['h2_w'], 'L1_ffn_h2_s': _L1_ffn_in['h2_s'], 'L1_ffn_w3_w': _L1_ffn_in['w3_w'], 'L1_ffn_w3_s': _L1_ffn_in['w3_s'], 'L2_attn_Wq': _L2_attn_in['Wq'], 'L2_attn_bq': _L2_attn_in['bq'], 'L2_attn_Wk': _L2_attn_in['Wk'], 'L2_attn_bk': _L2_attn_in['bk'], 'L2_attn_Wv': _L2_attn_in['Wv'], 'L2_attn_bv': _L2_attn_in['bv'], 'L2_attn_Wo': _L2_attn_in['Wo'], 'L2_attn_bo': _L2_attn_in['bo'], 'L2_ffn_Wr': _L2_ffn_in['Wr'], 'L2_ffn_br': _L2_ffn_in['br'], 'L2_ffn_W_up': _L2_ffn_in['W_up'], 'L2_ffn_b_up': _L2_ffn_in['b_up'], 'L2_ffn_W_down': _L2_ffn_in['W_down'], 'L2_ffn_b_down': _L2_ffn_in['b_down'], 'L3_attn_w_q': _L3_attn_in['w_q'], 'L3_attn_w_k': _L3_attn_in['w_k'], 'L3_attn_w_v': _L3_attn_in['w_v'], 'L3_attn_w_o': _L3_attn_in['w_o'], 'L3_ffn_Wr': _L3_ffn_in['Wr'], 'L3_ffn_br': _L3_ffn_in['br'], 'L3_ffn_W1': _L3_ffn_in['W1'], 'L3_ffn_b1': _L3_ffn_in['b1'], 'L3_ffn_W2': _L3_ffn_in['W2'], 'L3_ffn_b2': _L3_ffn_in['b2'], 'L3_ffn_W3': _L3_ffn_in['W3'], 'L3_ffn_b3': _L3_ffn_in['b3']}
    _x0 = _d['L0_attn_x']
    _d['L0_attn_x'] = jax.random.normal(jax.random.fold_in(jax.random.key(seed), 1), (4, 512, 128), dtype=_x0.dtype)
    del _x0
    return _d

def reference(L0_attn_x, L0_attn_wq, L0_attn_bq, L0_attn_wu, L0_attn_bu, L0_ffn_router_w, L0_ffn_w0_kernel, L0_ffn_w1_kernel, L0_ffn_wo_kernel, L1_attn_attention_mask, L1_attn_Wk, L1_attn_bk, L1_attn_Wka, L1_attn_bka, L1_attn_Wv, L1_attn_bv, L1_attn_gamma, L1_attn_beta, L1_ffn_w1_w, L1_ffn_w1_s, L1_ffn_w2_w, L1_ffn_w2_s, L1_ffn_h1_w, L1_ffn_h1_s, L1_ffn_h2_w, L1_ffn_h2_s, L1_ffn_w3_w, L1_ffn_w3_s, L2_attn_Wq, L2_attn_bq, L2_attn_Wk, L2_attn_bk, L2_attn_Wv, L2_attn_bv, L2_attn_Wo, L2_attn_bo, L2_ffn_Wr, L2_ffn_br, L2_ffn_W_up, L2_ffn_b_up, L2_ffn_W_down, L2_ffn_b_down, L3_attn_w_q, L3_attn_w_k, L3_attn_w_v, L3_attn_w_o, L3_ffn_Wr, L3_ffn_br, L3_ffn_W1, L3_ffn_b1, L3_ffn_W2, L3_ffn_b2, L3_ffn_W3, L3_ffn_b3):

    def _L0_attn_ref(x, wq, bq, wu, bu):
        import jax, jax.numpy as jnp
        import numpy as np
        import math
        EMB = 128
        HEADS = 16
        B, S = (2, 256)
        b, s, emb = x.shape
        hd = emb // HEADS
        q = jnp.einsum('bse,oe->bso', x, wq) + bq
        qh = q.reshape(HEADS, b, s, hd)
        kh = qh
        vh = qh
        scale = 1.0 / math.sqrt(emb)
        scores = jnp.einsum('hbqd,hbkd->hbqk', qh, kh) * scale
        attn = jax.nn.softmax(scores, axis=-1)
        out = jnp.einsum('hbqk,hbkd->hbqd', attn, vh)
        out = out.reshape(b, s, emb)
        return jnp.einsum('bse,oe->bso', out, wu) + bu

    def _L0_ffn_ref(inputs, router_w, w0_kernel, w1_kernel, wo_kernel):
        import jax, jax.numpy as jnp
        import numpy as np
        B, L, M = (4, 256, 128)
        G, E = (8, 8)
        CAP_FACTOR = 2.0

        def _ffn_size(m, widening=8.0):
            f = int(widening * m) * 2 // 3
            return f + (8 - f) % 8
        H = _ffn_size(M)

        def _gating_top2(logits, C):
            Gd, Sd, Ed = logits.shape
            raw = jax.nn.softmax(logits, axis=-1)
            idx1 = jnp.argmax(raw, axis=-1)
            m1 = jax.nn.one_hot(idx1, Ed, dtype=logits.dtype)
            gate1 = jnp.sum(raw * m1, axis=-1)
            rest = raw * (1.0 - m1)
            idx2 = jnp.argmax(rest, axis=-1)
            m2 = jax.nn.one_hot(idx2, Ed, dtype=logits.dtype)
            gate2 = jnp.sum(rest * m2, axis=-1)
            p1 = jnp.cumsum(m1, axis=-2) - m1
            m1 = m1 * (p1 < C).astype(m1.dtype)
            p1 = jnp.sum(p1 * m1, axis=-1)
            m1_flat = jnp.sum(m1, axis=-1)
            m1_count = jnp.sum(m1, axis=-2)
            p2 = jnp.cumsum(m2, axis=-2) - m2 + m1_count[:, None, :]
            m2 = m2 * (p2 < C).astype(m2.dtype)
            p2 = jnp.sum(p2 * m2, axis=-1)
            m2_flat = jnp.sum(m2, axis=-1)
            gate1 = gate1 * m1_flat
            gate2 = gate2 * m2_flat
            c1 = (gate1[..., None] * jax.nn.one_hot(idx1, Ed, dtype=jnp.float32))[..., None] * jax.nn.one_hot(p1.astype(jnp.int32), C, dtype=jnp.float32)[:, :, None, :]
            c2 = (gate2[..., None] * jax.nn.one_hot(idx2, Ed, dtype=jnp.float32))[..., None] * jax.nn.one_hot(p2.astype(jnp.int32), C, dtype=jnp.float32)[:, :, None, :]
            combine = (c1 + c2).astype(logits.dtype)
            dispatch = (combine != 0).astype(logits.dtype)
            return (dispatch, combine)
        Bb, Ll, Mm = inputs.shape
        S = Bb * Ll // G
        x = inputs.reshape(G, S, Mm)
        logits = jnp.einsum('GSM,ME->GSE', x, router_w)
        cap = int(CAP_FACTOR * S / E)
        C = (cap + 3) // 4 * 4
        dispatch, combine = _gating_top2(logits, C)
        expert_inputs = jnp.einsum('GSEC,GSM->EGCM', dispatch, x)
        layer_w0 = jnp.einsum('EGCM,EMH->EGCH', expert_inputs, w0_kernel)
        layer_w1 = jnp.einsum('EGCM,EMH->EGCH', expert_inputs, w1_kernel)
        hidden = jax.nn.gelu(layer_w0, approximate=True) * layer_w1
        expert_outputs = jnp.einsum('EGCH,EHM->EGCM', hidden, wo_kernel)
        out = jnp.einsum('EGCM,GSEC->GSM', expert_outputs, combine)
        return out.reshape(Bb, Ll, Mm)

    def _L1_attn_ref(hidden_states, attention_mask, Wk, bk, Wka, bka, Wv, bv, gamma, beta):
        import jax, jax.numpy as jnp
        import numpy as np
        D = 128
        B = 4
        S = 512
        LN_EPS = 1e-05

        def _layer_norm(x, gamma, beta):
            mu = jnp.mean(x, axis=-1, keepdims=True)
            var = jnp.mean(jnp.square(x - mu), axis=-1, keepdims=True)
            return (x - mu) * jax.lax.rsqrt(var + LN_EPS) * gamma + beta
        h = _layer_norm(hidden_states, gamma, beta)
        d_model = h.shape[-1]
        keys = jnp.einsum('bsd,ed->bse', h, Wk) + bk
        values = jnp.einsum('bsd,ed->bse', h, Wv) + bv
        key_att = jnp.einsum('bsd,ed->bse', keys, Wka) + bka
        keys_weight = jnp.exp(key_att / jnp.sqrt(jnp.asarray(d_model, h.dtype)))
        keys_weight = keys_weight / jnp.cumsum(keys_weight, axis=1)
        pooled_keys = jnp.cumsum(keys_weight * keys, axis=1)
        return pooled_keys * values

    def _L1_ffn_ref(x, w1_w, w1_s, w2_w, w2_s, h1_w, h1_s, h2_w, h2_s, w3_w, w3_s):
        import jax, jax.numpy as jnp
        import numpy as np
        D_IN, D_HID = (128, 512)

        def _ternary(key, shape):
            return jax.random.randint(key, shape, -1, 2).astype(jnp.float32)

        def _tlin(x, w, s):
            return jnp.einsum('bsi,oi->bso', x, w) * s
        h = jax.nn.silu(_tlin(x, w1_w, w1_s)) * _tlin(x, w2_w, w2_s)
        h = jax.nn.gelu(_tlin(h, h1_w, h1_s), approximate=False)
        h = jax.nn.gelu(_tlin(h, h2_w, h2_s), approximate=False)
        return _tlin(h, w3_w, w3_s)

    def _L2_attn_ref(x, Wq, bq, Wk, bk, Wv, bv, Wo, bo):
        import jax, jax.numpy as jnp
        import numpy as np
        EMBED_DIM = 128
        NUM_HEADS = 16
        BATCH = 4
        SEQ = 512
        B, S, E = x.shape
        H = NUM_HEADS
        D = E // H

        def proj(W, b):
            return (jnp.einsum('bse,fe->bsf', x, W) + b).reshape(B, S, H, D)
        q = jax.nn.elu(proj(Wq, bq)) + 1.0
        k = jax.nn.elu(proj(Wk, bk)) + 1.0
        v = proj(Wv, bv)
        kv = jnp.einsum('bshd,bshe->bhde', k, v)
        out = jnp.einsum('bshd,bhde->bshe', q, kv).reshape(B, S, E)
        out = jnp.einsum('bse,fe->bsf', out, Wo) + bo
        return out

    def _L2_ffn_ref(x, Wr, br, W_up, b_up, W_down, b_down):
        import jax, jax.numpy as jnp
        import numpy as np
        B, S, H = (4, 256, 128)
        E = 8
        GS = 2
        NG = E // GS
        F = int(H * 4 * (2.0 / 3.0))
        b, s, h = x.shape
        n_tok = b * s
        k = n_tok // E
        xf = x.reshape(n_tok, h)
        logits = xf @ Wr + br
        Sm = jax.nn.softmax(logits, axis=-1)
        G_t, idx_t = jax.lax.top_k(Sm.T, k)
        G = G_t.T
        idx = idx_t.T
        tokens = xf[idx]
        group = jnp.arange(E) // GS
        Wu = W_up[group]
        bu = b_up[group]
        mid = jax.nn.silu(jnp.einsum('keh,ehf->kef', tokens, Wu) + bu)
        out = jnp.einsum('kef,efh->keh', mid, W_down) + b_down
        y = jnp.zeros_like(xf).at[idx].add(G[..., None] * out)
        return y.reshape(b, s, h)

    def _L3_attn_ref(hidden_states, w_q, w_k, w_v, w_o):
        import jax, jax.numpy as jnp
        import numpy as np
        HIDDEN = 128
        HEADS = 16
        HEAD_DIM = HIDDEN // HEADS
        BLOCK = 128
        B, S = (1, 512)

        def _ring_attention(q, k, v, block, scale):
            b, h, s, d = q.shape
            nb = s // block
            kb = jnp.moveaxis(k.reshape(b, h, nb, block, d), 2, 0)
            vb = jnp.moveaxis(v.reshape(b, h, nb, block, d), 2, 0)

            def step(carry, kv):
                num, den = carry
                k_blk, v_blk = kv
                s_blk = jnp.einsum('bhqd,bhkd->bhqk', q, k_blk) * scale
                m = jnp.max(s_blk, axis=-1, keepdims=True)
                e = jnp.exp(s_blk - m)
                num = num + jnp.einsum('bhqk,bhkd->bhqd', e, v_blk)
                den = den + jnp.sum(e, axis=-1, keepdims=True)
                return ((num, den), None)
            init = (jnp.zeros_like(q), jnp.zeros((b, h, s, 1), dtype=q.dtype))
            (num, den), _ = jax.lax.scan(step, init, (kb, vb))
            return num / den
        b, s, _ = hidden_states.shape
        q = (hidden_states @ w_q).reshape(b, s, HEADS, HEAD_DIM).transpose(0, 2, 1, 3)
        k = (hidden_states @ w_k).reshape(b, s, HEADS, HEAD_DIM).transpose(0, 2, 1, 3)
        v = (hidden_states @ w_v).reshape(b, s, HEADS, HEAD_DIM).transpose(0, 2, 1, 3)
        scale = HEAD_DIM ** (-0.5)
        out = _ring_attention(q, k, v, BLOCK, scale)
        out = out.transpose(0, 2, 1, 3).reshape(b, s, HIDDEN)
        return out @ w_o

    def _L3_ffn_ref(hidden_states, Wr, br, W1, b1, W2, b2, W3, b3):
        import jax, jax.numpy as jnp
        import numpy as np
        B, S, D, E = (4, 256, 128, 8)
        b, s, d = hidden_states.shape
        num_experts = Wr.shape[1]
        x = hidden_states.reshape(-1, d)
        router_logits = x @ Wr + br
        expert_mask = jax.nn.one_hot(jnp.argmax(router_logits, axis=-1), num_experts, dtype=x.dtype)
        out = jnp.zeros_like(x)
        for e in range(num_experts):
            h = jax.nn.gelu(x @ W1[e] + b1[e], approximate=False)
            h = jax.nn.gelu(h @ W2[e] + b2[e], approximate=False)
            y = h @ W3[e] + b3[e]
            out = out + expert_mask[:, e:e + 1] * y
        return out.reshape(b, s, d)
    x = L0_attn_x
    x = x + 0.5 * _L0_ffn_ref(_layernorm(x, axis=-1), L0_ffn_router_w, L0_ffn_w0_kernel, L0_ffn_w1_kernel, L0_ffn_wo_kernel)
    x = x + _L0_attn_ref(_layernorm(x, axis=-1), L0_attn_wq, L0_attn_bq, L0_attn_wu, L0_attn_bu)
    x = x + 0.5 * _L0_ffn_ref(_layernorm(x, axis=-1), L0_ffn_router_w, L0_ffn_w0_kernel, L0_ffn_w1_kernel, L0_ffn_wo_kernel)
    x = x + 0.5 * _L1_ffn_ref(_layernorm(x, axis=-1), L1_ffn_w1_w, L1_ffn_w1_s, L1_ffn_w2_w, L1_ffn_w2_s, L1_ffn_h1_w, L1_ffn_h1_s, L1_ffn_h2_w, L1_ffn_h2_s, L1_ffn_w3_w, L1_ffn_w3_s)
    x = x + _L1_attn_ref(_layernorm(x, axis=-1), L1_attn_attention_mask, L1_attn_Wk, L1_attn_bk, L1_attn_Wka, L1_attn_bka, L1_attn_Wv, L1_attn_bv, L1_attn_gamma, L1_attn_beta)
    x = x + 0.5 * _L1_ffn_ref(_layernorm(x, axis=-1), L1_ffn_w1_w, L1_ffn_w1_s, L1_ffn_w2_w, L1_ffn_w2_s, L1_ffn_h1_w, L1_ffn_h1_s, L1_ffn_h2_w, L1_ffn_h2_s, L1_ffn_w3_w, L1_ffn_w3_s)
    x = x + 0.5 * _L2_ffn_ref(_layernorm(x, axis=-1), L2_ffn_Wr, L2_ffn_br, L2_ffn_W_up, L2_ffn_b_up, L2_ffn_W_down, L2_ffn_b_down)
    x = x + _L2_attn_ref(_layernorm(x, axis=-1), L2_attn_Wq, L2_attn_bq, L2_attn_Wk, L2_attn_bk, L2_attn_Wv, L2_attn_bv, L2_attn_Wo, L2_attn_bo)
    x = x + 0.5 * _L2_ffn_ref(_layernorm(x, axis=-1), L2_ffn_Wr, L2_ffn_br, L2_ffn_W_up, L2_ffn_b_up, L2_ffn_W_down, L2_ffn_b_down)
    x = x + 0.5 * _L3_ffn_ref(_layernorm(x, axis=-1), L3_ffn_Wr, L3_ffn_br, L3_ffn_W1, L3_ffn_b1, L3_ffn_W2, L3_ffn_b2, L3_ffn_W3, L3_ffn_b3)
    x = x + _L3_attn_ref(_layernorm(x, axis=-1), L3_attn_w_q, L3_attn_w_k, L3_attn_w_v, L3_attn_w_o)
    x = x + 0.5 * _L3_ffn_ref(_layernorm(x, axis=-1), L3_ffn_Wr, L3_ffn_br, L3_ffn_W1, L3_ffn_b1, L3_ffn_W2, L3_ffn_b2, L3_ffn_W3, L3_ffn_b3)
    return x

_drawn_inputs = setup_inputs


def setup_inputs(seed=0):
    import zlib

    import numpy as np

    out = dict(_drawn_inputs(seed))
    spreads = {'L1_attn_bk': (0.0, 0.1),
     'L1_attn_bka': (0.0, 0.1),
     'L1_attn_bv': (0.0, 0.1),
     'L1_attn_gamma': (1.0, 0.2),
     'L1_attn_beta': (0.0, 0.1),
     'L2_attn_bq': (0.0, 0.1),
     'L2_attn_bk': (0.0, 0.1),
     'L2_attn_bv': (0.0, 0.1),
     'L2_attn_bo': (0.0, 0.1),
     'L2_ffn_br': (0.0, 0.1),
     'L3_ffn_br': (0.0, 0.1),
     'L3_ffn_b1': (0.0, 0.1),
     'L3_ffn_b2': (0.0, 0.1),
     'L3_ffn_b3': (0.0, 0.1)}
    factors = {}
    for name, (base, spread) in spreads.items():
        noise = np.random.default_rng([zlib.crc32(name.encode()), seed]).standard_normal(out[name].shape)
        drawn = base * np.exp(spread * noise) if base else spread * noise
        out[name] = jnp.asarray(drawn.astype(out[name].dtype))
    for name, factor in factors.items():
        out[name] = (out[name] * factor).astype(out[name].dtype)
    return out
```

```python
from contextlib import ExitStack

import numpy as np

import concourse.bass as bass
from concourse import mybir

LAYERS = tuple(range(12))

ALU = mybir.AluOpType
ACT = mybir.ActivationFunctionType
F32 = mybir.dt.float32
BF16 = mybir.dt.bfloat16
I32 = mybir.dt.int32
AX = mybir.AxisListType
EPS = 1e-5
NT = 16
CHUNKS = 4
FH = 688
L0T = [(i * 128, min(128, FH - i * 128)) for i in range(6)]
FM = 341
L2T = [(0, 128), (128, 128), (256, 85)]


class Eng:

    def __init__(self, name, sem):
        self.name, self.sem, self.q, self.n, self.seen = name, sem, [], 0, {}

    def wait(self, *toks):
        ws = []
        for t in flat(toks):
            key, v = t
            if self.seen.get(key.name, 0) < v:
                self.seen[key.name] = v
                ws.append(t)
        return ws

    def __call__(self, fn, *toks, inc=True):
        self.q.append((self.wait(*toks), fn, (self.sem, 1) if inc else None))
        if inc:
            self.n += 1
        return (self.sem, self.n) if inc else None

    def stop_until(self, *toks):
        self.q.append((self.wait(*toks), None, None))

    def flush(self, eng):
        for ws, fn, inc in self.q:
            for s, v in ws:
                eng.wait_ge(s, v)
            if fn is not None:
                ins = fn(eng)
                if inc is not None:
                    ins.then_inc(*inc)


def flat(toks):
    for t in toks:
        if t is None:
            continue
        if isinstance(t, list):
            yield from flat(t)
        else:
            yield t


class Ring:

    def __init__(self, bufs):
        self.bufs, self.free, self.i = bufs, [[] for _ in bufs], -1

    def next(self):
        self.i = (self.i + 1) % len(self.bufs)
        return self.bufs[self.i], self.free[self.i], self.i


def build(nc, ins, out):
    ctx = ExitStack()
    with ctx:
        sem = lambda n: ctx.enter_context(nc.semaphore(n))
        sb = lambda n, s, d=F32: ctx.enter_context(nc.sbuf_tensor(n, s, d))
        bank = [ctx.enter_context(nc.psum_tensor(f"bank{i}", [128, 512], F32)) for i in range(8)]
        PE, AC, DV, PO, SP = (Eng(n, sem("s_" + n)) for n in ("pe", "act", "dve", "pool", "sp"))
        dsems = [sem(f"s_dma{i}") for i in range(96)]
        dcount = [0] * 96
        dma_last = {}
        state = {"d": 0}

        def dma(o, i, *w, eng=SP):
            k = state["d"] % 96
            state["d"] += 1
            dcount[k] += 16
            dma_last[k] = (dsems[k], dcount[k])
            eng.q.append((eng.wait(*w), lambda e, o=o, i=i: e.dma_start(o, i), (dsems[k], 16)))
            return dma_last[k]

        def barrier():
            toks = [(e.sem, e.n) for e in (PE, AC, DV, PO) if e.n] + list(dma_last.values())
            for e in (PE, AC, DV, PO, SP):
                e.stop_until(toks)

        def mm(o, l, r, *w, start=True, stop=True, inc=False, skip=False):
            return PE(lambda e: e.matmul(o, l, r, start=start, stop=stop, skip_group_check=skip), *w, inc=inc)

        def tp(o, i, *w, inc=False):
            p = i.shape[0]
            idn = ident[0:p, 0:p] if i.dtype == F32 else identb[0:p, 0:p]
            return PE(lambda e: e.transpose(o, i, idn), *w, inc=inc)

        def act(o, i, f, *w, bias=0.0, scale=1.0, accum=None):
            return AC(lambda e: e.activation(o, i, f, bias=bias, scale=scale, accum_out=accum), *w)

        def acopy(o, i, *w):
            return AC(lambda e: e.copy(o, i), *w)

        def tt(o, a, b, op, *w, eng=None):
            return (eng or DV)(lambda e: e.tensor_tensor(o, a, b, op), *w)

        def ts(o, a, s1, s2, op0, op1, *w, eng=None):
            return (eng or DV)(lambda e: e.tensor_scalar(o, a, s1, s2, op0, op1) if op1 is not None
                               else e.tensor_scalar(o, a, s1, None, op0), *w)

        def stt(o, a, s, b, op0, op1, *w):
            return DV(lambda e: e.scalar_tensor_tensor(o, a, s, b, op0, op1), *w)

        def red(o, a, op, *w, axis=None):
            return DV(lambda e: e.tensor_reduce(o, a, axis or AX.X, op), *w)

        def vcopy(o, i, *w, eng=None):
            return (eng or DV)(lambda e: e.tensor_copy(o, i), *w)

        def mset(o, v, *w, eng=None):
            return (eng or DV)(lambda e: e.memset(o, v), *w)

        x = sb("x", [128, NT, 128])
        xn = sb("xn", [128, NT, 128])
        xT = sb("xT", [128, 2048])
        NCF = CONST_F.shape[1]
        cf = sb("cf", [128, NCF])
        NCB = CONST_B.shape[1]
        cb = sb("cb", [128, NCB], BF16)
        st = sb("st", [128, NT, 6])
        mv = sb("mv", [128, NT, 2])
        rs = sb("rs", [128, NT])
        ARENA = 44000
        arena = sb("arena", [128, ARENA])
        cur = {"o": 0}

        def reset():
            cur["o"] = 0

        def take(n, dt=F32):
            w = n if dt == F32 else (n + 1) // 2
            a = arena[:, cur["o"]:cur["o"] + w]
            cur["o"] += w
            assert cur["o"] <= ARENA, cur["o"]
            return a if dt == F32 else a.bitcast(dt)

        def cF(name):
            a, b = CF_AT[name]
            return cf[:, a:b]

        def cB(name):
            a, b = CB_AT[name]
            return cb[:, a:b]

        ident, iota = cF("ident"), cF("iota")
        identb, tri, onesb = cB("ident"), cB("tri"), cB("ones")

        t_c = dma(cf[:, :], ins["const_f"])
        t_cb0 = dma(arena[:, 0:NCB], ins["const_b"])
        t_x = dma(x[:, :, :], ins["L0_attn_x"].rearrange("b (n p) d -> p (b n) d", p=128))
        t_cb = vcopy(cb[:, :], arena[:, 0:NCB], t_cb0)
        barrier()

        def layernorm(src, dst, *w):
            done = []
            for c in range(CHUNKS):
                s0, s1 = 4 * c, 4 * c + 4
                for t in range(s0, s1):
                    a = DV(lambda e, t=t: e.bn_stats(st[:, t, :], src[:, t, :]), *[q[c] if isinstance(q, list) and len(q) == CHUNKS else q for q in w])
                for t in range(s0, s1):
                    a = DV(lambda e, t=t: e.bn_aggr(mv[:, t, :], st[:, t, :]), (DV.sem, DV.n))
                b = ts(rs[:, s0:s1], mv[:, s0:s1, 1], EPS, None, ALU.add, None, a, eng=PO)
                b = tt(rs[:, s0:s1], rs[:, s0:s1], cF("mhalf")[:, s0:s1], ALU.pow, b, eng=PO)
                for t in range(s0, s1):
                    a = ts(dst[:, t, :], src[:, t, :], mv[:, t, 0:1], rs[:, t:t + 1], ALU.subtract, ALU.mult, b)
                done.append(a)
            return done

        def to_features(src, dst, w, banks, post=None):
            done = []
            for c in range(CHUNKS):
                p, free, i = banks.next()
                for j in range(4):
                    a = tp(p[:, j * 128:(j + 1) * 128], src[:, 4 * c + j, :], w[c], free, inc=(j == 3))
                if post is None:
                    a = acopy(dst[:, c * 512:(c + 1) * 512], p[:, :], a)
                else:
                    a = post(dst[:, c * 512:(c + 1) * 512], p[:, :], a)
                banks.free[i] = [a]
                done.append(a)
            return done

        def router(tx, w, wb, lgp, raw, tmp, mx, t_w, bias=None):
            for t in range(NT):
                a = mm(lgp[:, t * 8:t * 8 + 8], xT[:, t * 128:(t + 1) * 128], w, tx, t_w, inc=(t == NT - 1))
            lg = lgp[:, 0:128].rearrange("p (t e) -> p t e", e=8)
            if bias is not None:
                a = tt(tmp, lg, bias.unsqueeze(1).to_broadcast([128, NT, 8]), ALU.add, a)
                lg = tmp
            if raw is None:
                return lg, a
            a = red(mx, lg, ALU.max, a)
            a = tt(tmp, lg, mx.unsqueeze(2).to_broadcast([128, NT, 8]), ALU.subtract, a)
            a = act(tmp, tmp, ACT.Exp, a)
            b = red(mx, tmp, ALU.add, a)
            b = DV(lambda e: e.reciprocal(mx, mx), b)
            b = tt(raw, tmp, mx.unsqueeze(2).to_broadcast([128, NT, 8]), ALU.mult, b)
            return raw, b

        def argmax_mask(v, m, mx, tmp, vm, a):
            bc = lambda q: q.unsqueeze(2).to_broadcast([128, NT, 8])
            a = red(mx, v, ALU.max, a)
            a = tt(tmp, v, bc(mx), ALU.is_equal, a)
            a = tt(tmp, tmp, cF("ridx").rearrange("p (t e) -> p t e", e=8), ALU.mult, a)
            a = red(vm, tmp, ALU.max, a)
            return tt(m, tmp, bc(vm), ALU.is_equal, a)

        def l0_ffn():
            reset()
            banks = Ring(bank[0:2])
            txn = layernorm(x, xn)
            rw = take(8)
            t_rw = dma(rw, ins["L0_ffn_router_w"])
            wbuf = [(take(FH), take(FH), take(6 * 128).rearrange("p (f n) -> p f n", n=128)) for _ in range(2)]
            wfree = [[], []]

            def load_w(e):
                b0, b1, bo = wbuf[e % 2]
                w = wfree[e % 2]
                return [dma(b0, ins["L0_ffn_w0_kernel"][e], w),
                        dma(b1, ins["L0_ffn_w1_kernel"][e], w),
                        dma(bo[:, 0:5, :], ins["L0_ffn_wo_kernel"][e, 0:640].rearrange("(f p) n -> p f n", p=128), w),
                        dma(bo[0:48, 5, :], ins["L0_ffn_wo_kernel"][e, 640:FH], w)]

            t_we = {0: load_w(0), 1: load_w(1)}
            tx = to_features(xn, xT, txn, banks)
            v3 = lambda: take(128).rearrange("p (t e) -> p t e", e=8)
            raw, tmp, m1, m2, rest, q1 = v3(), v3(), v3(), v3(), v3(), v3()
            mx, mx1, mx2, vm, sl1, sl2 = (take(16) for _ in range(6))
            cnt = take(64).rearrange("p (g e) -> p g e", e=8)
            m1b, m2b = take(128, BF16), take(128, BF16)
            raw, a = router(tx, rw, None, bank[2], raw, tmp, mx, t_rw)
            a = argmax_mask(raw, m1, mx1, tmp, vm, a)
            b1 = vcopy(m1b, m1.rearrange("p t e -> p (t e)"), a)
            a = tt(rest, raw, m1, ALU.mult, a)
            a = tt(rest, raw, rest, ALU.subtract, a)
            a = argmax_mask(rest, m2, mx2, tmp, vm, a)
            b2 = vcopy(m2b, m2.rearrange("p t e -> p (t e)"), a)
            m4 = lambda m: m.rearrange("p (g j e) -> p g j e", j=2, e=8)

            def prefix(p, mb, w):
                mm(p[:, 0:128], tri, mb, w, start=True, stop=False, skip=True)
                return mm(m4(p[:, 0:128])[:, :, 1, :], onesb, m4(mb)[:, :, 0, :], start=False, stop=True, inc=True, skip=True)

            c1 = prefix(bank[3], m1b, [b1, t_cb])
            mm(bank[4][:, 0:64], onesb, m4(m1b)[:, :, 0, :], start=True, stop=False)
            c2 = mm(bank[4][:, 0:64], onesb, m4(m1b)[:, :, 1, :], start=False, stop=True, inc=True)
            c3 = prefix(bank[5], m2b, b2)
            t3 = lambda p: p[:, 0:128].rearrange("p (t e) -> p t e", e=8)
            coff = cF("coff").rearrange("p (t e) -> p t e", e=8)

            def slots(p, m, sl, w):
                a = stt(tmp, p, 64.0, m, ALU.is_lt, ALU.mult, w)
                b = tt(q1, p, coff, ALU.add, w, a)
                a = tt(q1, q1, tmp, ALU.mult, a, b)
                a = red(sl, q1, ALU.add, a)
                return ts(sl, sl, 1.0, None, ALU.subtract, None, a)

            s1 = slots(t3(bank[3]), m1, sl1, c1)
            a = ts(cnt, bank[4][:, 0:64].rearrange("p (g e) -> p g e", e=8), 64.0, None, ALU.min, None, c2)
            a = tt(rest.rearrange("p (g j) e -> p g j e", j=2), m4(bank[5][:, 0:128]),
                   cnt.unsqueeze(2).to_broadcast([128, 8, 2, 8]), ALU.add, a, c3, s1)
            s2 = slots(rest, m2, sl2, a)

            xd = take(8 * 512)
            xdv = xd.rearrange("p (k h g s c) -> p k h g s c", k=4, h=2, g=4, s=2)
            dt = [take(512) for _ in range(4)]
            d_r = Ring(dt)
            td = []
            for g in range(8):
                p, pf, pi = banks.next()
                for j in range(2):
                    t = 2 * g + j
                    d, df, di = d_r.next()
                    a = ts(d, iota, sl1[:, t:t + 1], None, ALU.is_equal, None, s1, df, t_c)
                    a = stt(d, iota, sl2[:, t:t + 1], d, ALU.is_equal, ALU.add, a, s2)
                    b = mm(p[:, :], xn[:, t, :], d, a, pf, start=(j == 0), stop=(j == 1), inc=True)
                    d_r.free[di] = [b]
                pv = p[:, :].rearrange("p (k s c) -> p k s c", k=4, s=2)
                e1 = acopy(xdv[:, :, g % 2, g // 2, 0, :], pv[:, :, 0, :], b)
                e2 = acopy(xdv[:, :, 1 - g % 2, g // 2, 1, :], pv[:, :, 1, :], b)
                banks.free[pi] = [e2]
                td.append(e2)
            ct = take(NT * 512).rearrange("p (t n) -> p t n", t=NT)
            cring = Ring([(take(512), take(512)) for _ in range(2)])
            cbank = Ring([bank[7]])
            tct = []

            def combine_tile(t):
                (ca, cc), cfree, ci = cring.next()
                a1 = ts(ca, iota, sl1[:, t:t + 1], mx1[:, t:t + 1], ALU.is_equal, ALU.mult, s1, cfree)
                a2 = ts(cc, iota, sl2[:, t:t + 1], mx2[:, t:t + 1], ALU.is_equal, ALU.mult, s2, cfree)
                a = tt(ca, ca, cc, ALU.add, a1, a2)
                p, pf, pi = cbank.next()
                for k in range(4):
                    b = tp(p[:, k * 128:(k + 1) * 128], ca[:, k * 128:(k + 1) * 128], a, pf, inc=(k == 3))
                cring.free[ci] = [b]
                b = vcopy(ct[:, t, :], p[:, :], b)
                cbank.free[pi] = [b]
                tct.append(b)

            eo = take(8 * 4 * 128).rearrange("p (g k n) -> p g k n", g=8, k=4)
            hid = [take(6 * 512).rearrange("p (f n) -> p f n", n=512) for _ in range(2)]
            hfree = [[], []]
            hb = Ring([(bank[0], bank[1]), (bank[2], bank[3]), (bank[4], bank[5])])
            hb.free[0] = [banks.free[0], banks.free[1]]
            hb.free[1] = [s2]
            hb.free[2] = [s2]
            ob = Ring([bank[6]])
            teo = []
            for e in range(8):
                w0, w1, wo = wbuf[e % 2]
                h = hid[e % 2]
                for f, (f0, fn) in enumerate(L0T):
                    (p0, p1), pf, pi = hb.next()
                    mm(p0[0:fn, :], w0[:, f0:f0 + fn], xd[:, e * 512:(e + 1) * 512], pf, td, t_we[e])
                    a = mm(p1[0:fn, :], w1[:, f0:f0 + fn], xd[:, e * 512:(e + 1) * 512], inc=True)
                    a = act(h[0:fn, f, :], p0[0:fn, :], ACT.Gelu_apprx_tanh, a, hfree[e % 2])
                    a = tt(h[0:fn, f, :], h[0:fn, f, :], p1[0:fn, :], ALU.mult, a)
                    hb.free[pi] = [a]
                p, pf, pi = ob.next()
                for s in range(4):
                    for f, (f0, fn) in enumerate(L0T):
                        b = mm(p[:, s * 128:(s + 1) * 128], h[0:fn, f, s * 128:(s + 1) * 128], wo[0:fn, f, :],
                               a, pf, start=(f == 0), stop=(f == 5), inc=(f == 5 and s == 3))
                hfree[e % 2] = [b]
                wfree[e % 2] = [b]
                if e + 2 < 8:
                    t_we[e + 2] = load_w(e + 2)
                eog = eo.rearrange("p (g h) k n -> p g h k n", h=2)
                pg = p[:, :].rearrange("p (g n) -> p g n", g=4)
                c_ = [acopy(eog[64 * s:64 * s + 64, :, s ^ (e % 2), e // 2, :], pg[64 * s:64 * s + 64, :, :], b)
                      for s in range(2)]
                ob.free[pi] = [c_[-1]]
                teo.append(c_[-1])
                combine_tile(2 * e)
                combine_tile(2 * e + 1)
            yb = Ring([bank[0], bank[1], bank[2], bank[3]])
            for i in range(4):
                yb.free[i] = [a]
            out_t = []
            for t in range(NT):
                p, pf, pi = yb.next()
                for k in range(4):
                    b = mm(p[:, 0:128], ct[:, t, k * 128:(k + 1) * 128], eo[:, t // 2, k, :], tct[t], teo, pf,
                           start=(k == 0), stop=(k == 3), inc=(k == 3))
                b = stt(x[:, t, :], p[:, 0:128], 0.5, x[:, t, :], ALU.mult, ALU.add, b)
                yb.free[pi] = [b]
                out_t.append(b)

        def l1_ffn():
            reset()
            w1, w2 = take(512), take(512)
            h1 = take(2048).rearrange("p (k n) -> p k n", k=4)
            h2 = take(2048).rearrange("p (k n) -> p k n", k=4)
            w3 = take(512).rearrange("p (k n) -> p k n", k=4)
            sc = take(16).rearrange("p (a f) -> p a f", a=4)
            s3 = take(128)
            t_w = [dma(w1, ins["w1T"]), dma(w2, ins["w2T"])]
            t_s = [dma(sc[:, i, :], ins[n]) for i, n in enumerate(("w1_s", "w2_s", "h1_s", "h2_s"))]
            t_h1 = dma(h1, ins["h1T"].rearrange("(k p) n -> p k n", p=128))
            t_h2 = dma(h2, ins["h2T"].rearrange("(k p) n -> p k n", p=128))
            t_w3 = dma(w3, ins["w3T"].rearrange("(k p) n -> p k n", p=128))
            t_s3 = dma(s3, ins["L1_ffn_w3_s"].partition_broadcast(128))
            banks = Ring(bank)
            txn = layernorm(x, xn)
            tx = to_features(xn, xT, txn, banks)
            hr = Ring([take(2048).rearrange("p (k n) -> p k n", k=4) for _ in range(4)])
            tmp = take(512)
            for c in range(CHUNKS):
                xc = xT[:, c * 512:(c + 1) * 512]
                h, hf, hi = hr.next()
                ta = []
                for f in range(4):
                    p0, pf0, i0 = banks.next()
                    a = mm(p0[:, :], w1[:, f * 128:(f + 1) * 128], xc, tx[c], t_w, pf0, inc=True)
                    p1, pf1, i1 = banks.next()
                    b = mm(p1[:, :], w2[:, f * 128:(f + 1) * 128], xc, pf1, inc=True)
                    a = act(h[:, f, :], p0[:, :], ACT.Silu, a, hf, t_s, scale=sc[:, 0, f:f + 1])
                    banks.free[i0] = [a]
                    a = stt(h[:, f, :], p1[:, :], sc[:, 1, f:f + 1], h[:, f, :], ALU.mult, ALU.mult, a, b)
                    banks.free[i1] = [a]
                    ta.append(a)
                for wgt, tw, si in ((h1, t_h1, 2), (h2, t_h2, 3)):
                    g, gf, gi = hr.next()
                    tb = []
                    for f in range(4):
                        p, pf, pi = banks.next()
                        for k in range(4):
                            a = mm(p[:, :], wgt[:, k, f * 128:(f + 1) * 128], h[:, k, :], ta[k], tw, pf,
                                   start=(k == 0), stop=(k == 3), inc=(k == 3))
                        b = act(g[:, f, :], p[:, :], ACT.Gelu, a, gf, scale=sc[:, si, f:f + 1])
                        banks.free[pi] = [b]
                        tb.append(b)
                    hr.free[hi] = [a]
                    h, hi, ta = g, gi, tb
                for j in range(4):
                    t = 4 * c + j
                    p, pf, pi = banks.next()
                    for k in range(4):
                        a = mm(p[:, 0:128], h[:, k, j * 128:(j + 1) * 128], w3[:, k, :], ta[k], t_w3, pf,
                               start=(k == 0), stop=(k == 3), inc=(k == 3))
                    b = stt(tmp[:, j * 128:(j + 1) * 128], p[:, 0:128], 0.5, s3, ALU.mult, ALU.mult, a, t_s3)
                    banks.free[pi] = [b]
                    b = tt(x[:, t, :], x[:, t, :], tmp[:, j * 128:(j + 1) * 128], ALU.add, b)
                hr.free[hi] = [a]

        def l1_attn():
            reset()
            wk, wka, wv = take(128), take(128), take(128)
            cols = take(5)
            t_w = [dma(wk, ins["WkT1"]), dma(wka, ins["WkaT1"]), dma(wv, ins["WvT1"])]
            t_w += [dma(cols[:, i:i + 1], ins["L1_attn_" + n].rearrange("(p a) -> p a", a=1))
                    for i, n in enumerate(("gamma", "beta", "bk", "bka", "bv"))]
            banks = Ring(bank)
            a = ts(cols[:, 3:4], cols[:, 3:4], 128 ** -0.5, None, ALU.mult, None, t_w)
            txn = layernorm(x, xn)
            txn = layernorm(xn, xn, txn)
            tx = to_features(xn, xT, txn, banks,
                             post=lambda o, p, w: ts(o, p, cols[:, 0:1], cols[:, 1:2], ALU.mult, ALU.add, w, t_w))
            ka = a
            keys, vals, kw, cum, pr = (take(2048) for _ in range(5))
            ones = cF("onesrow")
            for c in range(CHUNKS):
                s = slice(c * 512, (c + 1) * 512)
                p, pf, pi = banks.next()
                a = mm(p[:, :], wk, xT[:, s], tx[c], t_w, pf, inc=True)
                k_ = act(keys[:, s], p[:, :], ACT.Identity, a, bias=cols[:, 2:3])
                banks.free[pi] = [k_]
                p, pf, pi = banks.next()
                a = mm(p[:, :], wv, xT[:, s], pf, inc=True)
                v_ = act(vals[:, s], p[:, :], ACT.Identity, a, bias=cols[:, 4:5])
                banks.free[pi] = [v_]
                p, pf, pi = banks.next()
                a = mm(p[:, :], wka, keys[:, s], k_, pf, inc=True)
                w_ = act(kw[:, s], p[:, :], ACT.Exp, a, ka, bias=cols[:, 3:4], scale=128 ** -0.5)
                banks.free[pi] = [w_]
                a = DV(lambda e, s=s: e.tensor_tensor_scan(cum[:, s], ones, kw[:, s], 0.0, ALU.mult, ALU.add), w_)
                a = DV(lambda e, s=s: e.reciprocal(cum[:, s], cum[:, s]), a)
                a = tt(kw[:, s], kw[:, s], cum[:, s], ALU.mult, a)
                a = tt(kw[:, s], kw[:, s], keys[:, s], ALU.mult, a)
                a = DV(lambda e, s=s: e.tensor_tensor_scan(cum[:, s], ones, kw[:, s], 0.0, ALU.mult, ALU.add), a)
                a = tt(pr[:, s], cum[:, s], vals[:, s], ALU.mult, a, v_)
                p, pf, pi = banks.next()
                for j in range(4):
                    b = tp(p[:, j * 128:(j + 1) * 128], pr[:, c * 512 + j * 128:c * 512 + (j + 1) * 128], a, pf, inc=(j == 3))
                xc = x[:, 4 * c:4 * c + 4, :].rearrange("p t n -> p (t n)")
                b = tt(xc, xc, p[:, :], ALU.add, b)
                banks.free[pi] = [b]

        def transposed_gates(g, gT, p, a):
            for c in range(CHUNKS):
                for j in range(4):
                    t = 4 * c + j
                    b = tp(p[c][0:8, j * 128:(j + 1) * 128], g[:, t, :], a, inc=(j == 3))
                b = acopy(gT[0:8, c * 512:(c + 1) * 512], p[c][0:8, :], b)
            return b

        def l2_ffn():
            reset()
            wr = take(8)
            wrb = take(8)
            wu = take(4 * FM).rearrange("p (g f) -> p g f", g=4)
            bu = take(12).rearrange("p (g f) -> p g f", g=4)
            wd = take(8 * 3 * 128).rearrange("p (e f n) -> p e f n", e=8, f=3)
            bd = take(128)
            t_r = [dma(wr, ins["L2_ffn_Wr"]), dma(wrb, ins["L2_ffn_br"].partition_broadcast(128))]
            t_wu = dma(wu, ins["L2_ffn_W_up"].rearrange("g p f -> p g f"))
            t_bu = [dma(bu[:, :, :], ins["bup"])]
            t_wd = [dma(wd[:, e, 0:2, :], ins["L2_ffn_W_down"][e, 0:256].rearrange("(f p) n -> p f n", p=128)) for e in range(8)]
            t_wd += [dma(wd[0:85, :, 2, :], ins["L2_ffn_W_down"][:, 256:FM].rearrange("e p n -> p e n"))]
            t_bd = dma(bd[0:8, :], ins["L2_ffn_b_down"])
            banks = Ring(bank[0:2])
            txn = layernorm(x, xn)
            tx = to_features(xn, xT, txn, banks)
            v3 = lambda: take(128).rearrange("p (t e) -> p t e", e=8)
            raw, tmp, eq, gt, gate = v3(), v3(), v3(), v3(), v3()
            mx = take(16)
            lo, cand, cnt, tmp8, need = (take(8) for _ in range(5))
            raw, a = router(tx, wr, None, bank[2], raw, tmp, mx, t_r, bias=wrb)
            cmpb = take(128, BF16)
            cmpv = cmpb.rearrange("p (t e) -> p t e", e=8)
            b8 = lambda q: q.unsqueeze(1).to_broadcast([128, NT, 8])
            sp = bank[3]

            def count(fn, w):
                c_ = fn(w)
                c_ = mm(sp[:, 0:128], onesb, cmpb, c_, inc=True)
                return red(cnt, sp[:, 0:128].rearrange("p (t e) -> p e t", e=8), ALU.add, c_)

            b = mset(lo, 0.0, a)
            for bit in range(29, -1, -1):
                b = ts(cand.bitcast(I32), lo.bitcast(I32), 1 << bit, None, ALU.bitwise_or, None, b)
                b = count(lambda w: tt(cmpv, raw, b8(cand), ALU.is_ge, w), b)
                b = stt(tmp8, cnt, 256.0, cand, ALU.is_ge, ALU.mult, b)
                b = tt(lo, lo, tmp8, ALU.max, b)
            b = count(lambda w: tt(cmpv, raw, b8(lo), ALU.is_gt, w), b)
            b = ts(need, cnt, -1.0, 256.0, ALU.mult, ALU.add, b)
            g_ = tt(gt, raw, b8(lo), ALU.is_gt, b)
            q_ = tt(eq, raw, b8(lo), ALU.is_equal, g_)
            q_ = vcopy(cmpv, eq, q_)
            mm(bank[4][:, 0:128], tri, cmpb, q_, inc=False)
            q_ = mm(bank[5][:, 0:128], onesb, cmpb, q_, inc=True)
            tot = take(128)
            pre = take(128)
            q_ = vcopy(tot.rearrange("p (e t) -> p e t", e=8), bank[5][:, 0:128].rearrange("p (t e) -> p e t", e=8), q_)
            q_ = DV(lambda e: e.tensor_tensor_scan(pre, cF("scanreset"), tot, 0.0, ALU.mult, ALU.add), q_)
            q_ = tt(pre, pre, tot, ALU.subtract, q_)
            q_ = tt(tmp, bank[4][:, 0:128].rearrange("p (t e) -> p t e", e=8), pre.rearrange("p (e t) -> p t e", e=8), ALU.add, q_)
            q_ = tt(tmp, tmp, b8(need), ALU.is_lt, q_)
            q_ = tt(tmp, tmp, eq, ALU.mult, q_)
            q_ = tt(gt, gt, tmp, ALU.add, q_)
            q_ = stt(gate, gt, 0.5, raw, ALU.mult, ALU.mult, q_)
            gT = take(2048)
            t_g = transposed_gates(gate, gT, bank[4:8], q_)
            mid = [take(3 * 512).rearrange("p (f n) -> p f n", f=3) for _ in range(4 * 2)]
            mr = Ring(mid)
            ub = Ring([bank[i] for i in (0, 1, 2)])
            yb = Ring([bank[i] for i in (3, 4, 5, 6, 7)])
            for r in (ub, yb):
                for i in range(len(r.bufs)):
                    r.free[i] = [t_g, q_]
            for c in range(CHUNKS):
                ms = []
                for g in range(4):
                    m, mf, mi = mr.next()
                    for f, (f0, fn) in enumerate(L2T):
                        p, pf, pi = ub.next()
                        a = mm(p[0:fn, :], wu[:, g, f0:f0 + fn], xT[:, c * 512:(c + 1) * 512], tx[c], t_wu, pf, inc=True)
                        a = act(m[0:fn, f, :], p[0:fn, :], ACT.Silu, a, mf, t_bu, bias=bu[0:fn, g, f:f + 1])
                        ub.free[pi] = [a]
                    ms.append((m, mi, a))
                for j in range(4):
                    t = 4 * c + j
                    p, pf, pi = yb.next()
                    a = mm(p[:, 0:128], gT[0:8, t * 128:(t + 1) * 128], bd[0:8, :], t_g, t_bd, pf, inc=True)
                    b = tt(x[:, t, :], x[:, t, :], p[:, 0:128], ALU.add, a)
                    yb.free[pi] = [b]
                    for g in range(4):
                        m, mi, ta = ms[g]
                        p, pf, pi = yb.next()
                        for f, (f0, fn) in enumerate(L2T):
                            a = mm(p[:, 0:256], m[0:fn, f, j * 128:(j + 1) * 128], wd[0:fn, 2 * g:2 * g + 2, f, :],
                                   ta, t_wd, pf, start=(f == 0), stop=(f == 2), inc=(f == 2))
                        mr.free[mi] = [a]
                        for h in range(2):
                            e = 2 * g + h
                            b = stt(x[:, t, :], p[:, h * 128:(h + 1) * 128], gate[:, t, e:e + 1], x[:, t, :],
                                    ALU.mult, ALU.add, a, b)
                        yb.free[pi] = [b]

        def l2_attn():
            reset()
            wq, wk, wv, wo = (take(128) for _ in range(4))
            bq = take(1)
            bkb, bvb, bob = (take(128) for _ in range(3))
            t_w = [dma(wq, ins["WqT2"]), dma(wk, ins["WkT2"]), dma(wv, ins["WvT2"]), dma(wo, ins["WoT2"]),
                   dma(bq, ins["L2_attn_bq"].rearrange("(p a) -> p a", a=1))]
            t_w += [dma(o, ins["L2_attn_" + n].partition_broadcast(128)) for o, n in ((bkb, "bk"), (bvb, "bv"), (bob, "bo"))]
            banks = Ring(bank)
            txn = layernorm(x, xn)
            tx = to_features(xn, xT, txn, banks)
            q, tq, o = take(2048), take(2048), take(2048)
            k, tk, v = take(2048), take(2048), take(2048)
            kv = take(512)
            for b_ in range(4):
                s = slice(b_ * 512, (b_ + 1) * 512)
                p, pf, pi = banks.next()
                a = mm(p[:, :], wq, xT[:, s], tx[b_], t_w, pf, inc=True)
                q1 = ts(tq[:, s], p[:, :], bq, 0.0, ALU.add, ALU.min, a, t_w)
                q2 = ts(q[:, s], p[:, :], bq, 0.0, ALU.add, ALU.max, a)
                banks.free[pi] = [q2]
                q1 = act(tq[:, s], tq[:, s], ACT.Exp, q1)
                t_q = tt(q[:, s], q[:, s], tq[:, s], ALU.add, q1, q2)
                bc4 = lambda z: z.unsqueeze(1).to_broadcast([128, 4, 128])
                r4 = lambda z: z.rearrange("p (t n) -> p t n", t=4)
                p, pf, pi = banks.next()
                for j in range(4):
                    a = mm(p[:, j * 128:(j + 1) * 128], xT[:, b_ * 512 + j * 128:b_ * 512 + (j + 1) * 128], wk, pf, inc=(j == 3))
                k1 = tt(r4(k[:, s]), r4(p[:, :]), bc4(bkb), ALU.add, a)
                banks.free[pi] = [k1]
                k2 = ts(tk[:, s], k[:, s], 0.0, None, ALU.min, None, k1)
                k2 = act(tk[:, s], tk[:, s], ACT.Exp, k2)
                t_k = stt(k[:, s], k[:, s], 0.0, tk[:, s], ALU.max, ALU.add, k2)
                p, pf, pi = banks.next()
                for j in range(4):
                    a = mm(p[:, j * 128:(j + 1) * 128], xT[:, b_ * 512 + j * 128:b_ * 512 + (j + 1) * 128], wv, pf, inc=(j == 3))
                t_v = tt(r4(v[:, s]), r4(p[:, :]), bc4(bvb), ALU.add, a)
                banks.free[pi] = [t_v]
                p, pf, pi = banks.next()
                for j in range(4):
                    u = slice(b_ * 512 + j * 128, b_ * 512 + (j + 1) * 128)
                    a = mm(p[:, 0:128], k[:, u], v[:, u], t_k, t_v, pf, start=(j == 0), stop=(j == 3), inc=(j == 3))
                kvb = kv[:, b_ * 128:(b_ + 1) * 128]
                t_kv = tt(kvb, p[:, 0:128], cF("blockdiag"), ALU.mult, a)
                banks.free[pi] = [t_kv]
                p, pf, pi = banks.next()
                a = mm(p[:, :], kvb, q[:, s], t_kv, t_q, pf, inc=True)
                t_o = acopy(o[:, s], p[:, :], a)
                banks.free[pi] = [t_o]
                p, pf, pi = banks.next()
                for j in range(4):
                    a = mm(p[:, j * 128:(j + 1) * 128], o[:, b_ * 512 + j * 128:b_ * 512 + (j + 1) * 128], wo, t_o, pf, inc=(j == 3))
                xc = x[:, 4 * b_:4 * b_ + 4, :]
                a = tt(xc, xc, r4(p[:, :]), ALU.add, a)
                banks.free[pi] = [a]
                a = tt(xc, xc, bc4(bob), ALU.add, a)

        def l3_ffn():
            reset()
            wr, wrb = take(8), take(8)
            b3 = take(128)
            t_r = [dma(wr, ins["L3_ffn_Wr"]), dma(wrb, ins["L3_ffn_br"].partition_broadcast(128))]
            b1 = take(32).rearrange("p (e f) -> p e f", e=8)
            b2 = take(16).rearrange("p (e f) -> p e f", e=8)
            t_b1 = dma(b1, ins["b1c"])
            t_b2 = dma(b2, ins["b2c"])
            t_b3 = dma(b3[0:8, :], ins["L3_ffn_b3"])
            wb = [(take(512), take(1024).rearrange("p (k n) -> p k n", k=4), take(256).rearrange("p (k n) -> p k n", k=2))
                  for _ in range(2)]
            wfree = [[], []]

            def load_w(e):
                u, v, w = wb[e % 2]
                f = wfree[e % 2]
                return [dma(u, ins["L3_ffn_W1"][e], f),
                        dma(v, ins["L3_ffn_W2"][e].rearrange("(k p) n -> p k n", p=128), f),
                        dma(w, ins["L3_ffn_W3"][e].rearrange("(k p) n -> p k n", p=128), f)]

            t_we = {0: load_w(0), 1: load_w(1)}
            banks = Ring(bank)
            txn = layernorm(x, xn)
            tx = to_features(xn, xT, txn, banks)
            v3 = lambda: take(128).rearrange("p (t e) -> p t e", e=8)
            tmp, m, mh = v3(), v3(), v3()
            mx, vm = take(16), take(16)
            pl, plf, pli = banks.next()
            PE.stop_until(plf)
            lg, a = router(tx, wr, None, pl, None, mh, mx, t_r, bias=wrb)
            a = argmax_mask(lg, m, mx, tmp, vm, a)
            banks.free[pli] = [a]
            a = ts(m, m, 0.5, None, ALU.mult, None, a)
            gT = take(2048)
            four = []
            for _ in range(4):
                p, pf, pi = banks.next()
                PE.stop_until(pf)
                four.append((p, pi))
            t_g = transposed_gates(m, gT, [p for p, _ in four], a)
            for _, pi in four:
                banks.free[pi] = [t_g]
            t_m = [a, t_g]
            h1r = Ring([take(2048).rearrange("p (k n) -> p k n", k=4) for _ in range(2)])
            h2r = Ring([take(1024).rearrange("p (k n) -> p k n", k=2) for _ in range(2)])
            for t in range(NT):
                p, pf, pi = banks.next()
                a = mm(p[:, 0:128], gT[0:8, t * 128:(t + 1) * 128], b3[0:8, :], t_g, t_b3, pf, inc=True)
                b = tt(x[:, t, :], x[:, t, :], p[:, 0:128], ALU.add, a)
                banks.free[pi] = [b]
            for e in range(8):
                w1, w2, w3 = wb[e % 2]
                for c in range(CHUNKS):
                    h, hf, hi = h1r.next()
                    ta = []
                    for f in range(4):
                        p, pf, pi = banks.next()
                        a = mm(p[:, :], w1[:, f * 128:(f + 1) * 128], xT[:, c * 512:(c + 1) * 512], pf, t_we[e], inc=True)
                        a = act(h[:, f, :], p[:, :], ACT.Gelu, a, hf, t_b1, bias=b1[:, e, f:f + 1])
                        banks.free[pi] = [a]
                        ta.append(a)
                    g, gf, gi = h2r.next()
                    tb = []
                    for f in range(2):
                        p, pf, pi = banks.next()
                        for k in range(4):
                            a = mm(p[:, :], w2[:, k, f * 128:(f + 1) * 128], h[:, k, :], ta[k], pf,
                                   start=(k == 0), stop=(k == 3), inc=(k == 3))
                        h1r.free[hi] = [a]
                        a = act(g[:, f, :], p[:, :], ACT.Gelu, a, gf, t_b2, bias=b2[:, e, f:f + 1])
                        banks.free[pi] = [a]
                        tb.append(a)
                    for j in range(4):
                        t = 4 * c + j
                        p, pf, pi = banks.next()
                        for k in range(2):
                            a = mm(p[:, 0:128], g[:, k, j * 128:(j + 1) * 128], w3[:, k, :], tb[k], pf,
                                   start=(k == 0), stop=(k == 1), inc=(k == 1))
                        b = stt(x[:, t, :], p[:, 0:128], m[:, t, e:e + 1], x[:, t, :], ALU.mult, ALU.add, a, t_m, (DV.sem, DV.n))
                        banks.free[pi] = [b]
                    h2r.free[gi] = [a]
                wfree[e % 2] = [a]
                if e + 2 < 8:
                    t_we[e + 2] = load_w(e + 2)

        def attention(kind):
            reset()
            banks = Ring(bank)
            txn = layernorm(x, xn)
            tx = to_features(xn, xT, txn, banks)
            scale = 128 ** -0.5 if kind == 0 else 8 ** -0.5
            nm = 3 if kind == 0 else 12
            sides = 1 if kind == 0 else 2
            wq, wk, wv, wo = (take(128) for _ in range(4))
            bcol = take(1)
            bub = take(128)
            if kind == 0:
                t_w = [dma(wq, ins["wqT0"]), dma(wo, ins["wuT0"]), dma(bcol, ins["L0_attn_bq"].rearrange("(p a) -> p a", a=1)),
                       dma(bub, ins["L0_attn_bu"].partition_broadcast(128))]
                ws = [wq]
            else:
                t_w = [dma(wq, ins["L3_attn_w_q"]), dma(wk, ins["L3_attn_w_k"]), dma(wv, ins["L3_attn_w_v"]), dma(wo, ins["L3_attn_w_o"])]
                ws = [wq, wk]
            save = cur["o"]
            hand = take(512 * 4)
            parts = [take(2048, BF16) for _ in range(3)]
            rem = take(2048)
            full = take(2048)
            scr = ins["scratch"]
            t_scr = []
            prev = []
            for side, w in enumerate(ws):
                tf = []
                for c in range(CHUNKS):
                    p, pf, pi = banks.next()
                    s = slice(c * 512, (c + 1) * 512)
                    a = mm(p[:, :], w, xT[:, s], tx[c], t_w, pf, inc=True)
                    if kind == 0:
                        b = act(full[:, s], p[:, :], ACT.Identity, a, bias=bcol)
                    else:
                        b = acopy(full[:, s], p[:, :], a, prev)
                    banks.free[pi] = [b]
                    tf.append(b)
                a = vcopy(parts[0], full, tf, prev)
                a = tt(rem, full, parts[0], ALU.subtract, a)
                a = vcopy(parts[1], rem, a)
                a = tt(rem, rem, parts[1], ALU.subtract, a)
                a = vcopy(parts[2], rem, a)
                prev = [dma(scr[side, i], parts[i], a) for i in range(3)]
                t_scr.append(list(prev))
            if kind == 3:
                cur["o"] = save
                ve = take(16 * 16 * 32).rearrange("p (t h m) -> p t h m", t=16, h=16)
                b = mset(ve.rearrange("p t h m -> p (t h m)"), 0.0, prev, a)
                c_ = mset(ve[:, :, :, 8:9], 1.0, b)
                for t in range(NT):
                    p, pf, pi = banks.next()
                    a = mm(p[:, 0:128], xT[:, t * 128:(t + 1) * 128], wv, pf, inc=True)
                    a = vcopy(ve[:, t, :, 0:8], p[:, 0:128].rearrange("p (h d) -> p h d", h=16), a, b)
                    banks.free[pi] = [a]
                t_ve = [a, c_]
            else:
                cur["o"] = save
                t_ve = []
            PW = 4 if kind == 3 else 16
            pieces = [(take(8192, BF16), take(8192, BF16)) for _ in range(2)]
            pfree = [[prev, a], [prev, a]]
            stage = take(8192, BF16) if kind == 0 else None
            sfree = [prev, a]
            for z in [z for pc in pieces for z in pc] + ([stage] if kind == 0 else []):
                b = mset(z[64:128, :], 0.0, prev, a)
                pfree[0].append(b)
            ind = "ind0" if kind == 0 else "ind3"
            ib = cB(ind)
            for i, (qq, kk) in enumerate(pieces):
                for r in range(4 if kind == 3 else 16):
                    n = 8192 // (4 if kind == 3 else 16)
                    if kind == 0:
                        src = cB("onesrow")[96:99, 0:n]
                        b = vcopy(kk[96:99, r * n:(r + 1) * n], src, b)
                    else:
                        for z in range(4):
                            b = vcopy(kk[96:108, r * 2048 + z * 512:r * 2048 + (z + 1) * 512], ib[96:108, :], b)
            for f in pfree:
                f.append(b)
            t_ind = b

            def load_piece(i):
                qq, kk = pieces[i % 2]
                toks = []
                for a_ in range(3):
                    for b_ in range(3):
                        r = (3 * a_ + b_) * 8
                        for dst, side, part in ((qq, 0, a_), (kk if kind else stage, sides - 1, b_)):
                            if kind == 0:
                                src = scr[side, part].rearrange("(c d) t -> d c t", d=8)[:, :, i * 512:(i + 1) * 512]
                                o = dst[r:r + 8, :].rearrange("p (c t) -> p c t", c=16)
                            else:
                                src = scr[side, part].rearrange("(c d) t -> d c t", d=8)[:, 4 * i:4 * i + 4, :]
                                o = dst[r:r + 8, :].rearrange("p (c t) -> p c t", c=4)
                            toks.append(dma(o, src, t_scr, pfree[i % 2], sfree if kind == 0 else None))
                if kind == 0:
                    b = vcopy(kk[0:96, :].rearrange("p (g c t) -> p g c t", g=16, c=16),
                              stage[0:96, :].rearrange("p (c g t) -> p g c t", g=16, c=16), toks, pfree[i % 2])
                    sfree[:] = [b]
                    toks.append(b)
                return toks

            t_piece = {0: load_piece(0), 1: load_piece(1)}

            def blk(z, q, b, keys=False):
                if kind == 0 and keys:
                    o = ((q % 4) * 4 + b) * 512
                    return z[:, o:o + 512]
                if kind == 0:
                    o = (q % 4) * 128 + b * 32
                    return z.rearrange("p (c t) -> p c t", c=16)[:, :, o:o + 32]
                o = (q % 4) * 2048 + b * 512
                return z[:, o:o + 512]

            def blk128(z, q, b, k):
                if kind == 0:
                    o = ((q % 4) * 4 + b) * 512 + k * 128
                    return z[:, o:o + 128]
                o = (q % 4) * 2048 + b * 512 + k * 128
                return z[:, o:o + 128]

            K = 96 + nm
            sr = Ring([(bank[0], bank[1]), (bank[2], bank[3]), (bank[4], bank[5])])
            av, misc = Ring([bank[6]]), Ring([bank[7]])
            for r in (sr, av, misc):
                for i in range(len(r.bufs)):
                    r.free[i] = [t_ind, t_ve]
            nkb = 1 if kind == 0 else 4
            nmx = 16 * nkb
            mxa = [take(nmx) for _ in range(2)]
            mneg = take(nmx)
            mpt = [take(3 * nmx, BF16) for _ in range(2)]
            er = Ring([take(1024) for _ in range(8)])
            if kind == 0:
                vq = [take(4 * 4 * 32) for _ in range(2)]
                vqfree = [[], []]
            ot = [take(512) for _ in range(2)]
            rc = take(16)
            osb = take(NT * 128).rearrange("p (t n) -> p t n", t=NT)
            t_norm = {}
            stat = {}

            def stage_a(q, u):
                qq, kk = pieces[(q // 4) % 2]
                b, half = u // 2, u % 2
                (pa, pb), pf, pi = sr.next()
                for n, p in enumerate((pa, pb)):
                    qt = 2 * half + n
                    l, r = (kk, qq) if kind == 0 else (qq, kk)
                    a = mm(p[:, :], blk128(l[0:72], q, b, qt), blk(r[0:72], q, b), t_piece[q // 4], pf, inc=(n == 1))
                m = mxa[q % 2].rearrange("p (b t k) -> p b t k", b=4, t=4)
                for n, p in enumerate((pa, pb)):
                    qt = 2 * half + n
                    c = red(m[:, b, qt, :], p[:, :].rearrange("p (k n) -> p k n", k=nkb), ALU.max, a, stat.get(("split", q - 2)))
                sr.free[pi] = [c]
                stat[("max", q, u)] = c

            def stage_m(q):
                qq, kk = pieces[(q // 4) % 2]
                mx_ = mxa[q % 2]
                pt = mpt[q % 2].rearrange("p (b z) -> p b z", b=16)
                p0, p1, p2 = (pt[:, :, i * nkb:(i + 1) * nkb] for i in range(3))
                v = lambda z: z.rearrange("p (b k) -> p b k", k=nkb)
                w = [stat[("max", q, 7)], stat.get(("mt", q - 2))]
                a = ts(p0, v(mx_), -1.0, None, ALU.mult, None, w)
                a = stt(v(mneg), v(mx_), -1.0, p0, ALU.mult, ALU.subtract, a)
                a = vcopy(p1, v(mneg), a)
                a = tt(p2, v(mneg), p1, ALU.subtract, a)
                stat[("split", q)] = a
                for b in range(4):
                    p, pf, pi = misc.next()
                    for k in range(4):
                        c = mm(p[96:96 + nm, k * 128:(k + 1) * 128], pt[:, b * 4 + k, :], identb, a, pf, inc=(k == 3))
                    o = blk(qq[96:96 + nm], q, b)
                    i_ = p[96:96 + nm, :]
                    if kind == 0:
                        i_ = i_.rearrange("p (c t) -> p c t", c=16)
                    d = acopy(o, i_, c)
                    misc.free[pi] = [d]
                stat[("mt", q)] = c
                stat[("mrow", q)] = d

            def stage_v(q):
                qq, kk = pieces[(q // 4) % 2]
                for b in range(4):
                    p, pf, pi = misc.next()
                    for k in range(4):
                        c = mm(p[:, k * 32:(k + 1) * 32], blk128(kk[0:99], q, b, k), cB("sel")[0:99, :], pf, t_piece[q // 4], inc=(k == 3))
                    d = vcopy(vq[q % 2][:, b * 128:(b + 1) * 128], p[:, 0:128], c, vqfree[q % 2])
                    misc.free[pi] = [d]
                stat[("v", q)] = d

            def stage_b(q, u):
                qq, kk = pieces[(q // 4) % 2]
                half, b = u // 4, u % 4
                (pa, pb), pf, pi = sr.next()
                for n, p in enumerate((pa, pb)):
                    k = 2 * half + n
                    a = mm(p[:, :], blk128(kk[0:K], q, b, k), blk(qq[0:K], q, b), stat[("mrow", q)], pf, inc=(n == 1))
                e, ef, ei = er.next()
                for n, p in enumerate((pa, pb)):
                    c = act(e[:, n * 512:(n + 1) * 512], p[:, :], ACT.Exp, a, ef, scale=scale)
                sr.free[pi] = [c]
                stat[("e", q, u)] = (e, ei, c)
                if u == 7:
                    stat[("bdone", q)] = a

            def stage_o(q, half):
                if half == 0:
                    stat["av"] = av.next()
                p, pf, pi = stat["av"]
                for n in range(2):
                    k = 2 * half + n
                    for b in range(4):
                        e, ei, te = stat[("e", q, half * 4 + b)]
                        if kind == 0:
                            lv = vq[q % 2][:, b * 128 + k * 32:b * 128 + (k + 1) * 32]
                            tv = stat[("v", q)]
                        else:
                            lv, tv = ve[:, b * 4 + k, q, :], t_ve
                        a = mm(p[32 * b:32 * b + 32, :], lv, e[:, n * 512:(n + 1) * 512], te, tv, pf,
                               start=(k == 0), stop=(k == 3), inc=True, skip=True)
                        if n == 1:
                            er.free[ei] = [a]
                if half == 1:
                    if kind == 0:
                        vqfree[q % 2] = [a]
                    o = ot[q % 2]
                    a = DV(lambda e_: e_.transpose(o, p[:, :]), a)
                    av.free[pi] = [a]
                    ov = o.rearrange("p (c m) -> p c m", m=32)
                    a = DV(lambda e_: e_.reciprocal(rc, ov[:, :, 8]), a)
                    dst = osb[:, q, :].rearrange("p (c d) -> p c d", d=8) if kind == 0 else osb[:, :, q * 8:q * 8 + 8]
                    a = tt(dst, ov[:, :, 0:8], rc.unsqueeze(2).to_broadcast([128, 16, 8]), ALU.mult, a)
                    t_norm[q] = a
                    pfree[(q // 4) % 2] = [stat[("bdone", q)]]
                    if q % 4 == 3 and q // 4 + 2 < 4:
                        t_piece[q // 4 + 2] = load_piece(q // 4 + 2)

            for u in range(8):
                stage_a(0, u)
            stage_m(0)
            if kind == 0:
                stage_v(0)
            for q in range(16):
                for u in range(8):
                    if q + 1 < 16:
                        stage_a(q + 1, u)
                    stage_b(q, u)
                    if u == 5:
                        stage_o(q, 0)
                if q + 1 < 16:
                    stage_m(q + 1)
                    if kind == 0:
                        stage_v(q + 1)
                stage_o(q, 1)
            if kind == 3:
                pass
            oT = rem_oT = take(2048)
            rb = Ring([bank[0], bank[1], bank[2], bank[3]])
            for i in range(4):
                rb.free[i] = [t_norm[15], stat[("e", 15, 7)][2], stat[("max", 15, 7)]]
            tt_ = []
            for c in range(CHUNKS):
                p, pf, pi = rb.next()
                for j in range(4):
                    a = tp(p[:, j * 128:(j + 1) * 128], osb[:, 4 * c + j, :], list(t_norm.values()), pf, inc=(j == 3))
                if kind == 0:
                    a = acopy(oT[:, c * 512:(c + 1) * 512], p[:, :], a)
                else:
                    dst = oT.rearrange("p (b u t) -> p u b t", b=4, u=16)[:, 4 * c:4 * c + 4, :, :]
                    src = p[:, :].rearrange("p (u b t) -> p u b t", u=4, b=4)
                    for j in range(4):
                        a_ = acopy(dst[:, j, :, :], src[:, j, :, :], a)
                    a = a_
                rb.free[pi] = [a]
                tt_.append(a)
            for c in range(CHUNKS):
                p, pf, pi = rb.next()
                for j in range(4):
                    t = 4 * c + j
                    a = mm(p[:, j * 128:(j + 1) * 128], oT[:, t * 128:(t + 1) * 128], wo, tt_, pf, inc=(j == 3))
                xc = x[:, 4 * c:4 * c + 4, :]
                a = tt(xc, xc, p[:, :].rearrange("p (t n) -> p t n", t=4), ALU.add, a)
                rb.free[pi] = [a]
                if kind == 0:
                    a = tt(xc, xc, bub.unsqueeze(1).to_broadcast([128, 4, 128]), ALU.add, a)

        stages = [l0_ffn, lambda: attention(0), l0_ffn, l1_ffn, l1_attn, l1_ffn, l2_ffn, l2_attn, l2_ffn,
                  l3_ffn, lambda: attention(3), l3_ffn]
        for n in LAYERS:
            stages[n]()
            barrier()
        t_out = dma(out.rearrange("b (n p) d -> p (b n) d", p=128), x[:, :, :])
        SP.stop_until(t_out)

        block = ctx.enter_context(nc.Block())

        @block.sync
        def _(e):
            SP.flush(e)

        @block.gpsimd
        def _(e):
            PO.flush(e)

        @block.scalar
        def _(e):
            AC.flush(e)

        @block.vector
        def _(e):
            DV.flush(e)

        @block.tensor
        def _(e):
            PE.flush(e)


def constants():
    f, b = {}, {}
    r = np.arange(128)
    f["ident"] = np.eye(128)
    f["iota"] = np.tile(np.arange(512), (128, 1))
    f["mhalf"] = np.full((128, 16), -0.5)
    f["ridx"] = np.tile(8 - np.arange(8), (128, 16))
    g, e = np.arange(16)[:, None] // 2, np.arange(8)[None, :]
    f["coff"] = np.tile(((e // 2) * 128 + ((e % 2) ^ (g % 2)) * 64 + 1).reshape(1, 128), (128, 1))
    f["onesrow"] = np.ones((128, 512))
    f["scanreset"] = np.tile((np.arange(128) % 16 != 0), (128, 1))
    f["blockdiag"] = (r[:, None] // 8 == r[None, :] // 8)
    b["ident"] = np.eye(128)
    b["tri"] = r[:, None] < r[None, :]
    b["ones"] = np.ones((128, 128))
    b["onesrow"] = np.ones((128, 512))
    z = np.zeros((128, 512))
    for part in range(3):
        for kb in range(4):
            z[96 + part * 4 + kb, kb * 128:(kb + 1) * 128] = 1
    b["ind3"] = z
    b["ind0"] = np.zeros((128, 2))
    s = np.zeros((128, 32))
    for part in range(3):
        for d in range(8):
            s[part * 8 + d, d] = 1
    s[96, 8] = 1
    b["sel"] = s

    def pack(d):
        at, o = {}, 0
        for k, v in d.items():
            at[k] = (o, o + v.shape[1])
            o += v.shape[1]
        return np.concatenate([np.asarray(v, np.float32) for v in d.values()], 1).astype(np.float32), at

    return pack(f), pack(b)


(CONST_F, CF_AT), (CONST_B, CB_AT) = constants()

_INS = ["L0_attn_x", "L0_attn_bq", "L0_attn_bu", "L0_ffn_router_w", "L0_ffn_w0_kernel", "L0_ffn_w1_kernel",
        "L0_ffn_wo_kernel", "L1_attn_bk", "L1_attn_bka", "L1_attn_bv", "L1_attn_gamma", "L1_attn_beta",
        "L1_ffn_w3_s",
        "L2_attn_bq", "L2_attn_bk", "L2_attn_bv", "L2_attn_bo",
        "L2_ffn_Wr", "L2_ffn_br", "L2_ffn_W_up", "L2_ffn_W_down", "L2_ffn_b_down",
        "L3_attn_w_q", "L3_attn_w_k", "L3_attn_w_v", "L3_attn_w_o",
        "L3_ffn_Wr", "L3_ffn_br", "L3_ffn_W1", "L3_ffn_W2", "L3_ffn_W3", "L3_ffn_b3"]
_TRANSPOSED = {"wqT0": "L0_attn_wq", "wuT0": "L0_attn_wu", "WkT1": "L1_attn_Wk", "WkaT1": "L1_attn_Wka",
               "WvT1": "L1_attn_Wv", "w1T": "L1_ffn_w1_w", "w2T": "L1_ffn_w2_w", "h1T": "L1_ffn_h1_w",
               "h2T": "L1_ffn_h2_w", "w3T": "L1_ffn_w3_w", "WqT2": "L2_attn_Wq", "WkT2": "L2_attn_Wk",
               "WvT2": "L2_attn_Wv", "WoT2": "L2_attn_Wo"}


def kernel(**inputs):
    import concourse.bacc as _bacc
    from concourse.bass_utils import run_bass_kernel_spmd as _run

    nc = _bacc.Bacc("TRN2", target_bir_lowering=False, num_devices=1)
    arrays = {n: np.ascontiguousarray(inputs[n]) for n in _INS}
    for n, src in _TRANSPOSED.items():
        arrays[n] = np.ascontiguousarray(np.transpose(inputs[src]))
    for n in ("w1_s", "w2_s", "h1_s", "h2_s"):
        arrays[n] = np.ascontiguousarray(np.reshape(inputs["L1_ffn_" + n], (4, 128)).T)
    bup = np.zeros((128, 4, 3), np.float32)
    for f, (f0, fn) in enumerate(L2T):
        bup[0:fn, :, f] = np.transpose(inputs["L2_ffn_b_up"][:, f0:f0 + fn])
    arrays["bup"] = bup
    for n in ("b1", "b2"):
        v = np.reshape(inputs["L3_ffn_" + n], (8, -1, 128))
        arrays[n + "c"] = np.ascontiguousarray(np.transpose(v, (2, 0, 1)))
    arrays["const_f"], arrays["const_b"] = CONST_F, CONST_B
    ins = {n: nc.dram_tensor(f"in_{n}", a.shape, mybir.dt.from_np(a.dtype), kind="ExternalInput").ap()
           for n, a in arrays.items()}
    ins["scratch"] = nc.dram_tensor("scratch", (2, 3, 128, 2048), BF16, kind="Internal").ap()
    out = nc.dram_tensor("out_0", (4, 512, 128), F32, kind="ExternalOutput").ap()
    build(nc, ins, out)
    r = _run(nc, [{f"in_{n}": a for n, a in arrays.items()}], core_ids=[0])
    return r.results[0]["out_0"]
```

```python
from contextlib import ExitStack

import numpy as np

import concourse.bass as bass
from concourse import mybir

LAYERS = tuple(range(12))

ALU = mybir.AluOpType
ACT = mybir.ActivationFunctionType
F32 = mybir.dt.float32
BF16 = mybir.dt.bfloat16
F32R = mybir.dt.float32r
I32 = mybir.dt.int32
AX = mybir.AxisListType
EPS = 1e-5
NT = 16
CHUNKS = 4
FH = 688
L0T = [(i * 128, min(128, FH - i * 128)) for i in range(6)]
FM = 341
L2T = [(0, 128), (128, 128), (256, 85)]


class Eng:

    def __init__(self, name, sem):
        self.name, self.sem, self.q, self.n, self.seen = name, sem, [], 0, {}

    def wait(self, *toks):
        ws = []
        for t in flat(toks):
            key, v = t
            if self.seen.get(key.name, 0) < v:
                self.seen[key.name] = v
                ws.append(t)
        return ws

    def __call__(self, fn, *toks, inc=True):
        self.q.append((self.wait(*toks), fn, (self.sem, 1) if inc else None))
        if inc:
            self.n += 1
        return (self.sem, self.n) if inc else None

    def stop_until(self, *toks):
        self.q.append((self.wait(*toks), None, None))

    def flush(self, eng):
        for ws, fn, inc in self.q:
            for s, v in ws:
                eng.wait_ge(s, v)
            if fn is not None:
                ins = fn(eng)
                if inc is not None:
                    ins.then_inc(*inc)


def flat(toks):
    for t in toks:
        if t is None:
            continue
        if isinstance(t, list):
            yield from flat(t)
        else:
            yield t


class Ring:

    def __init__(self, bufs):
        self.bufs, self.free, self.i = bufs, [[] for _ in bufs], -1

    def next(self):
        self.i = (self.i + 1) % len(self.bufs)
        return self.bufs[self.i], self.free[self.i], self.i


def build(nc, ins, out):
    ctx = ExitStack()
    with ctx:
        sem = lambda n: ctx.enter_context(nc.semaphore(n))
        sb = lambda n, s, d=F32: ctx.enter_context(nc.sbuf_tensor(n, s, d))
        psum = ctx.enter_context(nc.psum_tensor("psum", [128, 4096], F32))
        bank = [psum[:, i * 512:(i + 1) * 512] for i in range(8)]
        PE, AC, DV, PO, SP = (Eng(n, sem("s_" + n)) for n in ("pe", "act", "dve", "pool", "sp"))
        dsems = [sem(f"s_dma{i}") for i in range(96)]
        dcount = [0] * 96
        dma_last = {}
        psems = [sem(f"s_pdma{i}") for i in range(16)]
        pcount = [0] * 16
        state = {"d": 0, "p": 0}

        def dma(o, i, *w, eng=SP):
            k = state["d"] % 96
            state["d"] += 1
            dcount[k] += 16
            dma_last[k] = (dsems[k], dcount[k])
            eng.q.append((eng.wait(*w), lambda e, o=o, i=i: e.dma_start(o, i), (dsems[k], 16)))
            return dma_last[k]

        def barrier():
            toks = [(e.sem, e.n) for e in (PE, AC, DV, PO) if e.n] + list(dma_last.values())
            for e in (PE, AC, DV, PO, SP):
                e.stop_until(toks)

        def mm(o, l, r, *w, start=True, stop=True, inc=False, skip=False):
            return PE(lambda e: e.matmul(o, l, r, start=start, stop=stop, skip_group_check=skip), *w, inc=inc)

        def fine(n, f=1):
            return take(n, F32R), take(n, F32R)

        def mm3(o, l, r, *w, start=True, stop=True, inc=False):
            mm(o, l[0], r[0], *w, start=start, stop=False)
            mm(o, l[0], r[1], start=False, stop=False)
            return mm(o, l[1], r[0], start=False, stop=stop, inc=inc)

        def halve(src, pair, *w, hi=None, lo=None):
            h, l = pair
            if hi is None:
                a = acopy(h, src, *w)
            else:
                a = vcopy(h, src, *w, eng=hi)
            return [a, tt(l, src, h.bitcast(F32), ALU.subtract, a, *w, eng=lo)]

        def tp(o, i, *w, inc=False):
            p = i.shape[0]
            idn = ident[0:p, 0:p] if i.dtype == F32 else identb[0:p, 0:p]
            return PE(lambda e: e.transpose(o, i, idn), *w, inc=inc)

        def act(o, i, f, *w, bias=0.0, scale=1.0, accum=None):
            return AC(lambda e: e.activation(o, i, f, bias=bias, scale=scale, accum_out=accum), *w)

        def acopy(o, i, *w):
            return AC(lambda e: e.copy(o, i), *w)

        def tt(o, a, b, op, *w, eng=None):
            return (eng or DV)(lambda e: e.tensor_tensor(o, a, b, op), *w)

        def ts(o, a, s1, s2, op0, op1, *w, eng=None):
            return (eng or DV)(lambda e: e.tensor_scalar(o, a, s1, s2, op0, op1) if op1 is not None
                               else e.tensor_scalar(o, a, s1, None, op0), *w)

        def stt(o, a, s, b, op0, op1, *w):
            return DV(lambda e: e.scalar_tensor_tensor(o, a, s, b, op0, op1), *w)

        def red(o, a, op, *w, axis=None):
            return DV(lambda e: e.tensor_reduce(o, a, axis or AX.X, op), *w)

        def vcopy(o, i, *w, eng=None):
            return (eng or DV)(lambda e: e.tensor_copy(o, i), *w)

        def mset(o, v, *w, eng=None):
            return (eng or DV)(lambda e: e.memset(o, v), *w)

        x = sb("x", [128, NT, 128])
        XN = [sb(f"xn{i}", [128, NT, 128]) for i in range(2)]
        XT = [sb(f"xT{i}", [128, 2048]) for i in range(2)]
        NCF = CONST_F.shape[1]
        cf = sb("cf", [128, NCF])
        NCB = CONST_B.shape[1]
        cb = sb("cb", [128, NCB], BF16)
        st = sb("st", [128, NT, 6])
        mv = sb("mv", [128, NT, 2])
        rs = sb("rs", [128, NT])
        scope = {"stack": ExitStack(), "n": 0}

        def reset():
            scope["stack"].close()
            scope["stack"] = ExitStack()

        def take(n, dt=F32):
            scope["n"] += 1
            t = scope["stack"].enter_context(nc.sbuf_tensor(f"t{scope['n']}", [128, n], dt))
            return t[:, :]

        def cF(name):
            a, b = CF_AT[name]
            return cf[:, a:b]

        def cB(name):
            a, b = CB_AT[name]
            return cb[:, a:b]

        ident, iota = cF("ident"), cF("iota")
        identb, tri, onesb = cB("ident"), cB("tri"), cB("ones")

        t_c = dma(cf[:, :], ins["const_f"])
        cb0 = take(NCB)
        t_cb0 = dma(cb0, ins["const_b"])
        x_dram = ins["L0_attn_x"].rearrange("b (n p) d -> p (b n) d", p=128)
        o_dram = out.rearrange("b (n p) d -> p (b n) d", p=128)
        t_x = [dma(x[:, 4 * c:4 * c + 4, :], x_dram[:, 4 * c:4 * c + 4, :]) for c in range(CHUNKS)]
        t_cb = vcopy(cb[:, :], cb0, t_cb0)
        S = {"par": 1, "last": False, "feat": True, "wait": None, "txn": [], "tx": []}

        def ln_chunk(c, src, dst, *w):
            s0, s1 = 4 * c, 4 * c + 4
            for t in range(s0, s1):
                a = DV(lambda e, t=t: e.bn_stats(st[:, t, :], src[:, t, :]), *w)
            for t in range(s0, s1):
                a = DV(lambda e, t=t: e.bn_aggr(mv[:, t, :], st[:, t, :]), a)
            b = ts(rs[:, s0:s1], mv[:, s0:s1, 1], EPS, None, ALU.add, None, a, eng=PO)
            b = tt(rs[:, s0:s1], rs[:, s0:s1], cF("mhalf")[:, s0:s1], ALU.pow, b, t_c, eng=PO)
            for t in range(s0, s1):
                a = ts(dst[:, t, :], src[:, t, :], mv[:, t, 0:1], rs[:, t:t + 1], ALU.subtract, ALU.mult, b)
            return a

        def features_chunk(c, src, dst, w, banks, post=None):
            p, free, i = banks.next()
            for j in range(4):
                a = tp(p[:, j * 128:(j + 1) * 128], src[:, 4 * c + j, :], w, free, t_c, inc=(j == 3))
            o = dst[:, c * 512:(c + 1) * 512]
            a = acopy(o, p[:, :], a) if post is None else post(o, p[:, :], a)
            banks.free[i] = [a]
            return a

        def finish(c, tok, banks):
            if S["last"]:
                S.setdefault("out", []).append(dma(o_dram[:, 4 * c:4 * c + 4, :], x[:, 4 * c:4 * c + 4, :], tok))
                return
            n = 1 - S["par"]
            S["txn"].append(ln_chunk(c, x, XN[n], tok))
            flush_features()
            if S["feat"]:
                S["wait"] = (c, S["txn"][c], banks)

        def flush_features():
            if S["wait"] is not None:
                c, t, banks = S["wait"]
                n = 1 - S["par"]
                S["tx"].append(features_chunk(c, XN[n], XT[n], t, banks))
                S["wait"] = None

        def begin():
            flush_features()
            barrier()
            reset()
            S["par"] = 1 - S["par"]
            r = XN[S["par"]], XT[S["par"]], S["txn"], S["tx"]
            S["txn"], S["tx"] = [], []
            return r

        def router(xT, tx, w, wb, lgp, raw, tmp, mx, t_w, bias=None):
            for t in range(NT):
                a = mm(lgp[:, t * 8:t * 8 + 8], xT[:, t * 128:(t + 1) * 128], w, tx, t_w, inc=(t == NT - 1))
            lg = lgp[:, 0:128].rearrange("p (t e) -> p t e", e=8)
            if bias is not None:
                a = tt(tmp, lg, bias.unsqueeze(1).to_broadcast([128, NT, 8]), ALU.add, a)
                lg = tmp
            if raw is None:
                return lg, a
            a = red(mx, lg, ALU.max, a)
            a = tt(tmp, lg, mx.unsqueeze(2).to_broadcast([128, NT, 8]), ALU.subtract, a)
            a = act(tmp, tmp, ACT.Exp, a)
            b = red(mx, tmp, ALU.add, a)
            b = DV(lambda e: e.reciprocal(mx, mx), b)
            b = tt(raw, tmp, mx.unsqueeze(2).to_broadcast([128, NT, 8]), ALU.mult, b)
            return raw, b

        def argmax_mask(v, m, mx, tmp, vm, a):
            bc = lambda q: q.unsqueeze(2).to_broadcast([128, NT, 8])
            a = red(mx, v, ALU.max, a)
            a = tt(tmp, v, bc(mx), ALU.is_equal, a)
            a = tt(tmp, tmp, cF("ridx").rearrange("p (t e) -> p t e", e=8), ALU.mult, a)
            a = red(vm, tmp, ALU.max, a)
            return tt(m, tmp, bc(vm), ALU.is_equal, a)

        def l0_ffn():
            xn, xT, txn, tx = begin()
            banks = Ring(bank[0:2])
            rw = take(8)
            t_rw = dma(rw, ins["L0_ffn_router_w"])
            wbuf = [(take(FH), take(FH), take(6 * 128).rearrange("p (f n) -> p f n", n=128)) for _ in range(2)]
            whl = [(fine(FH), fine(FH)) for _ in range(2)]
            t_in, t_wo, t_up, t_out, twh = {}, {}, {}, {}, {}

            def load_in(e):
                t_in[e] = [dma(wbuf[e % 2][i], ins[f"L0_ffn_w{i}_kernel"][e], twh.get(e - 2)) for i in range(2)]

            def load_out(e):
                bo = wbuf[e % 2][2]
                t_wo[e] = [dma(bo[:, 0:5, :], ins["L0_ffn_wo_kernel"][e, 0:640].rearrange("(f p) n -> p f n", p=128), t_out.get(e - 2)),
                           dma(bo[0:48, 5, :], ins["L0_ffn_wo_kernel"][e, 640:FH], t_out.get(e - 2))]

            def split_w(e):
                h = [halve(wbuf[e % 2][i], whl[e % 2][i], t_in[e][i], t_up.get(e - 2), hi=DV) for i in range(2)]
                twh[e] = [t for q in h for t in q]
                if e + 2 < 8:
                    load_in(e + 2)

            for e in range(2):
                load_in(e)
                load_out(e)
            v3 = lambda: take(128).rearrange("p (t e) -> p t e", e=8)
            raw, tmp, m1, m2, rest, q1 = v3(), v3(), v3(), v3(), v3(), v3()
            mx, mx1, mx2, vm, sl1, sl2 = (take(16) for _ in range(6))
            cnt = take(64).rearrange("p (g e) -> p g e", e=8)
            m1b, m2b = take(128, BF16), take(128, BF16)
            raw, a = router(xT, tx, rw, None, bank[2], raw, tmp, mx, t_rw)
            xsr = Ring([fine(256)])
            split_w(0)
            a = argmax_mask(raw, m1, mx1, tmp, vm, a)
            b1 = vcopy(m1b, m1.rearrange("p t e -> p (t e)"), a)
            a = tt(rest, raw, m1, ALU.mult, a)
            a = tt(rest, raw, rest, ALU.subtract, a)
            a = argmax_mask(rest, m2, mx2, tmp, vm, a)
            b2 = vcopy(m2b, m2.rearrange("p t e -> p (t e)"), a)
            m4 = lambda m: m.rearrange("p (g j e) -> p g j e", j=2, e=8)

            def prefix(p, mb, w):
                mm(p[:, 0:128], tri, mb, w, start=True, stop=False, skip=True)
                return mm(m4(p[:, 0:128])[:, :, 1, :], onesb, m4(mb)[:, :, 0, :], start=False, stop=True, inc=True, skip=True)

            c1 = prefix(bank[3], m1b, [b1, t_cb])
            mm(bank[4][:, 0:64], onesb, m4(m1b)[:, :, 0, :], start=True, stop=False)
            c2 = mm(bank[4][:, 0:64], onesb, m4(m1b)[:, :, 1, :], start=False, stop=True, inc=True)
            c3 = prefix(bank[5], m2b, b2)
            t3 = lambda p: p[:, 0:128].rearrange("p (t e) -> p t e", e=8)
            coff = cF("coff").rearrange("p (t e) -> p t e", e=8)

            def slots(p, m, sl, w):
                a = stt(tmp, p, 64.0, m, ALU.is_lt, ALU.mult, w)
                b = tt(q1, p, coff, ALU.add, w, a)
                a = tt(q1, q1, tmp, ALU.mult, a, b)
                a = red(sl, q1, ALU.add, a)
                return ts(sl, sl, 1.0, None, ALU.subtract, None, a)

            s1 = slots(t3(bank[3]), m1, sl1, c1)
            a = ts(cnt, bank[4][:, 0:64].rearrange("p (g e) -> p g e", e=8), 64.0, None, ALU.min, None, c2)
            a = tt(rest.rearrange("p (g j) e -> p g j e", j=2), m4(bank[5][:, 0:128]),
                   cnt.unsqueeze(2).to_broadcast([128, 8, 2, 8]), ALU.add, a, c3, s1)
            s2 = slots(rest, m2, sl2, a)

            xd = fine(8 * 512)
            xdv = [z.rearrange("p (k h g s c) -> p k h g s c", k=4, h=2, g=4, s=2) for z in xd]
            d_r = Ring([take(512, F32R) for _ in range(3)])
            td = []

            def arrange(g):
                p, pf, pi = banks.next()
                xs, xsf, xsi = xsr.next()
                t_xs = halve(xn[:, 2 * g:2 * g + 2, :].rearrange("p t n -> p (t n)"), xs, txn[g // 2], xsf)
                for j in range(2):
                    t = 2 * g + j
                    d, df, di = d_r.next()
                    a = ts(d, iota, sl1[:, t:t + 1], None, ALU.is_equal, None, s1, df, t_c, eng=PO)
                    a = stt(d, iota, sl2[:, t:t + 1], d.bitcast(F32), ALU.is_equal, ALU.add, a, s2)
                    u = slice(j * 128, (j + 1) * 128)
                    mm(p[:, :], xs[0][:, u], d, a, pf, t_xs, start=(j == 0), stop=False)
                    b = mm(p[:, :], xs[1][:, u], d, start=False, stop=(j == 1), inc=True)
                    d_r.free[di] = [b]
                xsr.free[xsi] = [b]
                return p, pi, b

            def place(g, p, pi, b):
                pv = p[:, :].rearrange("p (k s c) -> p k s c", k=4, s=2)
                to = [[z[:, :, s ^ (g % 2), g // 2, s, :] for z in xdv] for s in range(2)]
                b = [acopy(to[s][0], pv[:, :, s, :], b) for s in range(2)]
                b = [tt(to[s][1], pv[:, :, s, :], to[s][0].bitcast(F32), ALU.subtract, b) for s in range(2)]
                banks.free[pi] = [b[1]]
                td.append(b[1])

            ready = arrange(0)
            for g in range(8):
                after = arrange(g + 1) if g + 1 < 8 else None
                place(g, *ready)
                ready = after
            ct = take(NT * 512).rearrange("p (t n) -> p t n", t=NT)
            cring = Ring([take(512) for _ in range(2)])
            cc = ct[:, NT - 1, :]
            T = {}
            cbank = Ring([bank[7]])
            tct = []

            def weigh(t):
                ca, cfree, ci = cring.next()
                a1 = ts(ca, iota, sl1[:, t:t + 1], mx1[:, t:t + 1], ALU.is_equal, ALU.mult, s1, cfree)
                a2 = ts(cc, iota, sl2[:, t:t + 1], mx2[:, t:t + 1], ALU.is_equal, ALU.mult, s2, T.get("cc"))
                T["cc"] = tt(ca, ca, cc, ALU.add, a1, a2)
                T[t] = (ca, ci, T["cc"])

            def turn(t):
                ca, ci, a = T[t]
                p, pf, pi = cbank.next()
                for k in range(4):
                    b = tp(p[:, k * 128:(k + 1) * 128], ca[:, k * 128:(k + 1) * 128], a, pf, inc=(k == 3))
                cring.free[ci] = [b]
                b = acopy(ct[:, t, :], p[:, :], b)
                cbank.free[pi] = [b]
                tct.append(b)

            eo = take(8 * 4 * 128).rearrange("p (g k n) -> p g k n", g=8, k=4)
            hid = [take(6 * 512).rearrange("p (f n) -> p f n", n=512) for _ in range(2)]
            hb = Ring([(bank[0], bank[1]), (bank[2], bank[3]), (bank[4], bank[5])])
            hb.free[0] = [banks.free[0], banks.free[1]]
            hb.free[1] = [s2]
            hb.free[2] = [s2]
            ob = Ring([bank[6]])
            teo, t_hid = [], {}

            def up(e):
                h = hid[e % 2]
                xe = [z[:, e * 512:(e + 1) * 512] for z in xd]
                for f, (f0, fn) in enumerate(L0T):
                    (p0, p1), pf, pi = hb.next()
                    mm3(p0[0:fn, :], [z[:, f0:f0 + fn] for z in whl[e % 2][0]], xe, pf, td, twh[e])
                    a = mm3(p1[0:fn, :], [z[:, f0:f0 + fn] for z in whl[e % 2][1]], xe, inc=True)
                    b = act(h[0:fn, f, :], p0[0:fn, :], ACT.Gelu_apprx_tanh, a, t_out.get(e - 2))
                    b = tt(h[0:fn, f, :], h[0:fn, f, :], p1[0:fn, :], ALU.mult, b)
                    hb.free[pi] = [b]
                t_up[e], t_hid[e] = a, b

            def down(e):
                h, wo = hid[e % 2], wbuf[e % 2][2]
                p, pf, pi = ob.next()
                for s in range(4):
                    for f, (f0, fn) in enumerate(L0T):
                        b = mm(p[:, s * 128:(s + 1) * 128], h[0:fn, f, s * 128:(s + 1) * 128], wo[0:fn, f, :],
                               t_hid[e], pf, t_wo[e], start=(f == 0), stop=(f == 5), inc=(f == 5 and s == 3))
                t_out[e] = b
                if e + 2 < 8:
                    load_out(e + 2)
                eog = eo.rearrange("p (g h) k n -> p g h k n", h=2)
                pg = p[:, :].rearrange("p (g n) -> p g n", g=4)
                c_ = [acopy(eog[64 * s:64 * s + 64, :, s ^ (e % 2), e // 2, :], pg[64 * s:64 * s + 64, :, :], b)
                      for s in range(2)]
                ob.free[pi] = [c_[-1]]
                teo.append(c_[-1])

            for e in range(9):
                if e < 8:
                    up(e)
                if e > 0:
                    turn(2 * e - 1)
                if e + 1 < 8:
                    split_w(e + 1)
                if e < 8:
                    weigh(2 * e)
                if e > 0:
                    down(e - 1)
                if e < 8:
                    weigh(2 * e + 1)
                    turn(2 * e)
            yb = Ring([bank[0], bank[1], bank[2], bank[3]])
            for i in range(4):
                yb.free[i] = [t_hid[7]]
            for t in range(NT):
                p, pf, pi = yb.next()
                for k in range(4):
                    b = mm(p[:, 0:128], ct[:, t, k * 128:(k + 1) * 128], eo[:, t // 2, k, :], tct[t], teo, pf,
                           start=(k == 0), stop=(k == 3), inc=(k == 3))
                b = stt(x[:, t, :], p[:, 0:128], 0.5, x[:, t, :], ALU.mult, ALU.add, b)
                yb.free[pi] = [b]
                if t % 4 == 3:
                    finish(t // 4, b, yb)

        def l1_ffn():
            xn, xT, txn, tx = begin()
            w1, w2 = take(512), take(512)
            h1 = take(2048).rearrange("p (k n) -> p k n", k=4)
            h2 = take(2048).rearrange("p (k n) -> p k n", k=4)
            w3 = take(512).rearrange("p (k n) -> p k n", k=4)
            sc = take(16).rearrange("p (a f) -> p a f", a=4)
            s3 = take(128)
            t_w = [dma(w1, ins["w1T"]), dma(w2, ins["w2T"])]
            t_s = [dma(sc[:, i, :], ins[n]) for i, n in enumerate(("w1_s", "w2_s", "h1_s", "h2_s"))]
            t_h1 = dma(h1, ins["h1T"].rearrange("(k p) n -> p k n", p=128))
            t_h2 = dma(h2, ins["h2T"].rearrange("(k p) n -> p k n", p=128))
            t_w3 = dma(w3, ins["w3T"].rearrange("(k p) n -> p k n", p=128))
            t_s3 = dma(s3, ins["L1_ffn_w3_s"].partition_broadcast(128))
            banks = Ring(bank)
            W = {n: fine(z) for n, z in (("w1", 512), ("w2", 512), ("h1", 2048), ("h2", 2048))}
            xr = Ring([fine(512) for _ in range(2)])
            tw = {}

            def x_halves(c):
                xx, xf, xi = xr.next()
                return xx, xi, halve(xT[:, c * 512:(c + 1) * 512], xx, tx[c], xf)

            tw["w1"] = halve(w1, W["w1"], t_w[0])
            xx, xi, txx = x_halves(0)
            tw["w2"] = halve(w2, W["w2"], t_w[1])
            flat2 = lambda q: q.rearrange("p k n -> p (k n)")
            tw["h1"] = halve(flat2(h1), W["h1"], t_h1, hi=PO)
            tw["h2"] = halve(flat2(h2), W["h2"], t_h2, hi=PO, lo=PO)
            hr = Ring([fine(2048) for _ in range(3)])
            tr = Ring([take(512) for _ in range(3)])
            last = Ring([take(2048).rearrange("p (k n) -> p k n", k=4) for _ in range(2)])
            tmp = take(512)
            for c in range(CHUNKS):
                h, hf, hi = hr.next()
                ta = []
                for f in range(4):
                    fs = slice(f * 128, (f + 1) * 128)
                    p0, pf0, i0 = banks.next()
                    a = mm3(p0, [z[:, fs] for z in W["w1"]], xx, txx, tw["w1"], pf0, inc=True)
                    p1, pf1, i1 = banks.next()
                    b = mm3(p1, [z[:, fs] for z in W["w2"]], xx, tw["w2"], pf1, inc=True)
                    q, qf, qi = tr.next()
                    a = act(q, p0, ACT.Silu, a, qf, t_s, scale=sc[:, 0, f:f + 1])
                    banks.free[i0] = [a]
                    a = stt(q, p1, sc[:, 1, f:f + 1], q, ALU.mult, ALU.mult, a, b)
                    banks.free[i1] = [a]
                    a = halve(q, [z[:, f * 512:(f + 1) * 512] for z in h], a, hf)
                    tr.free[qi] = [a[1]]
                    ta.append(list(a))
                xr.free[xi] = [b]
                if c + 1 < CHUNKS:
                    xx, xi, txx = x_halves(c + 1)
                for wn, si in (("h1", 2), ("h2", 3)):
                    if wn == "h1":
                        g, gf, gi = hr.next()
                    else:
                        g, gf, gi = last.next()
                    tb = []
                    for f in range(4):
                        p, pf, pi = banks.next()
                        for k in range(4):
                            o = k * 512 + f * 128
                            a = mm3(p, [z[:, o:o + 128] for z in W[wn]], [z[:, k * 512:(k + 1) * 512] for z in h],
                                    ta[k], tw[wn], pf, start=(k == 0), stop=(k == 3), inc=(k == 3))
                        if wn == "h1":
                            q, qf, qi = tr.next()
                            b = act(q, p, ACT.Gelu, a, qf, scale=sc[:, si, f:f + 1])
                            banks.free[pi] = [b]
                            b = halve(q, [z[:, f * 512:(f + 1) * 512] for z in g], b, gf)
                            tr.free[qi] = [b[1]]
                            b = list(b)
                        else:
                            b = act(g[:, f, :], p, ACT.Gelu, a, gf, scale=sc[:, si, f:f + 1])
                            banks.free[pi] = [b]
                        tb.append(b)
                    hr.free[hi] = [a]
                    h, hi, ta = g, gi, tb
                for j in range(4):
                    t = 4 * c + j
                    p, pf, pi = banks.next()
                    for k in range(4):
                        a = mm(p[:, 0:128], h[:, k, j * 128:(j + 1) * 128], w3[:, k, :], ta[k], t_w3, pf,
                               start=(k == 0), stop=(k == 3), inc=(k == 3))
                    b = stt(tmp[:, j * 128:(j + 1) * 128], p[:, 0:128], 0.5, s3, ALU.mult, ALU.mult, a, t_s3)
                    banks.free[pi] = [b]
                    b = tt(x[:, t, :], x[:, t, :], tmp[:, j * 128:(j + 1) * 128], ALU.add, b)
                last.free[hi] = [a]
                finish(c, b, banks)

        def l1_attn():
            xn, xT, txn, tx = begin()
            wk, wka, wv = take(128), take(128), take(128)
            cols = take(5)
            t_w = [dma(wk, ins["WkT1"]), dma(wka, ins["WkaT1"]), dma(wv, ins["WvT1"])]
            t_w += [dma(cols[:, i:i + 1], ins["L1_attn_" + n].rearrange("(p a) -> p a", a=1))
                    for i, n in enumerate(("gamma", "beta", "bk", "bka", "bv"))]
            banks = Ring(bank)
            a = ts(cols[:, 3:4], cols[:, 3:4], 128 ** -0.5, None, ALU.mult, None, t_w)
            txn = [ln_chunk(c, xn, xn, txn[c]) for c in range(CHUNKS)]
            tx = [features_chunk(c, xn, xT, txn[c], banks, post=lambda o, p, w: ts(
                o, p, cols[:, 0:1], cols[:, 1:2], ALU.mult, ALU.add, w, t_w)) for c in range(CHUNKS)]
            ka = a
            keys, vals, kw, cum, pr = (take(2048) for _ in range(5))
            ones = cF("onesrow")
            for c in range(CHUNKS):
                s = slice(c * 512, (c + 1) * 512)
                p, pf, pi = banks.next()
                a = mm(p[:, :], wk, xT[:, s], tx[c], t_w, pf, inc=True)
                k_ = act(keys[:, s], p[:, :], ACT.Identity, a, bias=cols[:, 2:3])
                banks.free[pi] = [k_]
                p, pf, pi = banks.next()
                a = mm(p[:, :], wv, xT[:, s], pf, inc=True)
                v_ = act(vals[:, s], p[:, :], ACT.Identity, a, bias=cols[:, 4:5])
                banks.free[pi] = [v_]
                p, pf, pi = banks.next()
                a = mm(p[:, :], wka, keys[:, s], k_, pf, inc=True)
                w_ = act(kw[:, s], p[:, :], ACT.Exp, a, ka, bias=cols[:, 3:4], scale=128 ** -0.5)
                banks.free[pi] = [w_]
                a = DV(lambda e, s=s: e.tensor_tensor_scan(cum[:, s], ones, kw[:, s], 0.0, ALU.mult, ALU.add), w_)
                a = DV(lambda e, s=s: e.reciprocal(cum[:, s], cum[:, s]), a)
                a = tt(kw[:, s], kw[:, s], cum[:, s], ALU.mult, a)
                a = tt(kw[:, s], kw[:, s], keys[:, s], ALU.mult, a)
                a = DV(lambda e, s=s: e.tensor_tensor_scan(cum[:, s], ones, kw[:, s], 0.0, ALU.mult, ALU.add), a)
                a = tt(pr[:, s], cum[:, s], vals[:, s], ALU.mult, a, v_)
                p, pf, pi = banks.next()
                for j in range(4):
                    b = tp(p[:, j * 128:(j + 1) * 128], pr[:, c * 512 + j * 128:c * 512 + (j + 1) * 128], a, pf, inc=(j == 3))
                xc = x[:, 4 * c:4 * c + 4, :].rearrange("p t n -> p (t n)")
                b = tt(xc, xc, p[:, :], ALU.add, b)
                banks.free[pi] = [b]
                finish(c, b, banks)

        def transposed_gates(g, gT, p, a):
            last = {}
            for c in range(CHUNKS):
                for j in range(4):
                    t = 4 * c + j
                    b = tp(p[c][0:8, j * 128:(j + 1) * 128], g[:, t, :], a, last.get(c - 2), inc=(j == 3))
                b = acopy(gT[0:8, c * 512:(c + 1) * 512], p[c][0:8, :], b)
                last[c] = b
            return b

        def l2_ffn():
            xn, xT, txn, tx = begin()
            wr = take(8)
            wrb = take(8)
            wu = take(4 * FM)
            bu = take(12).rearrange("p (g f) -> p g f", g=4)
            wd = take(3 * 8 * 128)
            wdv = wd.rearrange("p (f e n) -> p f e n", f=3, e=8)
            bd = take(128)
            t_r = [dma(wr, ins["L2_ffn_Wr"]), dma(wrb, ins["L2_ffn_br"].partition_broadcast(128))]
            t_wu = dma(wu.rearrange("p (g f) -> p g f", g=4), ins["L2_ffn_W_up"].rearrange("g p f -> p g f"))
            t_bu = dma(bu[:, :, :], ins["bup"])
            t_wd = [dma(wdv[:, 0:2, e, :], ins["L2_ffn_W_down"][e, 0:256].rearrange("(f p) n -> p f n", p=128)) for e in range(8)]
            t_wd += [dma(wdv[0:85, 2, :, :], ins["L2_ffn_W_down"][:, 256:FM].rearrange("e p n -> p e n"))]
            t_bd = dma(bd[0:8, :], ins["L2_ffn_b_down"])
            v3 = lambda: take(128).rearrange("p (t e) -> p t e", e=8)
            raw, tmp, eq, gt, gate = v3(), v3(), v3(), v3(), v3()
            mx = take(16)
            cnt, tmp8, need = take(24), take(8), take(8)
            raw, a = router(xT, tx, wr, None, bank[2], raw, tmp, mx, t_r, bias=wrb)
            cmpb = take(384, BF16)
            cmpv = cmpb[:, 0:128].rearrange("p (t e) -> p t e", e=8)
            b8 = lambda q: q.unsqueeze(1).to_broadcast([128, NT, 8])
            sp = bank[3]

            whu, whd = fine(4 * FM), fine(3 * 8 * 128)
            xr = Ring([fine(512) for _ in range(2)])
            mr = Ring([take(3 * 512) for _ in range(10)])
            ub = Ring(bank[0:3])
            ub.free[2] = [a]
            item, xh = {}, {}

            def halve_rows(src, pair, cut, *w, lo=None):
                u = halve(src[:, 0:cut], [z[:, 0:cut] for z in pair], *w, lo=lo)
                v = halve(src[0:85, cut:], [z[0:85, cut:] for z in pair], *w, lo=PO)
                return u + v

            hl = Ring([fine(3 * 512) for _ in range(2)])
            halves = {}

            def halve_item(n):
                m, mi, tm, _ = item[n]
                pair, hf, hi = hl.next()
                halves[n] = (pair, hi, halve_rows(m, pair, 1024, tm, hf, lo=PO if n < 2 else None))
                mr.free[mi] = halves[n][2]

            t_whu = halve(wu, whu, t_wu)
            t_whd = []

            def halve_down(i):
                r, o = slice(0, 128 if i < 4 else 85), slice(i * 512, (i + 1) * 512)
                t_whd.extend(halve(wd[r, o], [z[r, o] for z in whd], t_wd, lo=PO))


            def x_halves(c):
                xx, xf, xi = xr.next()
                xh[c] = (xx, xi, halve(xT[:, c * 512:(c + 1) * 512], xx, tx[c], xf, lo=PO))

            def up(n, f):
                c, g = n // 4, n % 4
                xx, xi, txx = xh[c]
                if f == 0:
                    m, mf, mi = mr.next()
                    item[n] = [m, mi, [], mf]
                m, mi, tm, mf = item[n]
                f0, fn = L2T[f]
                p, pf, pi = ub.next()
                a = mm3(p[0:fn, :], [z[:, g * FM + f0:g * FM + f0 + fn] for z in whu], xx, txx, t_whu, pf, inc=True)
                b = act(m[0:fn, f * 512:(f + 1) * 512], p[0:fn, :], ACT.Silu, a, mf, t_bu, bias=bu[0:fn, g, f:f + 1])
                ub.free[pi] = [b]
                tm.append(b)
                if g == 3 and f == 2:
                    xr.free[xi] = [a]

            ups = iter([(n, f) for n in range(16) for f in range(3)])

            def up_next():
                n, f = next(ups)
                if n % 4 == 0 and f == 0 and n // 4 + 1 < CHUNKS:
                    x_halves(n // 4 + 1)
                up(n, f)

            def count(cols, w):
                c_ = mm(sp[:, 0:cols], onesb, cmpb[:, 0:cols], w, inc=True)
                k = cols // 128
                return red(cnt[:, 0:8 * k].rearrange("p (j e) -> p j e", e=8),
                           sp[:, 0:cols].rearrange("p (j t e) -> p j e t", j=k, e=8), ALU.add, c_)

            x_halves(0)
            sel = [take(32).rearrange("p (j e) -> p j e", e=8) for _ in range(2)]
            cand = take(24).rearrange("p (j e) -> p j e", e=8)
            b = mset(sel[0][:, 3, :], 0.0, a)
            r4 = lambda q: q.unsqueeze(1).to_broadcast([128, 3, NT, 8])
            for step, bit in enumerate(range(28, -1, -2)):
                s, lo = sel[step % 2], sel[step % 2][:, 3, :]
                w = b
                for j in range(3):
                    b = ts(cand[:, j, :].bitcast(I32), lo.bitcast(I32), (j + 1) << bit, None, ALU.bitwise_or, None, w)
                b = tt(cmpb.rearrange("p (j t e) -> p j t e", j=3, e=8), r4(raw),
                       cand.unsqueeze(2).to_broadcast([128, 3, NT, 8]), ALU.is_ge, b)
                b = count(384, b)
                up_next()
                up_next()
                if 4 <= step < 10:
                    halve_down(step - 4)
                if step in (10, 12):
                    halve_item(step // 2 - 5)
                b = stt(s[:, 0:3, :], cnt.rearrange("p (j e) -> p j e", e=8), 256.0, cand, ALU.is_ge, ALU.mult, b)
                b = red(sel[1 - step % 2][:, 3, :], s.rearrange("p j e -> p e j"), ALU.max, b)
            lo = sel[1][:, 3, :]
            g_ = tt(gt, raw, b8(lo), ALU.is_gt, b)
            q_ = tt(eq, raw, b8(lo), ALU.is_equal, g_)
            c_ = vcopy(cmpv, gt, g_)
            vcopy(cmpb[:, 128:256].rearrange("p (t e) -> p t e", e=8), eq, q_)
            b = count(128, (DV.sem, DV.n))
            b = ts(need, cnt[:, 0:8], -1.0, 256.0, ALU.mult, ALU.add, b)
            mm(bank[4][:, 0:128], tri, cmpb[:, 128:256], inc=False)
            q_ = mm(bank[5][:, 0:128], onesb, cmpb[:, 128:256], inc=True)
            tot = take(128)
            pre = take(128)
            q_ = vcopy(tot.rearrange("p (e t) -> p e t", e=8), bank[5][:, 0:128].rearrange("p (t e) -> p e t", e=8), q_)
            q_ = DV(lambda e: e.tensor_tensor_scan(pre, cF("scanreset"), tot, 0.0, ALU.mult, ALU.add), q_)
            q_ = tt(pre, pre, tot, ALU.subtract, q_)
            q_ = tt(tmp, bank[4][:, 0:128].rearrange("p (t e) -> p t e", e=8), pre.rearrange("p (e t) -> p t e", e=8), ALU.add, q_)
            q_ = tt(tmp, tmp, b8(need), ALU.is_lt, q_, b)
            q_ = tt(tmp, tmp, eq, ALU.mult, q_)
            q_ = tt(gt, gt, tmp, ALU.add, q_)
            q_ = stt(gate, gt, 0.5, raw, ALU.mult, ALU.mult, q_)

            gT = take(2048)
            yb = Ring([bank[i] for i in (6, 7, 3, 4, 5)])
            yb.free[2] = [b]
            yb.free[3] = yb.free[4] = [q_]
            for n in range(16):
                c, g = n // 4, n % 4
                pair, hi, th = halves[n]
                for j in range(4):
                    t = 4 * c + j
                    if (n, j) == (0, 3):
                        t_g = transposed_gates(gate, gT, [bank[i] for i in (4, 5, 4, 5)], q_)
                        yb.free[3] = yb.free[4] = [t_g]
                    if g == 1:
                        p, pf, pi = yb.next()
                        a = mm(p[:, 0:128], gT[0:8, t * 128:(t + 1) * 128], bd[0:8, :], t_g, t_bd, pf, inc=True)
                        b = tt(x[:, t, :], x[:, t, :], p[:, 0:128], ALU.add, a)
                        yb.free[pi] = [b]
                    p, pf, pi = yb.next()
                    for f, (f0, fn) in enumerate(L2T):
                        o = f * 512 + j * 128
                        wo = f * 1024 + g * 256
                        a = mm3(p[:, 0:256], [z[0:fn, o:o + 128] for z in pair], [z[0:fn, wo:wo + 256] for z in whd],
                                th, t_whd, pf, start=(f == 0), stop=(f == 2), inc=(f == 2))
                    for h in range(2):
                        e = 2 * g + h
                        b = stt(x[:, t, :], p[:, h * 128:(h + 1) * 128], gate[:, t, e:e + 1], x[:, t, :],
                                ALU.mult, ALU.add, a, b, q_)
                    yb.free[pi] = [b]
                hl.free[hi] = [a]
                if n + 10 < 16:
                    for _ in range(3):
                        up_next()
                if n + 2 < 16:
                    halve_item(n + 2)
                if g == 3:
                    finish(c, b, yb)

        def l2_attn():
            xn, xT, txn, tx = begin()
            wq, wk, wv, wo = (take(128) for _ in range(4))
            bq = take(1)
            bkb, bvb, bob = (take(128) for _ in range(3))
            t_w = [dma(wq, ins["WqT2"]), dma(wk, ins["WkT2"]), dma(wv, ins["WvT2"]), dma(wo, ins["WoT2"]),
                   dma(bq, ins["L2_attn_bq"].rearrange("(p a) -> p a", a=1))]
            t_w += [dma(o, ins["L2_attn_" + n].partition_broadcast(128)) for o, n in ((bkb, "bk"), (bvb, "bv"), (bob, "bo"))]
            banks = Ring(bank)
            q, tq, o = take(2048), take(2048), take(2048)
            k, tk, v = take(2048), take(2048), take(2048)
            kv = take(512)
            for b_ in range(4):
                s = slice(b_ * 512, (b_ + 1) * 512)
                p, pf, pi = banks.next()
                a = mm(p[:, :], wq, xT[:, s], tx[b_], t_w, pf, inc=True)
                q1 = ts(tq[:, s], p[:, :], bq, 0.0, ALU.add, ALU.min, a, t_w)
                q2 = ts(q[:, s], p[:, :], bq, 0.0, ALU.add, ALU.max, a)
                banks.free[pi] = [q2]
                q1 = act(tq[:, s], tq[:, s], ACT.Exp, q1)
                t_q = tt(q[:, s], q[:, s], tq[:, s], ALU.add, q1, q2)
                bc4 = lambda z: z.unsqueeze(1).to_broadcast([128, 4, 128])
                r4 = lambda z: z.rearrange("p (t n) -> p t n", t=4)
                p, pf, pi = banks.next()
                for j in range(4):
                    a = mm(p[:, j * 128:(j + 1) * 128], xT[:, b_ * 512 + j * 128:b_ * 512 + (j + 1) * 128], wk, pf, inc=(j == 3))
                k1 = tt(r4(k[:, s]), r4(p[:, :]), bc4(bkb), ALU.add, a)
                banks.free[pi] = [k1]
                k2 = ts(tk[:, s], k[:, s], 0.0, None, ALU.min, None, k1)
                k2 = act(tk[:, s], tk[:, s], ACT.Exp, k2)
                t_k = stt(k[:, s], k[:, s], 0.0, tk[:, s], ALU.max, ALU.add, k2)
                p, pf, pi = banks.next()
                for j in range(4):
                    a = mm(p[:, j * 128:(j + 1) * 128], xT[:, b_ * 512 + j * 128:b_ * 512 + (j + 1) * 128], wv, pf, inc=(j == 3))
                t_v = tt(r4(v[:, s]), r4(p[:, :]), bc4(bvb), ALU.add, a)
                banks.free[pi] = [t_v]
                p, pf, pi = banks.next()
                for j in range(4):
                    u = slice(b_ * 512 + j * 128, b_ * 512 + (j + 1) * 128)
                    a = mm(p[:, 0:128], k[:, u], v[:, u], t_k, t_v, pf, start=(j == 0), stop=(j == 3), inc=(j == 3))
                kvb = kv[:, b_ * 128:(b_ + 1) * 128]
                t_kv = tt(kvb, p[:, 0:128], cF("blockdiag"), ALU.mult, a)
                banks.free[pi] = [t_kv]
                p, pf, pi = banks.next()
                a = mm(p[:, :], kvb, q[:, s], t_kv, t_q, pf, inc=True)
                t_o = acopy(o[:, s], p[:, :], a)
                banks.free[pi] = [t_o]
                p, pf, pi = banks.next()
                for j in range(4):
                    a = mm(p[:, j * 128:(j + 1) * 128], o[:, b_ * 512 + j * 128:b_ * 512 + (j + 1) * 128], wo, t_o, pf, inc=(j == 3))
                xc = x[:, 4 * b_:4 * b_ + 4, :]
                a = tt(xc, xc, r4(p[:, :]), ALU.add, a)
                banks.free[pi] = [a]
                a = tt(xc, xc, bc4(bob), ALU.add, a)
                finish(b_, a, banks)

        def l3_ffn():
            xn, xT, txn, tx = begin()
            NTL = 15
            wr, wrb = take(8), take(8)
            t_r = [dma(wr, ins["L3_ffn_Wr"]), dma(wrb, ins["L3_ffn_br"].partition_broadcast(128))]
            wb = [(take(512), take(1024).rearrange("p (k n) -> p k n", k=4), take(256).rearrange("p (k n) -> p k n", k=2),
                   take(6), take(128)) for _ in range(4)]
            wfree = [[], [], [], []]
            wh = [(fine(512), fine(1024)) for _ in range(2)]
            t_up, t_down, tw1, tw2 = {}, {}, {}, {}

            def split_w(i):
                u, v = wb[i % 4][0:2]
                tw1[i] = halve(u, wh[i % 2][0], t_we[i], t_up.get(i - 2))
                tw2[i] = halve(v.rearrange("p k n -> p (k n)"), wh[i % 2][1], t_we[i], t_down.get(i - 2))

            v3 = lambda: take(128).rearrange("p (t e) -> p t e", e=8)
            tmp, m, mh, wi = v3(), v3(), v3(), v3()
            mx, vm = take(16), take(16)
            mb = take(128, BF16)
            a = None
            lg, a = router(xT, tx, wr, None, bank[0], None, mh, mx, t_r, bias=wrb)
            a = argmax_mask(lg, m, mx, tmp, vm, a)
            a = vcopy(mb, m.rearrange("p t e -> p (t e)"), a)
            mm(bank[1][:, 0:128], tri, mb, a)
            a = mm(bank[2][:, 0:128], onesb, mb, inc=True)
            tot, pre = take(128), take(128)
            et = lambda q: q.rearrange("p (e t) -> p e t", e=8)
            b = vcopy(et(tot), bank[2][:, 0:128].rearrange("p (t e) -> p e t", e=8), a)
            b = DV(lambda e: e.tensor_tensor_scan(pre, cF("scanreset"), tot, 0.0, ALU.mult, ALU.add), b)
            n8, cum = take(8), take(8)
            cmp8 = v3()
            k8 = cF("k256").rearrange("p (e k) -> p e k", e=8)
            c_ = tt(cmp8[:, 0:8, :], et(pre)[:, :, 15:16].to_broadcast([128, 8, 8]), k8, ALU.is_gt, b)
            c_ = red(n8, cmp8[:, 0:8, :], ALU.add, c_)
            c_ = DV(lambda e: e.tensor_tensor_scan(cum, cF("onesrow")[:, 0:8], n8, 0.0, ALU.mult, ALU.add), c_)
            i16 = cF("i16").rearrange("p (i e) -> p i e", e=8)
            d_ = tt(cmp8, cum.unsqueeze(1).to_broadcast([128, NT, 8]), i16, ALU.is_le, c_)
            te = take(16)
            d_ = red(te, cmp8, ALU.add, d_)
            d_ = ts(te.bitcast(I32), te, 7.0, None, ALU.min, None, d_)
            t_te = d_
            n8b = take(8)
            b = tt(pre, pre, tot, ALU.subtract, b, c_)
            c_ = tt(n8b, cum, n8, ALU.subtract, c_)
            c_ = ts(n8b, n8b, 256.0, None, ALU.mult, None, c_)
            b = tt(wi, bank[1][:, 0:128].rearrange("p (t e) -> p t e", e=8), pre.rearrange("p (e t) -> p t e", e=8), ALU.add, b, a)
            b = tt(wi, wi, n8b.unsqueeze(1).to_broadcast([128, NT, 8]), ALU.add, b, c_)
            b = tt(wi, wi, m, ALU.mult, b)
            slf = take(16)
            b = red(slf, wi, ALU.add, b)
            slot = take(16).bitcast(mybir.dt.uint32)
            t_slot = vcopy(slot, slf, b)
            Gd, Yd = ins["sorted_x"], ins["sorted_y"]

            def pool_dma(fn, *w):
                k = state["p"] % 16
                state["p"] += 1
                pcount[k] += 16
                dma_last["pool", k] = (psems[k], pcount[k])
                PO.q.append((PO.wait(*w), fn, (psems[k], 16)))
                return dma_last["pool", k]

            t_sc = [pool_dma(lambda e, t=t: e.indirect_dma_start(
                Gd, bass.IndirectOffsetOnAxis(ap=slot[:, t:t + 1], axis=0), xn[:, t, :], None), t_slot, txn[t // 4])
                for t in range(NT)]

            def load_w(i):
                u, v, w, bc, b3 = wb[i % 4]
                toks, incs = [], []
                for _ in range(5):
                    k = state["d"] % 96
                    state["d"] += 1
                    dcount[k] += 16
                    dma_last[k] = (dsems[k], dcount[k])
                    toks.append(dma_last[k])
                    incs.append(dsems[k])

                def fn(e):
                    ex = bass.ds(e.value_load(te[0:1, i:i + 1].bitcast(I32), min_val=0, max_val=7), 1)
                    one = lambda n: ins[n][ex]
                    e.dma_start(u, one("L3_ffn_W1").rearrange("a p n -> (a p) n")).then_inc(incs[0], 16)
                    e.dma_start(v, one("L3_ffn_W2").rearrange("a (k p) n -> (a p) k n", p=128)).then_inc(incs[1], 16)
                    e.dma_start(w, one("L3_ffn_W3").rearrange("a (k p) n -> (a p) k n", p=128)).then_inc(incs[2], 16)
                    e.dma_start(bc, one("b12c").rearrange("a p n -> (a p) n")).then_inc(incs[3], 16)
                    e.dma_start(b3, one("L3_ffn_b3").to_broadcast([128, 128])).then_inc(incs[4], 16)

                SP.q.append((SP.wait(t_te, wfree[i % 4]), fn, None))
                return toks

            t_we = {i: load_w(i) for i in range(4)}
            gr = Ring([take(256).rearrange("p (h n) -> p h n", h=2) for _ in range(3)])
            G2 = Gd.rearrange("(i h p) n -> i p h n", h=2, p=128)
            Y2 = Yd.rearrange("(i h p) n -> i p h n", h=2, p=128)
            gl = {}

            def load_g(i):
                g, gf, gi = gr.next()
                gl[i] = (g, gi, dma(g, G2[i], t_sc, gf))

            load_g(0)
            load_g(1)
            banks = Ring(bank[3:8] + bank[0:3])
            for i in range(8):
                banks.free[i] = [b, a]
            xr = Ring([fine(256) for _ in range(2)])
            h1r = Ring([fine(1024) for _ in range(2)])
            qr = Ring([take(256) for _ in range(3)])
            h2r = Ring([take(512).rearrange("p (k n) -> p k n", k=2) for _ in range(2)])
            yr = Ring([take(256).rearrange("p (h n) -> p h n", h=2) for _ in range(2)])
            t_y = []
            xg = {}

            def fetch(i):
                if i + 2 < NTL:
                    load_g(i + 2)
                g, gi, tg = gl[i]
                p, pf, pi = banks.next()
                for h in range(2):
                    a = tp(p[:, h * 128:(h + 1) * 128], g[:, h, :], tg, pf, inc=(h == 1))
                gr.free[gi] = [a]
                xx, xf, xi = xr.next()
                a = halve(p[:, 0:256], xx, a, xf)
                banks.free[pi] = [a[1]]
                xg[i] = (xx, xi, list(a))

            hs, gs = {}, {}

            def up(i):
                xx, xi, txx = xg[i]
                h, hf, hi = h1r.next()
                ta = []
                for f in range(4):
                    p, pf, pi = banks.next()
                    a = mm3(p[:, 0:256], [z[:, f * 128:(f + 1) * 128] for z in wh[i % 2][0]], xx, pf, tw1[i], txx, inc=True)
                    q, qf, qi = qr.next()
                    b = act(q, p[:, 0:256], ACT.Gelu, a, qf, t_we[i], bias=wb[i % 4][3][:, f:f + 1])
                    banks.free[pi] = [b]
                    b = halve(q, [z[:, f * 256:(f + 1) * 256] for z in h], b, hf)
                    qr.free[qi] = [b[1]]
                    ta.append(b)
                t_up[i] = xr.free[xi] = [a]
                hs[i] = (h, hi, ta)

            def down(i):
                h, hi, ta = hs[i]
                g, gf, gi = h2r.next()
                tb = []
                for f in range(2):
                    p, pf, pi = banks.next()
                    for k in range(4):
                        o = k * 256 + f * 128
                        a = mm3(p[:, 0:256], [z[:, o:o + 128] for z in wh[i % 2][1]], [z[:, k * 256:(k + 1) * 256] for z in h],
                                ta[k], tw2[i], pf, start=(k == 0), stop=(k == 3), inc=(k == 3))
                    b = act(g[:, f, :], p[:, 0:256], ACT.Gelu, a, gf, bias=wb[i % 4][3][:, 4 + f:5 + f])
                    banks.free[pi] = [b]
                    tb.append(b)
                t_down[i] = h1r.free[hi] = [a]
                gs[i] = (g, gi, tb)

            def last(i):
                g, gi, tb = gs[i]
                w3, b3 = wb[i % 4][2], wb[i % 4][4]
                p, pf, pi = banks.next()
                for s in range(2):
                    for k in range(2):
                        a = mm(p[:, s * 128:(s + 1) * 128], g[:, k, s * 128:(s + 1) * 128], w3[:, k, :], tb[k], pf,
                               start=(k == 0), stop=(k == 1), inc=(k == 1))
                h2r.free[gi] = [a]
                y, yf, yi = yr.next()
                b = tt(y, p[:, 0:256].rearrange("p (h n) -> p h n", h=2), b3.unsqueeze(1).to_broadcast([128, 2, 128]),
                       ALU.add, a, yf)
                banks.free[pi] = [b]
                wfree[i % 4] = [a, b, tw1[i], tw2[i]]
                yr.free[yi] = [dma(Y2[i], y, b)]
                t_y.extend(yr.free[yi])
                if i + 4 < NTL:
                    t_we[i + 4] = load_w(i + 4)

            split_w(0)
            fetch(0)
            split_w(1)
            up(0)
            fetch(1)
            for i in range(NTL):
                down(i)
                if i + 1 < NTL:
                    up(i + 1)
                if i + 2 < NTL:
                    fetch(i + 2)
                    split_w(i + 2)
                last(i)
            yg = take(2048).rearrange("p (t n) -> p t n", t=NT)
            for c in range(CHUNKS):
                for t in range(4 * c, 4 * c + 4):
                    g_ = pool_dma(lambda e, t=t: e.indirect_dma_start(
                        yg[:, t, :], None, Yd, bass.IndirectOffsetOnAxis(ap=slot[:, t:t + 1], axis=0)), t_y, t_slot)
                    a = stt(x[:, t, :], yg[:, t, :], 0.5, x[:, t, :], ALU.mult, ALU.add, g_)
                finish(c, a, banks)

        def attention(kind):
            xn, xT, txn, tx = begin()
            scale = 128 ** -0.5 if kind == 0 else 8 ** -0.5
            nm = 3 if kind == 0 else 12
            K = 96 + nm
            wq, wk, wv, wo = (take(128) for _ in range(4))
            bcol = take(1)
            bub = take(128)
            if kind == 0:
                t_w = [dma(wq, ins["wqT0"]), dma(bcol, ins["L0_attn_bq"].rearrange("(p a) -> p a", a=1)),
                       dma(wo, ins["wuT0"]), dma(bub, ins["L0_attn_bu"].partition_broadcast(128))]
                ws = [wq]
            else:
                t_w = [dma(wq, ins["L3_attn_w_q"]), dma(wk, ins["L3_attn_w_k"]), dma(wv, ins["L3_attn_w_v"]), dma(wo, ins["L3_attn_w_o"])]
                ws = [wq, wk]
            pieces = [(take(8192, BF16), take(8192, BF16)) for _ in range(2)]
            pfree = [[], []]
            stage = take(8192, BF16) if kind == 0 else None
            rows = ins["key_rows0" if kind == 0 else "key_rows3"]
            t_init = [[dma(kk[72:K, :].bitcast(F32), rows), dma(qq[72:96, :].bitcast(F32), rows[0:24])] for qq, kk in pieces]
            if kind == 0:
                t_init[0].append(dma(stage[72:96, :].bitcast(F32), rows[0:24]))
            ebuf = take(8192)
            er = Ring([ebuf[:, i * 1024:(i + 1) * 1024] for i in range(8)])
            ve, t_ve = None, None
            if kind == 3:
                ve = take(16 * 16 * 32).rearrange("p (t h m) -> p t h m", t=16, h=16)
                b = mset(ve.rearrange("p t h m -> p (t h m)"), 0.0, eng=PO)
                t_vi = mset(ve[:, :, :, 8:9], 1.0, b, eng=PO)
            banks = Ring(bank[0:4])
            n_buf, size = (4, 1792) if kind == 0 else (6, 1280)
            pr = Ring([(ebuf[:, o:o + 512], [ebuf[:, o + 512 + 256 * i:o + 768 + 256 * i].bitcast(BF16) for i in range(3)],
                        ebuf[:, o + 1280:o + size])
                       for o in range(0, n_buf * size, size)])
            scr = ins["scratch"]
            t_scr = [[[] for _ in ws] for _ in range(CHUNKS)]

            items = [(c, side) for c in range(CHUNKS) for side in range(len(ws))]
            live = {}

            def step(i, k):
                c, side = items[i]
                s = slice(c * 512, (c + 1) * 512)
                if k == 0:
                    buf, rf, ri = pr.next()
                    p, pf, pi = banks.next()
                    a = mm(p[:, :], ws[side], xT[:, s], tx[c], t_w, pf, inc=True)
                    if kind == 0:
                        a = act(buf[2], p[:, :], ACT.Identity, a, rf, bias=bcol)
                        banks.free[pi] = [a]
                        b = vcopy(buf[1][0], buf[2], a)
                    else:
                        b = acopy(buf[1][0], p[:, :], a, rf)
                    live[i] = (buf, ri, pi, p, b, rf)
                    return
                (rem, parts, full), ri, pi, p, b, rf = live[i]
                if k == 1:
                    b = tt(rem, full if kind == 0 else p[:, :], parts[0], ALU.subtract, b, rf)
                    if kind == 3:
                        banks.free[pi] = [b]
                elif k == 2:
                    b = acopy(parts[1], rem, b)
                elif k == 3:
                    b = tt(rem, rem, parts[1], ALU.subtract, b)
                else:
                    b = acopy(parts[2], rem, b)
                    t_scr[c][side] = [dma(scr[side, :, 8 * j:8 * j + 8, s], parts[j], b) for j in range(3)]
                    pr.free[ri] = t_scr[c][side]
                    if (c, side) == ((0, 0) if kind == 0 else items[-1]):
                        for lo, hi in PARTS[0]:
                            load_queries(0, lo, hi)
                            load_keys(0, lo, hi)
                live[i] = ((rem, parts, full), ri, pi, p, b, rf)

            sfree, ksrc = [], {}
            t_q, t_k = {}, {}
            PARTS = {0: [(0, 2), (2, 4)] if kind == 0 else [(0, 1), (1, 4)]}

            def load(i, dst, side, part_of, lo, hi, *w):
                toks = []
                runs = [(0, 0, 3), (1, 0, 3), (2, 0, 3)] if part_of == 0 else [(0, 0, 3), (1, 1, 3), (1, 0, 1), (2, 2, 3), (2, 0, 2)]
                for j, p0, p1 in runs:
                    r = 24 * j + 8 * ((p0 - part_of * j) % 3)
                    o = dst[r:r + 8 * (p1 - p0), :].rearrange("r (c t) -> r c t", c=16 if kind == 0 else 4)
                    v = scr[side, :, 8 * p0:8 * p1, :].rearrange("c r t -> r c t")
                    if kind == 0:
                        o, v = o[:, :, lo * 128:hi * 128], v[:, :, i * 512 + lo * 128:i * 512 + hi * 128]
                        ready = t_scr[i]
                    else:
                        o, v = o[:, lo:hi, :], v[:, 4 * i + lo:4 * i + hi, :]
                        ready = [t_scr[c][side] for c in range(CHUNKS)]
                    toks.append(dma(o, v, ready, *w))
                return toks

            def load_queries(i, lo, hi):
                a = load(i, pieces[i % 2][0], 0, 0, lo, hi, pfree[i % 2])
                for q in range(4 * i + lo, 4 * i + hi):
                    t_q[q] = [a, t_init[i % 2], t_init[0]]

            def load_keys(i, lo, hi):
                if kind == 0:
                    ksrc[i, lo] = load(i, stage, 0, 1, lo, hi, sfree)
                    return
                a = load(i, pieces[i % 2][1], 1, 1, lo, hi, pfree[i % 2])
                for q in range(4 * i + lo, 4 * i + hi):
                    t_k[q] = [a, t_init[i % 2]]

            def order_keys(i):
                if kind == 0:
                    kk = pieces[i % 2][1]
                    for lo, hi in PARTS.get(i, [(0, 4)]):
                        b = vcopy(kk[0:96, :].rearrange("p (g c t) -> p g c t", g=16, c=16)[:, 4 * lo:4 * hi, :, :],
                                  stage[0:96, :].rearrange("p (c g t) -> p g c t", g=16, c=16)[:, 4 * lo:4 * hi, :, :],
                                  ksrc[i, lo], t_init, pfree[i % 2])
                        for q in range(4 * i + lo, 4 * i + hi):
                            t_k[q] = [b, t_init[i % 2]]
                    sfree[:] = [b]
                    if i + 1 < 4:
                        load_keys(i + 1, 0, 4)

            for n in range(len(items) + 4):
                for k in range(5):
                    if 0 <= n - k < len(items):
                        step(n - k, k)
            for f in er.free:
                f.extend([t for c in t_scr for side in c for t in side])
            if kind == 3:
                for t in range(NT):
                    p, pf, pi = banks.next()
                    a = mm(p[:, 0:128], xT[:, t * 128:(t + 1) * 128], wv, pf, inc=True)
                    a = acopy(ve[:, t, :, 0:8], p[:, 0:128].rearrange("p (h d) -> p h d", h=16), a, t_vi)
                    banks.free[pi] = [a]
                t_ve = [a, t_vi]
            order_keys(0)
            load_queries(1, 0, 4)
            if kind == 3:
                load_keys(1, 0, 4)

            def queries(z, q, b):
                if kind == 0:
                    o = (q % 4) * 128 + b * 32
                    return z.rearrange("p (c t) -> p c t", c=16)[:, :, o:o + 32]
                o = (q % 4) * 2048 + b * 512
                return z[:, o:o + 512]

            def keys(z, q, b):
                o = ((q % 4) * 4 + b) * 512
                return z[:, o:o + 512]

            ar, br = Ring(bank[0:3]), Ring(bank[3:6])
            av, misc = Ring([bank[6]]), Ring([bank[7]])
            for r in (ar, br, av, misc):
                for i in range(len(r.bufs)):
                    r.free[i] = [f for g in banks.free for f in g]
            nkb = 1 if kind == 0 else 4
            nmx = 16 * nkb
            mxa = [take(nmx) for _ in range(3)]
            mneg = take(nmx)
            mpt = [take(3 * nmx, BF16) for _ in range(3)]
            vq = [take(512) for _ in range(2)] if kind == 0 else None
            vqfree = [[], []]
            ot = [take(512) for _ in range(2)]
            rcs = [take(16) for _ in range(2)]
            osb = take(NT * 128).rearrange("p (t n) -> p t n", t=NT)
            otr = Ring([take(512) for _ in range(2)])
            T = {}

            def stage_a(q, u):
                qq, kk = pieces[(q // 4) % 2]
                b, half = u // 2, u % 2
                for n in range(2):
                    p, pf, pi = ar.next()
                    qt = 2 * half + n
                    l, r = (keys(kk[0:72], q, b), queries(qq[0:72], q, b)) if kind == 0 else (
                        queries(qq[0:72], q, b), keys(kk[0:72], q, b))
                    a = mm(p[:, :], l[:, qt * 128:(qt + 1) * 128], r, t_q[q], t_k[q], pf, inc=True)
                    m = mxa[q % 3][:, (b * 4 + qt) * nkb:(b * 4 + qt + 1) * nkb]
                    c = red(m, p.rearrange("p (k n) -> p k n", k=nkb), ALU.max, a, T.get(("split", q - 3)))
                    ar.free[pi] = [c]
                T["max", q, u] = c

            def split(q):
                mx_ = mxa[q % 3]
                pt = mpt[q % 3].rearrange("p (b z) -> p b z", b=16)
                p0, p1, p2 = (pt[:, :, i * nkb:(i + 1) * nkb] for i in range(3))
                v = lambda z: z.rearrange("p (b k) -> p b k", k=nkb)
                a = ts(p0, v(mx_), -1.0, None, ALU.mult, None, T["max", q, 7], T.get(("place", q - 3, 3)))
                a = stt(v(mneg), v(mx_), -1.0, p0, ALU.mult, ALU.subtract, a)
                a = vcopy(p1, v(mneg), a)
                T["split", q] = tt(p2, v(mneg), p1, ALU.subtract, a)

            def place(q, b):
                qq, kk = pieces[(q // 4) % 2]
                pt = mpt[q % 3].rearrange("p (b z) -> p b z", b=16)
                p, pf, pi = misc.next()
                for k in range(4):
                    c = mm(p[96:K, k * 128:(k + 1) * 128], pt[:, b * 4 + k, :], identb, T["split", q], pf, inc=(k == 3))
                i_ = p[96:K, :]
                if kind == 0:
                    i_ = i_.rearrange("p (c t) -> p c t", c=16)
                T["place", q, b] = c
                T["mrow", q, b] = acopy(queries(qq[96:K], q, b), i_, c)
                misc.free[pi] = [T["mrow", q, b]]

            def values(q):
                qq, kk = pieces[(q // 4) % 2]
                p, pf, pi = misc.next()
                for b in range(4):
                    for k in range(4):
                        c = mm(p[:, b * 128 + k * 32:b * 128 + (k + 1) * 32], keys(kk[0:99], q, b)[:, k * 128:(k + 1) * 128],
                               cB("sel")[0:99, :], pf, t_k[q], inc=(b == 3 and k == 3))
                T["v", q] = acopy(vq[q % 2], p[:, :], c, vqfree[q % 2])
                misc.free[pi] = [T["v", q]]

            def stage_b(q, u):
                qq, kk = pieces[(q // 4) % 2]
                half, b = u // 4, u % 4
                e, ef, ei = er.next()
                for n in range(2):
                    p, pf, pi = br.next()
                    k = 2 * half + n
                    a = mm(p[:, :], keys(kk[0:K], q, b)[:, k * 128:(k + 1) * 128],
                           queries(qq[0:K], q, b), T["mrow", q, b], pf, inc=True)
                    c = act(e[:, n * 512:(n + 1) * 512], p, ACT.Exp, a, ef, scale=scale)
                    br.free[pi] = [c]
                T["e", q, u] = (e, ei, c)
                if u == 7:
                    pfree[(q // 4) % 2] = [a]
                    if q % 4 == 3 and q // 4 + 2 < 4:
                        load_queries(q // 4 + 2, 0, 4)
                        if kind == 3:
                            load_keys(q // 4 + 2, 0, 4)

            def stage_o(q, k):
                if k == 0:
                    T["av"] = av.next()
                p, pf, pi = T["av"]
                half, n = k // 2, k % 2
                for b in range(4):
                    e, ei, te = T["e", q, half * 4 + b]
                    if kind == 0:
                        lv, tv = vq[q % 2][:, b * 128 + k * 32:b * 128 + (k + 1) * 32], T["v", q]
                    else:
                        lv, tv = ve[:, b * 4 + k, q, :], t_ve
                    a = mm(p[32 * b:32 * b + 32, :], lv, e[:, n * 512:(n + 1) * 512], te, tv, pf,
                           start=(k == 0), stop=(k == 3), inc=(n == 1 and b == 3), skip=True)
                if n == 1:
                    for b in range(4):
                        er.free[T["e", q, half * 4 + b][1]] = [a]
                if k == 3:
                    vqfree[q % 2] = [a]
                    o = ot[q % 2]
                    a = DV(lambda e_: e_.transpose(o, p[:, :]), a, T.get(("norm", q - 2)))
                    av.free[pi] = [a]
                    ov = o.rearrange("p (c m) -> p c m", m=32)
                    rc = rcs[q % 2]
                    a = DV(lambda e_: e_.reciprocal(rc, ov[:, :, 8]), a)
                    dst = osb[:, q, :].rearrange("p (c d) -> p c d", d=8) if kind == 0 else osb[:, :, q * 8:q * 8 + 8]
                    T["norm", q] = tt(dst, ov[:, :, 0:8], rc.unsqueeze(2).to_broadcast([128, 16, 8]), ALU.mult, a, eng=PO)

            def out_a(c, ring):
                oT, of, oi = otr.next()
                p, pf, pi = ring.next()
                for j in range(4):
                    a = tp(p[:, j * 128:(j + 1) * 128], osb[:, 4 * c + j, :], [T["norm", q] for q in range(16) if ("norm", q) in T],
                           pf, inc=(j == 3))
                return oT, of, oi, p, pi, a

            def project(oT, t_o, c, ring):
                p, pf, pi = ring.next()
                for j in range(4):
                    a = mm(p[:, j * 128:(j + 1) * 128], oT[:, j * 128:(j + 1) * 128], wo, t_o, pf, inc=(j == 3))
                t_p = a
                xc = x[:, 4 * c:4 * c + 4, :]
                a = tt(xc, xc, p[:, :].rearrange("p (t n) -> p t n", t=4), ALU.add, a)
                ring.free[pi] = [a]
                if kind == 0:
                    a = tt(xc, xc, bub.unsqueeze(1).to_broadcast([128, 4, 128]), ALU.add, a)
                finish(c, a, ring)
                return t_p

            def chunk_out(c):
                oT, of, oi, p, pi, a = out_a(c, misc)
                a = acopy(oT, p[:, :], a, of)
                misc.free[pi] = [a]
                otr.free[oi] = [project(oT, a, c, misc)]

            AHEAD = 15

            def ahead(n):
                if n < 128:
                    stage_a(n // 8, n % 8)
                    if n % 8 == 7:
                        split(n // 8)

            for n in range(AHEAD):
                ahead(n)
                if 8 <= n < 12:
                    place(0, n - 8)
            if kind == 0:
                values(0)
            for n in range(128):
                q, u = n // 8, n % 8
                if n % 32 == 16 and n // 32 + 1 < 4:
                    order_keys(n // 32 + 1)
                stage_b(q, u)
                ahead(n + AHEAD)
                if u in (0, 2) and q > 0:
                    stage_o(q - 1, 2 + (0, 2).index(u))
                if u in (1, 3, 5, 7) and q + 1 < 16:
                    place(q + 1, (1, 3, 5, 7).index(u))
                if u == 3 and kind == 0 and q >= 4 and q % 4 == 0:
                    chunk_out(q // 4 - 1)
                if u in (4, 6):
                    stage_o(q, (4, 6).index(u))
                if u == 6 and q + 1 < 16 and kind == 0:
                    values(q + 1)
            stage_o(15, 2)
            stage_o(15, 3)
            if kind == 0:
                chunk_out(3)
            else:
                rb = Ring(bank[0:4])
                for i in range(4):
                    rb.free[i] = [T["norm", 15], T["e", 15, 7][2]]
                oT = ebuf[:, 0:2048]
                tt_ = []
                for c in range(CHUNKS):
                    _, _, _, p, pi, a = out_a(c, rb)
                    dst = oT.rearrange("p (b u t) -> p u b t", b=4, u=16)[:, 4 * c:4 * c + 4, :, :]
                    src = p[:, :].rearrange("p (u b t) -> p u b t", u=4, b=4)
                    a = acopy(dst, src, a)
                    rb.free[pi] = [a]
                    tt_.append(a)
                for c in range(CHUNKS):
                    project(oT[:, c * 512:(c + 1) * 512], tt_, c, rb)

        stages = [l0_ffn, lambda: attention(0), l0_ffn, l1_ffn, l1_attn, l1_ffn, l2_ffn, l2_attn, l2_ffn,
                  l3_ffn, lambda: attention(3), l3_ffn]
        if 9 in LAYERS or 11 in LAYERS:
            zz = take(3840)
            z = mset(zz, 0.0, eng=PO)
            dma(ins["sorted_x"].rearrange("(i p) n -> p i n", p=128), zz.rearrange("p (i n) -> p i n", n=128), z)
        first = Ring([bank[7], bank[6]])
        S["feat"] = LAYERS[0] != 4
        for c in range(CHUNKS):
            finish(c, t_x[c], first)
        for n in LAYERS:
            S["last"] = n == LAYERS[-1]
            S["feat"] = n != 3
            stages[n]()
        SP.stop_until(S["out"])
        reset()

        block = ctx.enter_context(nc.Block())

        @block.sync
        def _(e):
            SP.flush(e)

        @block.gpsimd
        def _(e):
            PO.flush(e)

        @block.scalar
        def _(e):
            AC.flush(e)

        @block.vector
        def _(e):
            DV.flush(e)

        @block.tensor
        def _(e):
            PE.flush(e)


def constants():
    f, b = {}, {}
    r = np.arange(128)
    f["ident"] = np.eye(128)
    f["iota"] = np.tile(np.arange(512), (128, 1))
    f["mhalf"] = np.full((128, 16), -0.5)
    f["ridx"] = np.tile(8 - np.arange(8), (128, 16))
    g, e = np.arange(16)[:, None] // 2, np.arange(8)[None, :]
    f["coff"] = np.tile(((e // 2) * 128 + ((e % 2) ^ (g % 2)) * 64 + 1).reshape(1, 128), (128, 1))
    f["onesrow"] = np.ones((128, 512))
    f["scanreset"] = np.tile((np.arange(128) % 16 != 0), (128, 1))
    f["k256"] = np.tile(256 * np.arange(8), (128, 8))
    f["i16"] = np.tile(np.repeat(np.arange(16), 8), (128, 1))
    f["blockdiag"] = (r[:, None] // 8 == r[None, :] // 8)
    b["ident"] = np.eye(128)
    b["tri"] = r[:, None] < r[None, :]
    b["ones"] = np.ones((128, 128))
    s = np.zeros((128, 32))
    for part in range(3):
        for d in range(8):
            s[part * 8 + d, d] = 1
    s[96, 8] = 1
    b["sel"] = s

    def pack(d):
        at, o = {}, 0
        for k, v in d.items():
            at[k] = (o, o + v.shape[1])
            o += v.shape[1]
        return np.concatenate([np.asarray(v, np.float32) for v in d.values()], 1).astype(np.float32), at

    return pack(f), pack(b)


def key_rows(blocks):
    z = np.zeros((24 + 3 * blocks, 8192), np.uint16)
    for part in range(3):
        for kb in range(blocks):
            z[24 + part * blocks + kb, (np.arange(8192) % 512) // (512 // blocks) == kb] = 0x3F80
    return z.view(np.float32)


(CONST_F, CF_AT), (CONST_B, CB_AT) = constants()

_INS = ["L0_attn_x", "L0_attn_bq", "L0_attn_bu", "L0_ffn_router_w", "L0_ffn_w0_kernel", "L0_ffn_w1_kernel",
        "L0_ffn_wo_kernel", "L1_attn_bk", "L1_attn_bka", "L1_attn_bv", "L1_attn_gamma", "L1_attn_beta",
        "L1_ffn_w3_s",
        "L2_attn_bq", "L2_attn_bk", "L2_attn_bv", "L2_attn_bo",
        "L2_ffn_Wr", "L2_ffn_br", "L2_ffn_W_up", "L2_ffn_W_down", "L2_ffn_b_down",
        "L3_attn_w_q", "L3_attn_w_k", "L3_attn_w_v", "L3_attn_w_o",
        "L3_ffn_Wr", "L3_ffn_br", "L3_ffn_W1", "L3_ffn_W2", "L3_ffn_W3", "L3_ffn_b3"]
_TRANSPOSED = {"wqT0": "L0_attn_wq", "wuT0": "L0_attn_wu", "WkT1": "L1_attn_Wk", "WkaT1": "L1_attn_Wka",
               "WvT1": "L1_attn_Wv", "w1T": "L1_ffn_w1_w", "w2T": "L1_ffn_w2_w", "h1T": "L1_ffn_h1_w",
               "h2T": "L1_ffn_h2_w", "w3T": "L1_ffn_w3_w", "WqT2": "L2_attn_Wq", "WkT2": "L2_attn_Wk",
               "WvT2": "L2_attn_Wv", "WoT2": "L2_attn_Wo"}


def kernel(**inputs):
    import concourse.bacc as _bacc
    from concourse.bass_utils import run_bass_kernel_spmd as _run

    nc = _bacc.Bacc("TRN2", target_bir_lowering=False, num_devices=1)
    arrays = {n: np.ascontiguousarray(inputs[n]) for n in _INS}
    for n, src in _TRANSPOSED.items():
        arrays[n] = np.ascontiguousarray(np.transpose(inputs[src]))
    for n in ("w1_s", "w2_s", "h1_s", "h2_s"):
        arrays[n] = np.ascontiguousarray(np.reshape(inputs["L1_ffn_" + n], (4, 128)).T)
    bup = np.zeros((128, 4, 3), np.float32)
    for f, (f0, fn) in enumerate(L2T):
        bup[0:fn, :, f] = np.transpose(inputs["L2_ffn_b_up"][:, f0:f0 + fn])
    arrays["bup"] = bup
    arrays["b12c"] = np.ascontiguousarray(np.concatenate(
        [np.transpose(np.reshape(inputs["L3_ffn_" + n], (8, -1, 128)), (0, 2, 1)) for n in ("b1", "b2")], 2))
    arrays["key_rows0"], arrays["key_rows3"] = key_rows(1), key_rows(4)
    arrays["const_f"], arrays["const_b"] = CONST_F, CONST_B
    ins = {n: nc.dram_tensor(f"in_{n}", a.shape, mybir.dt.from_np(a.dtype), kind="ExternalInput").ap()
           for n, a in arrays.items()}
    ins["scratch"] = nc.dram_tensor("scratch", (2, 16, 24, 2048), BF16, kind="Internal").ap()
    ins["sorted_x"] = nc.dram_tensor("sorted_x", (3840, 128), F32, kind="Internal").ap()
    ins["sorted_y"] = nc.dram_tensor("sorted_y", (3840, 128), F32, kind="Internal").ap()
    out = nc.dram_tensor("out_0", (4, 512, 128), F32, kind="ExternalOutput").ap()
    build(nc, ins, out)
    r = _run(nc, [{f"in_{n}": a for n, a in arrays.items()}], core_ids=[0])
    return r.results[0]["out_0"]
```

```python
from contextlib import ExitStack

import numpy as np

import concourse.bass as bass
from concourse import mybir

LAYERS = tuple(range(12))

ALU = mybir.AluOpType
ACT = mybir.ActivationFunctionType
F32 = mybir.dt.float32
BF16 = mybir.dt.bfloat16
F32R = mybir.dt.float32r
I32 = mybir.dt.int32
AX = mybir.AxisListType
EPS = 1e-5
NT = 16
CHUNKS = 4
FH = 688
L0T = [(i * 128, min(128, FH - i * 128)) for i in range(6)]
FM = 341
L2T = [(0, 128), (128, 128), (256, 85)]


class Eng:

    def __init__(self, name, sem):
        self.name, self.sem, self.q, self.n, self.seen = name, sem, [], 0, {}

    def wait(self, *toks):
        ws = []
        for t in flat(toks):
            key, v = t
            if self.seen.get(key.name, 0) < v:
                self.seen[key.name] = v
                ws.append(t)
        return ws

    def __call__(self, fn, *toks, inc=True):
        self.q.append((self.wait(*toks), fn, (self.sem, 1) if inc else None))
        if inc:
            self.n += 1
        return (self.sem, self.n) if inc else None

    def stop_until(self, *toks):
        self.q.append((self.wait(*toks), None, None))

    def flush(self, eng):
        for ws, fn, inc in self.q:
            for s, v in ws:
                eng.wait_ge(s, v)
            if fn is not None:
                ins = fn(eng)
                if inc is not None:
                    ins.then_inc(*inc)


def flat(toks):
    for t in toks:
        if t is None:
            continue
        if isinstance(t, list):
            yield from flat(t)
        else:
            yield t


class Ring:

    def __init__(self, bufs):
        self.bufs, self.free, self.i = bufs, [[] for _ in bufs], -1

    def next(self):
        self.i = (self.i + 1) % len(self.bufs)
        return self.bufs[self.i], self.free[self.i], self.i


def build(nc, ins, out):
    ctx = ExitStack()
    with ctx:
        sem = lambda n: ctx.enter_context(nc.semaphore(n))
        sb = lambda n, s, d=F32: ctx.enter_context(nc.sbuf_tensor(n, s, d))
        psum = ctx.enter_context(nc.psum_tensor("psum", [128, 4096], F32))
        bank = [psum[:, i * 512:(i + 1) * 512] for i in range(8)]
        PE, AC, DV, PO, SP = (Eng(n, sem("s_" + n)) for n in ("pe", "act", "dve", "pool", "sp"))
        dsems = [sem(f"s_dma{i}") for i in range(96)]
        dcount = [0] * 96
        dma_last = {}
        psems = [sem(f"s_pdma{i}") for i in range(16)]
        pcount = [0] * 16
        state = {"d": 0, "p": 0}

        def dma(o, i, *w, eng=SP):
            k = state["d"] % 96
            state["d"] += 1
            dcount[k] += 16
            dma_last[k] = (dsems[k], dcount[k])
            eng.q.append((eng.wait(*w), lambda e, o=o, i=i: e.dma_start(o, i), (dsems[k], 16)))
            return dma_last[k]

        def barrier():
            toks = [(e.sem, e.n) for e in (PE, AC, DV, PO) if e.n] + list(dma_last.values())
            for e in (PE, AC, DV, PO, SP):
                e.stop_until(toks)

        def mm(o, l, r, *w, start=True, stop=True, inc=False, skip=False):
            return PE(lambda e: e.matmul(o, l, r, start=start, stop=stop, skip_group_check=skip), *w, inc=inc)

        def fine(n, f=1):
            return take(n, F32R), take(n, F32R)

        def mm3(o, l, r, *w, start=True, stop=True, inc=False):
            mm(o, l[0], r[0], *w, start=start, stop=False)
            mm(o, l[0], r[1], start=False, stop=False)
            return mm(o, l[1], r[0], start=False, stop=stop, inc=inc)

        def halve(src, pair, *w, hi=None, lo=None):
            h, l = pair
            if hi is None:
                a = acopy(h, src, *w)
            else:
                a = vcopy(h, src, *w, eng=hi)
            return [a, tt(l, src, h.bitcast(F32), ALU.subtract, a, *w, eng=lo)]

        def tp(o, i, *w, inc=False):
            p = i.shape[0]
            idn = ident[0:p, 0:p] if i.dtype == F32 else identb[0:p, 0:p]
            return PE(lambda e: e.transpose(o, i, idn), *w, inc=inc)

        def act(o, i, f, *w, bias=0.0, scale=1.0, accum=None):
            return AC(lambda e: e.activation(o, i, f, bias=bias, scale=scale, accum_out=accum), *w)

        def acopy(o, i, *w):
            return AC(lambda e: e.copy(o, i), *w)

        def tt(o, a, b, op, *w, eng=None):
            return (eng or DV)(lambda e: e.tensor_tensor(o, a, b, op), *w)

        def ts(o, a, s1, s2, op0, op1, *w, eng=None):
            return (eng or DV)(lambda e: e.tensor_scalar(o, a, s1, s2, op0, op1) if op1 is not None
                               else e.tensor_scalar(o, a, s1, None, op0), *w)

        def stt(o, a, s, b, op0, op1, *w):
            return DV(lambda e: e.scalar_tensor_tensor(o, a, s, b, op0, op1), *w)

        def red(o, a, op, *w, axis=None):
            return DV(lambda e: e.tensor_reduce(o, a, axis or AX.X, op), *w)

        def vcopy(o, i, *w, eng=None):
            return (eng or DV)(lambda e: e.tensor_copy(o, i), *w)

        def mset(o, v, *w, eng=None):
            return (eng or DV)(lambda e: e.memset(o, v), *w)

        x = sb("x", [128, NT, 128])
        XN = [sb(f"xn{i}", [128, NT, 128]) for i in range(2)]
        XT = [sb(f"xT{i}", [128, 2048]) for i in range(2)]
        NCF = CONST_F.shape[1]
        cf = sb("cf", [128, NCF])
        NCB = CONST_B.shape[1]
        cb = sb("cb", [128, NCB], BF16)
        st = sb("st", [128, NT, 6])
        mv = sb("mv", [128, NT, 2])
        rs = sb("rs", [128, NT])
        lg_sb = sb("lg", [128, 128])
        mem = {"n": 0, "used": []}

        def take(n, dt=F32):
            size = -(-n * (2 if dt == BF16 else 4) // 64) * 64
            a = nc.sbuf_base
            for lo, hi in sorted(mem["used"]):
                if a < hi and a + size > lo:
                    a = hi
            assert a + size <= nc.sbuf_top, (n, a + size, nc.sbuf_top)
            mem["n"] += 1
            mem["used"].append((a, a + size))
            return nc.alloc_sbuf_tensor_at(f"t{mem['n']}", [128, n], dt, offset=a)[:, :]

        def prefetch(*w, over=()):
            nxt = S["next"]
            if nxt is None:
                return
            kept = mem["used"]
            mem["used"] = [u for u in kept if u not in over]
            n = len(mem["used"])
            S["pre"], S["work"] = PRE[nxt](list(w))
            S["held"] = mem["used"][n:]
            mem["used"] = kept

        def work():
            if S["work"] is not None:
                f, S["work"] = S["work"], None
                f()


        def cF(name):
            a, b = CF_AT[name]
            return cf[:, a:b]

        def cB(name):
            a, b = CB_AT[name]
            return cb[:, a:b]

        ident, iota = cF("ident"), cF("iota")
        identb, tri, onesb = cB("ident"), cB("tri"), cB("ones")

        t_c = dma(cf[:, :], ins["const_f"])
        cb0 = take(NCB)
        t_cb0 = dma(cb0, ins["const_b"])
        x_dram = ins["L0_attn_x"].rearrange("b (n p) d -> p (b n) d", p=128)
        o_dram = out.rearrange("b (n p) d -> p (b n) d", p=128)
        t_x = [dma(x[:, 4 * c:4 * c + 4, :], x_dram[:, 4 * c:4 * c + 4, :]) for c in range(CHUNKS)]
        t_cb = vcopy(cb[:, :], cb0, t_cb0)
        S = {"par": 1, "last": False, "feat": True, "wait": [], "stats": None, "work": None, "route": None, "held": [], "pre": None, "txn": [], "tx": []}

        def ln_stats(c, src, *w):
            s0, s1 = 4 * c, 4 * c + 4
            for t in range(s0, s1):
                a = DV(lambda e, t=t: e.bn_stats(st[:, t, :], src[:, t, :]), *w)
            for t in range(s0, s1):
                a = DV(lambda e, t=t: e.bn_aggr(mv[:, t, :], st[:, t, :]), a)
            b = ts(rs[:, s0:s1], mv[:, s0:s1, 1], EPS, None, ALU.add, None, a, eng=PO)
            return tt(rs[:, s0:s1], rs[:, s0:s1], cF("mhalf")[:, s0:s1], ALU.pow, b, t_c, eng=PO)

        def ln_apply(c, src, dst, b):
            for t in range(4 * c, 4 * c + 4):
                a = ts(dst[:, t, :], src[:, t, :], mv[:, t, 0:1], rs[:, t:t + 1], ALU.subtract, ALU.mult, b)
            return a

        def features_chunk(c, src, dst, w, banks, post=None):
            p, free, i = banks.next()
            for j in range(4):
                a = tp(p[:, j * 128:(j + 1) * 128], src[:, 4 * c + j, :], w, free, t_c, inc=(j == 3))
            o = dst[:, c * 512:(c + 1) * 512]
            a = acopy(o, p[:, :], a) if post is None else post(o, p[:, :], a)
            banks.free[i] = [a]
            return a

        def finish(c, tok, banks):
            if S["last"]:
                S.setdefault("out", []).append(dma(o_dram[:, 4 * c:4 * c + 4, :], x[:, 4 * c:4 * c + 4, :], tok))
                return
            if c == CHUNKS - 1:
                work()
            flush_ln()
            S["stats"] = (c, ln_stats(c, x, tok))
            if S["feat"]:
                if len(S["wait"]) > 1:
                    flush_features()
                S["wait"].append((c, banks))

        def flush_ln():
            if S["stats"] is not None:
                c, b = S["stats"]
                S["txn"].append(ln_apply(c, x, XN[1 - S["par"]], b))
                S["stats"] = None

        def flush_features():
            c, banks = S["wait"].pop(0)
            n = 1 - S["par"]
            S["tx"].append(features_chunk(c, XN[n], XT[n], S["txn"][c], banks))

        def begin():
            flush_ln()
            if S["route"] is None:
                while S["wait"]:
                    flush_features()
            else:
                w, t_w = S["route"]
                assert len(S["wait"][-1][1].bufs) > 2
                lgp, free, _ = S["wait"][-1][1].next()
                for c in range(CHUNKS):
                    if len(S["tx"]) <= c:
                        flush_features()
                    for t in range(4 * c, 4 * c + 4):
                        a = mm(lgp[:, t * 8:t * 8 + 8], XT[1 - S["par"]][:, t * 128:(t + 1) * 128], w, S["tx"][c], t_w, free,
                               inc=(t == NT - 1))
                acopy(lg_sb[:, :], lgp[:, 0:128], a)
                S["route"] = None
            work()
            barrier()
            mem["used"] = list(S["held"])
            S["par"] = 1 - S["par"]
            r = XN[S["par"]], XT[S["par"]], S["txn"], S["tx"]
            S["txn"], S["tx"] = [], []
            return r + (S["pre"],)

        def router(raw, tmp, mx, bias=None):
            lg, a = lg_sb[:, :].rearrange("p (t e) -> p t e", e=8), []
            if bias is not None:
                a = tt(tmp, lg, bias.unsqueeze(1).to_broadcast([128, NT, 8]), ALU.add, a)
                lg = tmp
            if raw is None:
                return lg, a
            a = red(mx, lg, ALU.max, a)
            a = tt(tmp, lg, mx.unsqueeze(2).to_broadcast([128, NT, 8]), ALU.subtract, a)
            a = act(tmp, tmp, ACT.Exp, a)
            b = red(mx, tmp, ALU.add, a)
            b = DV(lambda e: e.reciprocal(mx, mx), b)
            b = tt(raw, tmp, mx.unsqueeze(2).to_broadcast([128, NT, 8]), ALU.mult, b)
            return raw, b

        def argmax_mask(v, m, mx, tmp, vm, a):
            bc = lambda q: q.unsqueeze(2).to_broadcast([128, NT, 8])
            a = red(mx, v, ALU.max, a)
            a = tt(tmp, v, bc(mx), ALU.is_equal, a)
            a = tt(tmp, tmp, cF("ridx").rearrange("p (t e) -> p t e", e=8), ALU.mult, a)
            a = red(vm, tmp, ALU.max, a)
            return tt(m, tmp, bc(vm), ALU.is_equal, a)

        def pre_l0(w):
            rw = take(8)
            S["route"] = (rw, dma(rw, ins["L0_ffn_router_w"], w))
            return None, None

        def l0_ffn():
            xn, xT, txn, tx, _ = begin()
            banks = Ring(bank[0:2])
            wbuf = [[None, None, take(6 * 128).rearrange("p (f n) -> p f n", n=128)] for _ in range(2)]
            first = len(mem["used"])
            for b in wbuf:
                b[0], b[1] = take(FH), take(FH)
            whl = [(fine(FH), fine(FH)) for _ in range(2)]
            xsr = Ring([fine(256)])
            xd = fine(8 * 512)
            d_r = Ring([take(512, F32R) for _ in range(3)])
            passing = mem["used"][first:]
            t_in, t_wo, t_up, t_out, twh = {}, {}, {}, {}, {}

            def load_in(e):
                t_in[e] = [dma(wbuf[e % 2][i], ins[f"L0_ffn_w{i}_kernel"][e], twh.get(e - 2)) for i in range(2)]

            def load_out(e):
                bo = wbuf[e % 2][2]
                t_wo[e] = [dma(bo[:, 0:5, :], ins["L0_ffn_wo_kernel"][e, 0:640].rearrange("(f p) n -> p f n", p=128), t_out.get(e - 2)),
                           dma(bo[0:48, 5, :], ins["L0_ffn_wo_kernel"][e, 640:FH], t_out.get(e - 2))]

            def split_w(e):
                h = [halve(wbuf[e % 2][i], whl[e % 2][i], t_in[e][i], t_up.get(e - 2), hi=DV) for i in range(2)]
                twh[e] = [t for q in h for t in q]
                if e + 2 < 8:
                    load_in(e + 2)

            for e in range(2):
                load_in(e)
                load_out(e)
            v3 = lambda: take(128).rearrange("p (t e) -> p t e", e=8)
            raw, tmp, m1, m2, rest, q1 = v3(), v3(), v3(), v3(), v3(), v3()
            mx, mx1, mx2, vm, sl1, sl2 = (take(16) for _ in range(6))
            cnt = take(64).rearrange("p (g e) -> p g e", e=8)
            m1b, m2b = take(128, BF16), take(128, BF16)
            raw, a = router(raw, tmp, mx)
            split_w(0)
            a = argmax_mask(raw, m1, mx1, tmp, vm, a)
            b1 = vcopy(m1b, m1.rearrange("p t e -> p (t e)"), a)
            a = tt(rest, raw, m1, ALU.mult, a)
            a = tt(rest, raw, rest, ALU.subtract, a)
            a = argmax_mask(rest, m2, mx2, tmp, vm, a)
            b2 = vcopy(m2b, m2.rearrange("p t e -> p (t e)"), a)
            m4 = lambda m: m.rearrange("p (g j e) -> p g j e", j=2, e=8)

            def prefix(p, mb, w):
                mm(p[:, 0:128], tri, mb, w, start=True, stop=False, skip=True)
                return mm(m4(p[:, 0:128])[:, :, 1, :], onesb, m4(mb)[:, :, 0, :], start=False, stop=True, inc=True, skip=True)

            c1 = prefix(bank[3], m1b, [b1, t_cb])
            mm(bank[4][:, 0:64], onesb, m4(m1b)[:, :, 0, :], start=True, stop=False)
            c2 = mm(bank[4][:, 0:64], onesb, m4(m1b)[:, :, 1, :], start=False, stop=True, inc=True)
            c3 = prefix(bank[5], m2b, b2)
            t3 = lambda p: p[:, 0:128].rearrange("p (t e) -> p t e", e=8)
            coff = cF("coff").rearrange("p (t e) -> p t e", e=8)

            def slots(p, m, sl, w):
                a = stt(tmp, p, 64.0, m, ALU.is_lt, ALU.mult, w)
                b = tt(q1, p, coff, ALU.add, w, a)
                a = tt(q1, q1, tmp, ALU.mult, a, b)
                a = red(sl, q1, ALU.add, a)
                return ts(sl, sl, 1.0, None, ALU.subtract, None, a)

            s1 = slots(t3(bank[3]), m1, sl1, c1)
            a = ts(cnt, bank[4][:, 0:64].rearrange("p (g e) -> p g e", e=8), 64.0, None, ALU.min, None, c2)
            a = tt(rest.rearrange("p (g j) e -> p g j e", j=2), m4(bank[5][:, 0:128]),
                   cnt.unsqueeze(2).to_broadcast([128, 8, 2, 8]), ALU.add, a, c3, s1)
            s2 = slots(rest, m2, sl2, a)

            xdv = [z.rearrange("p (k h g s c) -> p k h g s c", k=4, h=2, g=4, s=2) for z in xd]
            td = []

            def arrange(g):
                p, pf, pi = banks.next()
                xs, xsf, xsi = xsr.next()
                t_xs = halve(xn[:, 2 * g:2 * g + 2, :].rearrange("p t n -> p (t n)"), xs, txn[g // 2], xsf)
                for j in range(2):
                    t = 2 * g + j
                    d, df, di = d_r.next()
                    a = ts(d, iota, sl1[:, t:t + 1], None, ALU.is_equal, None, s1, df, t_c, eng=PO)
                    a = stt(d, iota, sl2[:, t:t + 1], d.bitcast(F32), ALU.is_equal, ALU.add, a, s2)
                    u = slice(j * 128, (j + 1) * 128)
                    mm(p[:, :], xs[0][:, u], d, a, pf, t_xs, start=(j == 0), stop=False)
                    b = mm(p[:, :], xs[1][:, u], d, start=False, stop=(j == 1), inc=True)
                    d_r.free[di] = [b]
                xsr.free[xsi] = [b]
                return p, pi, b

            def place(g, p, pi, b):
                pv = p[:, :].rearrange("p (k s c) -> p k s c", k=4, s=2)
                to = [[z[:, :, s ^ (g % 2), g // 2, s, :] for z in xdv] for s in range(2)]
                b = [acopy(to[s][0], pv[:, :, s, :], b) for s in range(2)]
                b = [tt(to[s][1], pv[:, :, s, :], to[s][0].bitcast(F32), ALU.subtract, b) for s in range(2)]
                banks.free[pi] = [b[1]]
                td.append(b[1])

            ready = arrange(0)
            for g in range(8):
                after = arrange(g + 1) if g + 1 < 8 else None
                place(g, *ready)
                ready = after
            ct = take(NT * 512).rearrange("p (t n) -> p t n", t=NT)
            cring = Ring([xT[:, 0:512], xT[:, 512:1024]])
            cc = ct[:, NT - 1, :]
            T = {}
            cbank = Ring([bank[7]])
            tct = []

            def weigh(t):
                ca, cfree, ci = cring.next()
                a1 = ts(ca, iota, sl1[:, t:t + 1], mx1[:, t:t + 1], ALU.is_equal, ALU.mult, s1, cfree)
                a2 = ts(cc, iota, sl2[:, t:t + 1], mx2[:, t:t + 1], ALU.is_equal, ALU.mult, s2, T.get("cc"))
                T["cc"] = tt(ca, ca, cc, ALU.add, a1, a2)
                T[t] = (ca, ci, T["cc"])

            def turn(t):
                ca, ci, a = T[t]
                p, pf, pi = cbank.next()
                for k in range(4):
                    b = tp(p[:, k * 128:(k + 1) * 128], ca[:, k * 128:(k + 1) * 128], a, pf, inc=(k == 3))
                cring.free[ci] = [b]
                b = acopy(ct[:, t, :], p[:, :], b)
                cbank.free[pi] = [b]
                tct.append(b)

            eo = take(8 * 4 * 128).rearrange("p (g k n) -> p g k n", g=8, k=4)
            hid = [take(6 * 512).rearrange("p (f n) -> p f n", n=512) for _ in range(2)]
            hb = Ring([(bank[0], bank[1]), (bank[2], bank[3]), (bank[4], bank[5])])
            hb.free[0] = [banks.free[0], banks.free[1]]
            hb.free[1] = [s2]
            hb.free[2] = [s2]
            ob = Ring([bank[6]])
            teo, t_hid = [], {}

            def up(e):
                h = hid[e % 2]
                xe = [z[:, e * 512:(e + 1) * 512] for z in xd]
                for f, (f0, fn) in enumerate(L0T):
                    (p0, p1), pf, pi = hb.next()
                    mm3(p0[0:fn, :], [z[:, f0:f0 + fn] for z in whl[e % 2][0]], xe, pf, td, twh[e])
                    a = mm3(p1[0:fn, :], [z[:, f0:f0 + fn] for z in whl[e % 2][1]], xe, inc=True)
                    b = act(h[0:fn, f, :], p0[0:fn, :], ACT.Gelu_apprx_tanh, a, t_out.get(e - 2))
                    b = tt(h[0:fn, f, :], h[0:fn, f, :], p1[0:fn, :], ALU.mult, b)
                    hb.free[pi] = [b]
                t_up[e], t_hid[e] = a, b

            def down(e):
                h, wo = hid[e % 2], wbuf[e % 2][2]
                p, pf, pi = ob.next()
                for s in range(4):
                    for f, (f0, fn) in enumerate(L0T):
                        b = mm(p[:, s * 128:(s + 1) * 128], h[0:fn, f, s * 128:(s + 1) * 128], wo[0:fn, f, :],
                               t_hid[e], pf, t_wo[e], start=(f == 0), stop=(f == 5), inc=(f == 5 and s == 3))
                t_out[e] = b
                if e + 2 < 8:
                    load_out(e + 2)
                eog = eo.rearrange("p (g h) k n -> p g h k n", h=2)
                pg = p[:, :].rearrange("p (g n) -> p g n", g=4)
                c_ = [acopy(eog[64 * s:64 * s + 64, :, s ^ (e % 2), e // 2, :], pg[64 * s:64 * s + 64, :, :], b)
                      for s in range(2)]
                ob.free[pi] = [c_[-1]]
                teo.append(c_[-1])

            for e in range(9):
                if e < 8:
                    up(e)
                if e > 0:
                    turn(2 * e - 1)
                if e + 1 < 8:
                    split_w(e + 1)
                if e < 8:
                    weigh(2 * e)
                if e > 0:
                    down(e - 1)
                if e < 8:
                    weigh(2 * e + 1)
                    turn(2 * e)
                if e == 7:
                    prefetch(t_up[7], t_hid[7], over=passing)
            yb = Ring([bank[0], bank[1], bank[2], bank[3]])
            for i in range(4):
                yb.free[i] = [t_hid[7]]
            for t in range(NT):
                p, pf, pi = yb.next()
                for k in range(4):
                    b = mm(p[:, 0:128], ct[:, t, k * 128:(k + 1) * 128], eo[:, t // 2, k, :], tct[t], teo, pf,
                           start=(k == 0), stop=(k == 3), inc=(k == 3))
                b = stt(x[:, t, :], p[:, 0:128], 0.5, x[:, t, :], ALU.mult, ALU.add, b)
                yb.free[pi] = [b]
                if t % 4 == 3:
                    finish(t // 4, b, yb)

        def pre_l1(w):
            n = len(mem["used"])
            w1, w2, h1, h2 = take(512), take(512), take(2048), take(2048)
            passing = mem["used"][n:]
            w3 = take(512)
            sc = take(16).rearrange("p (a f) -> p a f", a=4)
            s3 = take(128)
            v4 = lambda z: z.rearrange("p (k n) -> p k n", k=4)
            rows = lambda n: ins[n].rearrange("(k p) n -> p k n", p=128)
            t = {"w1": dma(w1, ins["w1T"], w), "w2": dma(w2, ins["w2T"], w),
                 "h1": dma(v4(h1), rows("h1T"), w), "h2": dma(v4(h2), rows("h2T"), w)}
            t_s = [dma(sc[:, i, :], ins[n], w) for i, n in enumerate(("w1_s", "w2_s", "h1_s", "h2_s"))]
            t_w3 = dma(v4(w3), rows("w3T"), w)
            t_s3 = dma(s3, ins["L1_ffn_w3_s"].partition_broadcast(128), w)
            W = {n: fine(z) for n, z in (("w1", 512), ("w2", 512), ("h1", 2048), ("h2", 2048))}
            tw = {}

            def split():
                for n, src in (("w1", w1), ("w2", w2), ("h1", h1), ("h2", h2)):
                    tw[n] = halve(src, W[n], t[n])

            return (v4(w3), sc, s3, t_s, t_w3, t_s3, W, tw, passing), split

        def l1_ffn():
            xn, xT, txn, tx, (w3, sc, s3, t_s, t_w3, t_s3, W, tw, passing) = begin()
            banks = Ring(bank)
            xr = Ring([fine(512) for _ in range(2)])

            def x_halves(c):
                xx, xf, xi = xr.next()
                return xx, xi, halve(xT[:, c * 512:(c + 1) * 512], xx, tx[c], xf)

            xx, xi, txx = x_halves(0)
            hr = Ring([fine(2048) for _ in range(3)])
            tr = Ring([take(512) for _ in range(3)])
            last = Ring([take(2048).rearrange("p (k n) -> p k n", k=4) for _ in range(2)])
            tmp = take(512)
            prefetch(*[t for q in tw.values() for t in q], over=passing)
            T = {0: (xx, xi, txx)}

            def up(c):
                xx, xi, txx = T[c]
                h, hf, hi = hr.next()
                ta = []
                for f in range(4):
                    fs = slice(f * 128, (f + 1) * 128)
                    p0, pf0, i0 = banks.next()
                    a = mm3(p0, [z[:, fs] for z in W["w1"]], xx, txx, tw["w1"], pf0, inc=True)
                    p1, pf1, i1 = banks.next()
                    b = mm3(p1, [z[:, fs] for z in W["w2"]], xx, tw["w2"], pf1, inc=True)
                    q, qf, qi = tr.next()
                    a = act(q, p0, ACT.Silu, a, qf, t_s, scale=sc[:, 0, f:f + 1])
                    banks.free[i0] = [a]
                    a = stt(q, p1, sc[:, 1, f:f + 1], q, ALU.mult, ALU.mult, a, b)
                    banks.free[i1] = [a]
                    a = halve(q, [z[:, f * 512:(f + 1) * 512] for z in h], a, hf)
                    tr.free[qi] = [a[1]]
                    ta.append(a)
                xr.free[xi] = [b]
                if c + 1 < CHUNKS:
                    T[c + 1] = x_halves(c + 1)
                T["h1", c] = (h, hi, ta)

            def middle(wn, c):
                h, hi, ta = T[wn, c]
                g, gf, gi = hr.next() if wn == "h1" else last.next()
                si = 2 if wn == "h1" else 3
                tb = []
                for f in range(4):
                    p, pf, pi = banks.next()
                    for k in range(4):
                        o = k * 512 + f * 128
                        a = mm3(p, [z[:, o:o + 128] for z in W[wn]], [z[:, k * 512:(k + 1) * 512] for z in h],
                                ta[k], tw[wn], pf, start=(k == 0), stop=(k == 3), inc=(k == 3))
                    if wn == "h1":
                        q, qf, qi = tr.next()
                        b = act(q, p, ACT.Gelu, a, qf, scale=sc[:, si, f:f + 1])
                        banks.free[pi] = [b]
                        b = halve(q, [z[:, f * 512:(f + 1) * 512] for z in g], b, gf)
                        tr.free[qi] = [b[1]]
                    else:
                        b = act(g[:, f, :], p, ACT.Gelu, a, gf, scale=sc[:, si, f:f + 1])
                        banks.free[pi] = [b]
                    tb.append(b)
                hr.free[hi] = [a]
                T["h2" if wn == "h1" else "w3", c] = (g, gi, tb)

            def down(c):
                h, hi, ta = T["w3", c]
                for j in range(4):
                    t = 4 * c + j
                    p, pf, pi = banks.next()
                    for k in range(4):
                        a = mm(p[:, 0:128], h[:, k, j * 128:(j + 1) * 128], w3[:, k, :], ta[k], t_w3, pf,
                               start=(k == 0), stop=(k == 3), inc=(k == 3))
                    b = stt(tmp[:, j * 128:(j + 1) * 128], p[:, 0:128], 0.5, s3, ALU.mult, ALU.mult, a, t_s3)
                    banks.free[pi] = [b]
                    b = tt(x[:, t, :], x[:, t, :], tmp[:, j * 128:(j + 1) * 128], ALU.add, b)
                last.free[hi] = [a]
                finish(c, b, banks)

            up(0)
            middle("h1", 0)
            for c in range(CHUNKS):
                if c + 1 < CHUNKS:
                    up(c + 1)
                middle("h2", c)
                if c + 1 < CHUNKS:
                    middle("h1", c + 1)
                down(c)

        def pre_l1_attn(w):
            wk, wka, wv = take(128), take(128), take(128)
            cols = take(5)
            t_w = [dma(wk, ins["WkT1"], w), dma(wka, ins["WkaT1"], w), dma(wv, ins["WvT1"], w)]
            t_w += [dma(cols[:, i:i + 1], ins["L1_attn_" + n].rearrange("(p a) -> p a", a=1), w)
                    for i, n in enumerate(("gamma", "beta", "bk", "bka", "bv"))]
            return (wk, wka, wv, cols, t_w), None

        def l1_attn():
            xn, xT, txn, tx, (wk, wka, wv, cols, t_w) = begin()
            banks = Ring(bank)
            ka = ts(cols[:, 3:4], cols[:, 3:4], 128 ** -0.5, None, ALU.mult, None, t_w)
            keys, vals, kw, kk, cum, pr = (take(2048) for _ in range(6))
            prefetch()
            ones = cF("onesrow")
            T = {}

            def normalise(c):
                T["n", c] = ln_apply(c, xn, xn, T["s", c])

            def turn(c):
                T["x", c] = features_chunk(c, xn, xT, T["n", c], banks, post=lambda o, p, w: ts(
                    o, p, cols[:, 0:1], cols[:, 1:2], ALU.mult, ALU.add, w, t_w))

            def project(c):
                s = slice(c * 512, (c + 1) * 512)
                p, pf, pi = banks.next()
                a = mm(p[:, :], wk, xT[:, s], T["x", c], t_w, pf, inc=True)
                k_ = act(keys[:, s], p[:, :], ACT.Identity, a, bias=cols[:, 2:3])
                banks.free[pi] = [k_]
                p, pf, pi = banks.next()
                a = mm(p[:, :], wv, xT[:, s], pf, inc=True)
                v_ = act(vals[:, s], p[:, :], ACT.Identity, a, bias=cols[:, 4:5])
                banks.free[pi] = [v_]
                p, pf, pi = banks.next()
                a = mm(p[:, :], wka, keys[:, s], k_, pf, inc=True)
                w_ = act(kw[:, s], p[:, :], ACT.Exp, a, ka, bias=cols[:, 3:4], scale=128 ** -0.5)
                banks.free[pi] = [w_]
                b = tt(kk[:, s], kw[:, s], keys[:, s], ALU.mult, w_, eng=PO)
                T["p", c] = (w_, v_, b)

            def pool_keys(c):
                s = slice(c * 512, (c + 1) * 512)
                w_, v_, kk_ = T["p", c]
                a = DV(lambda e: e.tensor_tensor_scan(cum[:, s], ones, kw[:, s], 0.0, ALU.mult, ALU.add), w_)
                a = DV(lambda e: e.reciprocal(cum[:, s], cum[:, s]), a)
                a = tt(kk[:, s], kk[:, s], cum[:, s], ALU.mult, a, kk_)
                a = DV(lambda e: e.tensor_tensor_scan(cum[:, s], ones, kk[:, s], 0.0, ALU.mult, ALU.add), a)
                T["r", c] = tt(pr[:, s], cum[:, s], vals[:, s], ALU.mult, a, v_)

            def add(c):
                p, pf, pi = banks.next()
                for j in range(4):
                    b = tp(p[:, j * 128:(j + 1) * 128], pr[:, c * 512 + j * 128:c * 512 + (j + 1) * 128], T["r", c], pf, inc=(j == 3))
                xc = x[:, 4 * c:4 * c + 4, :].rearrange("p t n -> p (t n)")
                b = tt(xc, xc, p[:, :], ALU.add, b)
                banks.free[pi] = [b]
                finish(c, b, banks)

            for c in range(CHUNKS):
                T["s", c] = ln_stats(c, xn, txn[c])
            normalise(0)
            turn(0)
            normalise(1)
            project(0)
            for c in range(CHUNKS):
                if c + 1 < CHUNKS:
                    turn(c + 1)
                if c + 2 < CHUNKS:
                    normalise(c + 2)
                pool_keys(c)
                if c + 1 < CHUNKS:
                    project(c + 1)
                if c > 0:
                    add(c - 1)
            add(CHUNKS - 1)

        def transposed_gates(g, gT, p, a):
            last = {}
            for c in range(CHUNKS):
                for j in range(4):
                    t = 4 * c + j
                    b = tp(p[c][0:8, j * 128:(j + 1) * 128], g[:, t, :], a, last.get(c - 2), inc=(j == 3))
                b = acopy(gT[0:8, c * 512:(c + 1) * 512], p[c][0:8, :], b)
                last[c] = b
            return b

        def pre_l2(w):
            wr, wrb, wu = take(8), take(8), take(4 * FM)
            bu = take(12).rearrange("p (g f) -> p g f", g=4)
            S["route"] = (wr, [dma(wr, ins["L2_ffn_Wr"], w), dma(wrb, ins["L2_ffn_br"].partition_broadcast(128), w)])
            t_wu = dma(wu.rearrange("p (g f) -> p g f", g=4), ins["L2_ffn_W_up"].rearrange("g p f -> p g f"), w)
            t_bu = dma(bu[:, :, :], ins["bup"], w)
            whu = fine(4 * FM)
            t_whu = []
            return (wrb, bu, t_bu, whu, t_whu), lambda: t_whu.extend(halve(wu, whu, t_wu))

        def l2_ffn():
            xn, xT, txn, tx, (wrb, bu, t_bu, whu, t_whu) = begin()
            wd = take(3 * 8 * 128)
            passing = mem["used"][-1:]
            wdv = wd.rearrange("p (f e n) -> p f e n", f=3, e=8)
            bd = take(128)
            t_wd = [dma(wdv[:, 0:2, e, :], ins["L2_ffn_W_down"][e, 0:256].rearrange("(f p) n -> p f n", p=128)) for e in range(8)]
            t_wd += [dma(wdv[0:85, 2, :, :], ins["L2_ffn_W_down"][:, 256:FM].rearrange("e p n -> p e n"))]
            t_bd = dma(bd[0:8, :], ins["L2_ffn_b_down"])
            v3 = lambda: take(128).rearrange("p (t e) -> p t e", e=8)
            raw, tmp, eq, gt, gate = v3(), v3(), v3(), v3(), v3()
            mx = take(16)
            cnt, tmp8, need = take(24), take(8), take(8)
            raw, a = router(raw, tmp, mx, bias=wrb)
            cmpb = take(384, BF16)
            cmpv = cmpb[:, 0:128].rearrange("p (t e) -> p t e", e=8)
            b8 = lambda q: q.unsqueeze(1).to_broadcast([128, NT, 8])
            sp = bank[3]

            whd = fine(3 * 8 * 128)
            xr = Ring([fine(512) for _ in range(2)])
            mr = Ring([take(3 * 512) for _ in range(10)])
            ub = Ring(bank[0:3])
            ub.free[2] = [a]
            item, xh = {}, {}

            def halve_rows(src, pair, cut, *w, lo=None):
                u = halve(src[:, 0:cut], [z[:, 0:cut] for z in pair], *w, lo=lo)
                v = halve(src[0:85, cut:], [z[0:85, cut:] for z in pair], *w, lo=PO)
                return u + v

            hl = Ring([fine(3 * 512) for _ in range(2)])
            halves = {}

            def halve_item(n):
                m, mi, tm, _ = item[n]
                pair, hf, hi = hl.next()
                halves[n] = (pair, hi, halve_rows(m, pair, 1024, tm, hf, lo=PO if n < 2 else None))
                mr.free[mi] = halves[n][2]

            t_whd = []

            def halve_down(i):
                r, o = slice(0, 128 if i < 4 else 85), slice(i * 512, (i + 1) * 512)
                t_whd.extend(halve(wd[r, o], [z[r, o] for z in whd], t_wd, lo=PO))


            def x_halves(c):
                xx, xf, xi = xr.next()
                xh[c] = (xx, xi, halve(xT[:, c * 512:(c + 1) * 512], xx, tx[c], xf, lo=PO))

            def up(n, f):
                c, g = n // 4, n % 4
                xx, xi, txx = xh[c]
                if f == 0:
                    m, mf, mi = mr.next()
                    item[n] = [m, mi, [], mf]
                m, mi, tm, mf = item[n]
                f0, fn = L2T[f]
                p, pf, pi = ub.next()
                a = mm3(p[0:fn, :], [z[:, g * FM + f0:g * FM + f0 + fn] for z in whu], xx, txx, t_whu, pf, inc=True)
                b = act(m[0:fn, f * 512:(f + 1) * 512], p[0:fn, :], ACT.Silu, a, mf, t_bu, bias=bu[0:fn, g, f:f + 1])
                ub.free[pi] = [b]
                tm.append(b)
                if g == 3 and f == 2:
                    xr.free[xi] = [a]

            ups = iter([(n, f) for n in range(16) for f in range(3)])

            def up_next():
                n, f = next(ups)
                if n % 4 == 0 and f == 0 and n // 4 + 1 < CHUNKS:
                    x_halves(n // 4 + 1)
                up(n, f)

            def count(cols, w):
                c_ = mm(sp[:, 0:cols], onesb, cmpb[:, 0:cols], w, inc=True)
                k = cols // 128
                return red(cnt[:, 0:8 * k].rearrange("p (j e) -> p j e", e=8),
                           sp[:, 0:cols].rearrange("p (j t e) -> p j e t", j=k, e=8), ALU.add, c_)

            x_halves(0)
            sel = [take(32).rearrange("p (j e) -> p j e", e=8) for _ in range(2)]
            cand = take(24).rearrange("p (j e) -> p j e", e=8)
            b = mset(sel[0][:, 3, :], 0.0, a)
            r4 = lambda q: q.unsqueeze(1).to_broadcast([128, 3, NT, 8])
            for step, bit in enumerate(range(28, -1, -2)):
                s, lo = sel[step % 2], sel[step % 2][:, 3, :]
                w = b
                for j in range(3):
                    b = ts(cand[:, j, :].bitcast(I32), lo.bitcast(I32), (j + 1) << bit, None, ALU.bitwise_or, None, w)
                b = tt(cmpb.rearrange("p (j t e) -> p j t e", j=3, e=8), r4(raw),
                       cand.unsqueeze(2).to_broadcast([128, 3, NT, 8]), ALU.is_ge, b)
                b = count(384, b)
                up_next()
                up_next()
                if 4 <= step < 10:
                    halve_down(step - 4)
                if step in (10, 12):
                    halve_item(step // 2 - 5)
                b = stt(s[:, 0:3, :], cnt.rearrange("p (j e) -> p j e", e=8), 256.0, cand, ALU.is_ge, ALU.mult, b)
                b = red(sel[1 - step % 2][:, 3, :], s.rearrange("p j e -> p e j"), ALU.max, b)
            lo = sel[1][:, 3, :]
            g_ = tt(gt, raw, b8(lo), ALU.is_gt, b)
            q_ = tt(eq, raw, b8(lo), ALU.is_equal, g_)
            c_ = vcopy(cmpv, gt, g_)
            vcopy(cmpb[:, 128:256].rearrange("p (t e) -> p t e", e=8), eq, q_)
            b = count(128, (DV.sem, DV.n))
            b = ts(need, cnt[:, 0:8], -1.0, 256.0, ALU.mult, ALU.add, b)
            mm(bank[4][:, 0:128], tri, cmpb[:, 128:256], inc=False)
            q_ = mm(bank[5][:, 0:128], onesb, cmpb[:, 128:256], inc=True)
            tot = take(128)
            pre = take(128)
            q_ = vcopy(tot.rearrange("p (e t) -> p e t", e=8), bank[5][:, 0:128].rearrange("p (t e) -> p e t", e=8), q_)
            q_ = DV(lambda e: e.tensor_tensor_scan(pre, cF("scanreset"), tot, 0.0, ALU.mult, ALU.add), q_)
            q_ = tt(pre, pre, tot, ALU.subtract, q_)
            q_ = tt(tmp, bank[4][:, 0:128].rearrange("p (t e) -> p t e", e=8), pre.rearrange("p (e t) -> p t e", e=8), ALU.add, q_)
            q_ = tt(tmp, tmp, b8(need), ALU.is_lt, q_, b)
            q_ = tt(tmp, tmp, eq, ALU.mult, q_)
            q_ = tt(gt, gt, tmp, ALU.add, q_)
            q_ = stt(gate, gt, 0.5, raw, ALU.mult, ALU.mult, q_)

            gT = xn[:, :, :].rearrange("p t n -> p (t n)")
            prefetch(*t_whd, over=passing)
            yb = Ring([bank[i] for i in (6, 7, 3, 4, 5)])
            yb.free[2] = [b]
            yb.free[3] = yb.free[4] = [q_]
            for n in range(16):
                c, g = n // 4, n % 4
                pair, hi, th = halves[n]
                for j in range(4):
                    t = 4 * c + j
                    if (n, j) == (0, 3):
                        t_g = transposed_gates(gate, gT, [bank[i] for i in (4, 5, 4, 5)], q_)
                        yb.free[3] = yb.free[4] = [t_g]
                    if g == 1:
                        p, pf, pi = yb.next()
                        a = mm(p[:, 0:128], gT[0:8, t * 128:(t + 1) * 128], bd[0:8, :], t_g, t_bd, pf, inc=True)
                        b = tt(x[:, t, :], x[:, t, :], p[:, 0:128], ALU.add, a)
                        yb.free[pi] = [b]
                    p, pf, pi = yb.next()
                    for f, (f0, fn) in enumerate(L2T):
                        o = f * 512 + j * 128
                        wo = f * 1024 + g * 256
                        a = mm3(p[:, 0:256], [z[0:fn, o:o + 128] for z in pair], [z[0:fn, wo:wo + 256] for z in whd],
                                th, t_whd, pf, start=(f == 0), stop=(f == 2), inc=(f == 2))
                    for h in range(2):
                        e = 2 * g + h
                        b = stt(x[:, t, :], p[:, h * 128:(h + 1) * 128], gate[:, t, e:e + 1], x[:, t, :],
                                ALU.mult, ALU.add, a, b, q_)
                    yb.free[pi] = [b]
                hl.free[hi] = [a]
                if n + 10 < 16:
                    for _ in range(3):
                        up_next()
                if n + 2 < 16:
                    halve_item(n + 2)
                if g == 3:
                    finish(c, b, yb)

        def pre_l2_attn(w):
            wq, wk, wv, wo = (take(128) for _ in range(4))
            bq = take(1)
            bkb, bvb, bob = (take(128) for _ in range(3))
            t_w = [dma(wq, ins["WqT2"], w), dma(wk, ins["WkT2"], w), dma(wv, ins["WvT2"], w), dma(wo, ins["WoT2"], w),
                   dma(bq, ins["L2_attn_bq"].rearrange("(p a) -> p a", a=1), w)]
            t_w += [dma(o, ins["L2_attn_" + n].partition_broadcast(128), w) for o, n in ((bkb, "bk"), (bvb, "bv"), (bob, "bo"))]
            return (wq, wk, wv, wo, bq, bkb, bvb, bob, t_w), None

        def l2_attn():
            xn, xT, txn, tx, (wq, wk, wv, wo, bq, bkb, bvb, bob, t_w) = begin()
            banks = Ring(bank)
            q, tq, o = take(2048), take(2048), take(2048)
            k, tk, v = take(2048), take(2048), take(2048)
            kv = take(512)
            prefetch()
            for b_ in range(4):
                s = slice(b_ * 512, (b_ + 1) * 512)
                p, pf, pi = banks.next()
                a = mm(p[:, :], wq, xT[:, s], tx[b_], t_w, pf, inc=True)
                q1 = ts(tq[:, s], p[:, :], bq, 0.0, ALU.add, ALU.min, a, t_w)
                q2 = ts(q[:, s], p[:, :], bq, 0.0, ALU.add, ALU.max, a)
                banks.free[pi] = [q2]
                q1 = act(tq[:, s], tq[:, s], ACT.Exp, q1)
                t_q = tt(q[:, s], q[:, s], tq[:, s], ALU.add, q1, q2)
                bc4 = lambda z: z.unsqueeze(1).to_broadcast([128, 4, 128])
                r4 = lambda z: z.rearrange("p (t n) -> p t n", t=4)
                p, pf, pi = banks.next()
                for j in range(4):
                    a = mm(p[:, j * 128:(j + 1) * 128], xT[:, b_ * 512 + j * 128:b_ * 512 + (j + 1) * 128], wk, pf, inc=(j == 3))
                k1 = tt(r4(k[:, s]), r4(p[:, :]), bc4(bkb), ALU.add, a)
                banks.free[pi] = [k1]
                k2 = ts(tk[:, s], k[:, s], 0.0, None, ALU.min, None, k1)
                k2 = act(tk[:, s], tk[:, s], ACT.Exp, k2)
                t_k = stt(k[:, s], k[:, s], 0.0, tk[:, s], ALU.max, ALU.add, k2)
                p, pf, pi = banks.next()
                for j in range(4):
                    a = mm(p[:, j * 128:(j + 1) * 128], xT[:, b_ * 512 + j * 128:b_ * 512 + (j + 1) * 128], wv, pf, inc=(j == 3))
                t_v = tt(r4(v[:, s]), r4(p[:, :]), bc4(bvb), ALU.add, a)
                banks.free[pi] = [t_v]
                p, pf, pi = banks.next()
                for j in range(4):
                    u = slice(b_ * 512 + j * 128, b_ * 512 + (j + 1) * 128)
                    a = mm(p[:, 0:128], k[:, u], v[:, u], t_k, t_v, pf, start=(j == 0), stop=(j == 3), inc=(j == 3))
                kvb = kv[:, b_ * 128:(b_ + 1) * 128]
                t_kv = tt(kvb, p[:, 0:128], cF("blockdiag"), ALU.mult, a)
                banks.free[pi] = [t_kv]
                p, pf, pi = banks.next()
                a = mm(p[:, :], kvb, q[:, s], t_kv, t_q, pf, inc=True)
                t_o = acopy(o[:, s], p[:, :], a)
                banks.free[pi] = [t_o]
                p, pf, pi = banks.next()
                for j in range(4):
                    a = mm(p[:, j * 128:(j + 1) * 128], o[:, b_ * 512 + j * 128:b_ * 512 + (j + 1) * 128], wo, t_o, pf, inc=(j == 3))
                xc = x[:, 4 * b_:4 * b_ + 4, :]
                a = tt(xc, xc, r4(p[:, :]), ALU.add, a)
                banks.free[pi] = [a]
                a = tt(xc, xc, bc4(bob), ALU.add, a)
                finish(b_, a, banks)

        def pre_l3(w):
            wr, wrb = take(8), take(8)
            S["route"] = (wr, [dma(wr, ins["L3_ffn_Wr"], w), dma(wrb, ins["L3_ffn_br"].partition_broadcast(128), w)])
            return wrb, None

        def l3_ffn():
            xn, xT, txn, tx, wrb = begin()
            NTL, EARLY = 15, 2
            xh = fine(2048)
            t_xh = halve(xn[:, :, :].rearrange("p t n -> p (t n)"), xh, txn, lo=PO)
            wb = [(take(512), take(1024).rearrange("p (k n) -> p k n", k=4), take(256).rearrange("p (k n) -> p k n", k=2),
                   take(6), take(128)) for _ in range(4)]
            wfree = [[], [], [], []]
            wh = [(fine(512), fine(1024)) for _ in range(2)]
            t_up, t_down, tw1, tw2 = {}, {}, {}, {}

            def split_w(i):
                u, v = wb[i % 4][0:2]
                tw1[i] = halve(u, wh[i % 2][0], t_we[i], t_up.get(i - 2))
                tw2[i] = halve(v.rearrange("p k n -> p (k n)"), wh[i % 2][1], t_we[i], t_down.get(i - 2))

            v3 = lambda: take(128).rearrange("p (t e) -> p t e", e=8)
            tmp, m, mh, wi = v3(), v3(), v3(), v3()
            mx, vm = take(16), take(16)
            mb = take(128, BF16)
            a = None
            lg, a = router(None, mh, mx, bias=wrb)
            a = argmax_mask(lg, m, mx, tmp, vm, a)
            a = vcopy(mb, m.rearrange("p t e -> p (t e)"), a)
            mm(bank[1][:, 0:128], tri, mb, a)
            a = mm(bank[2][:, 0:128], onesb, mb, inc=True)
            tot, pre = take(128), take(128)
            et = lambda q: q.rearrange("p (e t) -> p e t", e=8)
            b = vcopy(et(tot), bank[2][:, 0:128].rearrange("p (t e) -> p e t", e=8), a)
            b = DV(lambda e: e.tensor_tensor_scan(pre, cF("scanreset"), tot, 0.0, ALU.mult, ALU.add), b)
            n8, cum = take(8), take(8)
            cmp8 = v3()
            k8 = cF("k256").rearrange("p (e k) -> p e k", e=8)
            c_ = tt(cmp8[:, 0:8, :], et(pre)[:, :, 15:16].to_broadcast([128, 8, 8]), k8, ALU.is_gt, b)
            c_ = red(n8, cmp8[:, 0:8, :], ALU.add, c_)
            c_ = DV(lambda e: e.tensor_tensor_scan(cum, cF("onesrow")[:, 0:8], n8, 0.0, ALU.mult, ALU.add), c_)
            i16 = cF("i16").rearrange("p (i e) -> p i e", e=8)
            d_ = tt(cmp8, cum.unsqueeze(1).to_broadcast([128, NT, 8]), i16, ALU.is_le, c_)
            te = take(16)
            d_ = red(te, cmp8, ALU.add, d_)
            d_ = ts(te.bitcast(I32), te, 7.0, None, ALU.min, None, d_)
            t_te = d_
            n8b = take(8)
            b = tt(pre, pre, tot, ALU.subtract, b, c_)
            c_ = tt(n8b, cum, n8, ALU.subtract, c_)
            c_ = ts(n8b, n8b, 256.0, None, ALU.mult, None, c_)
            b = tt(wi, bank[1][:, 0:128].rearrange("p (t e) -> p t e", e=8), pre.rearrange("p (e t) -> p t e", e=8), ALU.add, b, a)
            b = tt(wi, wi, n8b.unsqueeze(1).to_broadcast([128, NT, 8]), ALU.add, b, c_)
            b = tt(wi, wi, m, ALU.mult, b)
            slf = take(16)
            b = red(slf, wi, ALU.add, b)
            slot = take(16).bitcast(mybir.dt.uint32)
            t_slot = vcopy(slot, slf, b)
            Gd, Yd = ins["sorted_x"], ins["sorted_y"]

            def pool_dma(fn, *w):
                k = state["p"] % 16
                state["p"] += 1
                pcount[k] += 16
                dma_last["pool", k] = (psems[k], pcount[k])
                PO.q.append((PO.wait(*w), fn, (psems[k], 16)))
                return dma_last["pool", k]

            t_sc = [pool_dma(lambda e, t=t: e.indirect_dma_start(
                Gd, bass.IndirectOffsetOnAxis(ap=slot[:, t:t + 1], axis=0), xn[:, t, :], None), t_slot, txn[t // 4])
                for t in range(NT)]

            def load_w(i):
                u, v, w, bc, b3 = wb[i % 4]
                toks, incs = [], []
                for _ in range(5):
                    k = state["d"] % 96
                    state["d"] += 1
                    dcount[k] += 16
                    dma_last[k] = (dsems[k], dcount[k])
                    toks.append(dma_last[k])
                    incs.append(dsems[k])

                def fn(e):
                    ex = bass.ds(e.value_load(te[0:1, i:i + 1].bitcast(I32), min_val=0, max_val=7), 1)
                    one = lambda n: ins[n][ex]
                    e.dma_start(u, one("L3_ffn_W1").rearrange("a p n -> (a p) n")).then_inc(incs[0], 16)
                    e.dma_start(v, one("L3_ffn_W2").rearrange("a (k p) n -> (a p) k n", p=128)).then_inc(incs[1], 16)
                    e.dma_start(w, one("L3_ffn_W3").rearrange("a (k p) n -> (a p) k n", p=128)).then_inc(incs[2], 16)
                    e.dma_start(bc, one("b12c").rearrange("a p n -> (a p) n")).then_inc(incs[3], 16)
                    e.dma_start(b3, one("L3_ffn_b3").to_broadcast([128, 128])).then_inc(incs[4], 16)

                SP.q.append((SP.wait(t_te, wfree[i % 4]), fn, None))
                return toks

            t_we = {i: load_w(i) for i in range(4)}
            gr = Ring([take(256).rearrange("p (h n) -> p h n", h=2) for _ in range(3)])
            G2 = Gd.rearrange("(i h p) n -> i p h n", h=2, p=128)
            Y2 = Yd.rearrange("(i h p) n -> i p h n", h=2, p=128)
            gl = {}

            def load_g(i):
                g, gf, gi = gr.next()
                gl[i] = (g, gi, dma(g, G2[i], t_sc, gf))

            banks = Ring(bank[3:8] + bank[0:3])
            for i in range(8):
                banks.free[i] = [b, a]
            xr = Ring([fine(256) for _ in range(2)])
            h1r = Ring([fine(1024) for _ in range(2)])
            qr = Ring([take(256) for _ in range(3)])
            h2r = Ring([take(512).rearrange("p (k n) -> p k n", k=2) for _ in range(2)])
            yr = Ring([take(256).rearrange("p (h n) -> p h n", h=2) for _ in range(2)])
            t_y = []
            xg = {}
            hot = Ring([take(16 * 256, F32R) for _ in range(2)])
            here = take(16)

            def pick(i):
                d, df, di = hot.next()
                b = ts(here, slf, 256.0 * i, None, ALU.subtract, None, t_slot, T.get("pick"))
                p, pf, pi = banks.next()
                for t in range(NT):
                    o = slice(t * 256, (t + 1) * 256)
                    T["pick"] = c_ = ts(d[:, o], iota[:, 0:256], here[:, t:t + 1], None, ALU.is_equal, None, b, df, t_c)
                    u = slice(t * 128, (t + 1) * 128)
                    mm(p[:, 0:256], xh[0][:, u], d[:, o], c_, t_xh, pf, start=(t == 0), stop=False)
                    a = mm(p[:, 0:256], xh[1][:, u], d[:, o], start=False, stop=(t == NT - 1), inc=(t == NT - 1))
                hot.free[di] = [a]
                xx, xf, xi = xr.next()
                a = halve(p[:, 0:256], xx, a, xf)
                banks.free[pi] = [a[1]]
                xg[i] = (xx, xi, a)

            def fetch(i):
                if EARLY <= i and i + 2 < NTL:
                    load_g(i + 2)
                if i < EARLY:
                    return pick(i)
                g, gi, tg = gl[i]
                p, pf, pi = banks.next()
                for h in range(2):
                    a = tp(p[:, h * 128:(h + 1) * 128], g[:, h, :], tg, pf, inc=(h == 1))
                gr.free[gi] = [a]
                xx, xf, xi = xr.next()
                a = halve(p[:, 0:256], xx, a, xf)
                banks.free[pi] = [a[1]]
                xg[i] = (xx, xi, list(a))

            hs, gs, T = {}, {}, {}

            def up(i):
                xx, xi, txx = xg[i]
                h, hf, hi = h1r.next()
                ta = []
                for f in range(4):
                    p, pf, pi = banks.next()
                    a = mm3(p[:, 0:256], [z[:, f * 128:(f + 1) * 128] for z in wh[i % 2][0]], xx, pf, tw1[i], txx, inc=True)
                    q, qf, qi = qr.next()
                    b = act(q, p[:, 0:256], ACT.Gelu, a, qf, t_we[i], bias=wb[i % 4][3][:, f:f + 1])
                    banks.free[pi] = [b]
                    b = halve(q, [z[:, f * 256:(f + 1) * 256] for z in h], b, hf, hi=DV)
                    qr.free[qi] = [b[1]]
                    ta.append(b)
                t_up[i] = xr.free[xi] = [a]
                hs[i] = (h, hi, ta)

            def down(i):
                h, hi, ta = hs[i]
                g, gf, gi = h2r.next()
                tb = []
                for f in range(2):
                    p, pf, pi = banks.next()
                    for k in range(4):
                        o = k * 256 + f * 128
                        a = mm3(p[:, 0:256], [z[:, o:o + 128] for z in wh[i % 2][1]], [z[:, k * 256:(k + 1) * 256] for z in h],
                                ta[k], tw2[i], pf, start=(k == 0), stop=(k == 3), inc=(k == 3))
                    b = act(g[:, f, :], p[:, 0:256], ACT.Gelu, a, gf, bias=wb[i % 4][3][:, 4 + f:5 + f])
                    banks.free[pi] = [b]
                    tb.append(b)
                t_down[i] = h1r.free[hi] = [a]
                gs[i] = (g, gi, tb)

            def last(i):
                g, gi, tb = gs[i]
                w3, b3 = wb[i % 4][2], wb[i % 4][4]
                p, pf, pi = banks.next()
                for s in range(2):
                    for k in range(2):
                        a = mm(p[:, s * 128:(s + 1) * 128], g[:, k, s * 128:(s + 1) * 128], w3[:, k, :], tb[k], pf,
                               start=(k == 0), stop=(k == 1), inc=(k == 1))
                h2r.free[gi] = [a]
                y, yf, yi = yr.next()
                b = tt(y, p[:, 0:256].rearrange("p (h n) -> p h n", h=2), b3.unsqueeze(1).to_broadcast([128, 2, 128]),
                       ALU.add, a, yf)
                banks.free[pi] = [b]
                wfree[i % 4] = [a, b, tw1[i], tw2[i]]
                yr.free[yi] = [dma(Y2[i], y, b)]
                t_y.extend(yr.free[yi])
                if i + 4 < NTL:
                    t_we[i + 4] = load_w(i + 4)

            fetch(0)
            split_w(0)
            up(0)
            fetch(1)
            split_w(1)
            load_g(EARLY)
            load_g(EARLY + 1)
            for i in range(NTL):
                down(i)
                if i + 1 < NTL:
                    up(i + 1)
                if i + 2 < NTL:
                    fetch(i + 2)
                    split_w(i + 2)
                last(i)
            yg = take(2048).rearrange("p (t n) -> p t n", t=NT)
            prefetch()
            for c in range(CHUNKS):
                for t in range(4 * c, 4 * c + 4):
                    g_ = pool_dma(lambda e, t=t: e.indirect_dma_start(
                        yg[:, t, :], None, Yd, bass.IndirectOffsetOnAxis(ap=slot[:, t:t + 1], axis=0)), t_y, t_slot)
                    a = stt(x[:, t, :], yg[:, t, :], 0.5, x[:, t, :], ALU.mult, ALU.add, g_)
                finish(c, a, banks)

        def pre_attention(kind, w):
            wq, wk, wv, wo = (take(128) for _ in range(4))
            bcol, bub = take(1), take(128)
            if kind == 0:
                t_w = [dma(wq, ins["wqT0"], w), dma(bcol, ins["L0_attn_bq"].rearrange("(p a) -> p a", a=1), w),
                       dma(wo, ins["wuT0"], w), dma(bub, ins["L0_attn_bu"].partition_broadcast(128), w)]
            else:
                t_w = [dma(o, ins["L3_attn_w_" + n], w) for o, n in ((wq, "q"), (wk, "k"), (wv, "v"), (wo, "o"))]
            return (wq, wk, wv, wo, bcol, bub, t_w), None

        def attention(kind):
            xn, xT, txn, tx, (wq, wk, wv, wo, bcol, bub, t_w) = begin()
            scale = 128 ** -0.5 if kind == 0 else 8 ** -0.5
            nm = 3 if kind == 0 else 12
            K = 96 + nm
            ws = [wq] if kind == 0 else [wq, wk]
            pieces = [(take(8192, BF16), take(8192, BF16)) for _ in range(2)]
            pfree = [[], []]
            stage = take(8192, BF16) if kind == 0 else None
            rows = ins["key_rows0" if kind == 0 else "key_rows3"]
            t_init = [[dma(kk[72:K, :].bitcast(F32), rows), dma(qq[72:96, :].bitcast(F32), rows[0:24])] for qq, kk in pieces]
            if kind == 0:
                t_init[0].append(dma(stage[72:96, :].bitcast(F32), rows[0:24]))
            ebuf = take(8192)
            er = Ring([ebuf[:, i * 1024:(i + 1) * 1024] for i in range(8)])
            ve, t_ve = None, None
            if kind == 3:
                ve = take(16 * 16 * 32).rearrange("p (t h m) -> p t h m", t=16, h=16)
                b = mset(ve.rearrange("p t h m -> p (t h m)"), 0.0, eng=PO)
                t_vi = mset(ve[:, :, :, 8:9], 1.0, b, eng=PO)
            banks = Ring(bank[0:4])
            n_buf, size = (4, 1792) if kind == 0 else (6, 1280)
            pr = Ring([(ebuf[:, o:o + 512], [ebuf[:, o + 512 + 256 * i:o + 768 + 256 * i].bitcast(BF16) for i in range(3)],
                        ebuf[:, o + 1280:o + size])
                       for o in range(0, n_buf * size, size)])
            scr = ins["scratch"]
            t_scr = [[[] for _ in ws] for _ in range(CHUNKS)]

            items = [(c, side) for c in range(CHUNKS) for side in range(len(ws))]
            live = {}

            def step(i, k):
                c, side = items[i]
                s = slice(c * 512, (c + 1) * 512)
                if k == 0:
                    buf, rf, ri = pr.next()
                    p, pf, pi = banks.next()
                    a = mm(p[:, :], ws[side], xT[:, s], tx[c], t_w, pf, inc=True)
                    if kind == 0:
                        a = act(buf[2], p[:, :], ACT.Identity, a, rf, bias=bcol)
                        banks.free[pi] = [a]
                        b = vcopy(buf[1][0], buf[2], a)
                    else:
                        b = acopy(buf[1][0], p[:, :], a, rf)
                    live[i] = (buf, ri, pi, p, b, rf)
                    return
                (rem, parts, full), ri, pi, p, b, rf = live[i]
                if k == 1:
                    b = tt(rem, full if kind == 0 else p[:, :], parts[0], ALU.subtract, b, rf)
                    if kind == 3:
                        banks.free[pi] = [b]
                elif k == 2:
                    b = acopy(parts[1], rem, b)
                elif k == 3:
                    b = tt(rem, rem, parts[1], ALU.subtract, b)
                else:
                    b = acopy(parts[2], rem, b)
                    t_scr[c][side] = [dma(scr[side, :, 8 * j:8 * j + 8, s], parts[j], b) for j in range(3)]
                    pr.free[ri] = t_scr[c][side]
                    if (c, side) == ((0, 0) if kind == 0 else items[-1]):
                        for lo, hi in PARTS[0]:
                            load_queries(0, lo, hi)
                            load_keys(0, lo, hi)
                live[i] = ((rem, parts, full), ri, pi, p, b, rf)

            sfree, ksrc = [], {}
            t_q, t_k = {}, {}
            PARTS = {0: [(0, 2), (2, 4)] if kind == 0 else [(0, 1), (1, 4)]}

            def load(i, dst, side, part_of, lo, hi, *w):
                toks = []
                runs = [(0, 0, 3), (1, 0, 3), (2, 0, 3)] if part_of == 0 else [(0, 0, 3), (1, 1, 3), (1, 0, 1), (2, 2, 3), (2, 0, 2)]
                for j, p0, p1 in runs:
                    r = 24 * j + 8 * ((p0 - part_of * j) % 3)
                    o = dst[r:r + 8 * (p1 - p0), :].rearrange("r (c t) -> r c t", c=16 if kind == 0 else 4)
                    v = scr[side, :, 8 * p0:8 * p1, :].rearrange("c r t -> r c t")
                    if kind == 0:
                        o, v = o[:, :, lo * 128:hi * 128], v[:, :, i * 512 + lo * 128:i * 512 + hi * 128]
                        ready = t_scr[i]
                    else:
                        o, v = o[:, lo:hi, :], v[:, 4 * i + lo:4 * i + hi, :]
                        ready = [t_scr[c][side] for c in range(CHUNKS)]
                    toks.append(dma(o, v, ready, *w))
                return toks

            def load_queries(i, lo, hi):
                a = load(i, pieces[i % 2][0], 0, 0, lo, hi, pfree[i % 2])
                for q in range(4 * i + lo, 4 * i + hi):
                    t_q[q] = [a, t_init[i % 2], t_init[0]]

            def load_keys(i, lo, hi):
                if kind == 0:
                    ksrc[i, lo] = load(i, stage, 0, 1, lo, hi, sfree)
                    return
                a = load(i, pieces[i % 2][1], 1, 1, lo, hi, pfree[i % 2])
                for q in range(4 * i + lo, 4 * i + hi):
                    t_k[q] = [a, t_init[i % 2]]

            def order_keys(i):
                if kind == 0:
                    kk = pieces[i % 2][1]
                    for lo, hi in PARTS.get(i, [(0, 4)]):
                        b = vcopy(kk[0:96, :].rearrange("p (g c t) -> p g c t", g=16, c=16)[:, 4 * lo:4 * hi, :, :],
                                  stage[0:96, :].rearrange("p (c g t) -> p g c t", g=16, c=16)[:, 4 * lo:4 * hi, :, :],
                                  ksrc[i, lo], t_init, pfree[i % 2])
                        for q in range(4 * i + lo, 4 * i + hi):
                            t_k[q] = [b, t_init[i % 2]]
                    sfree[:] = [b]
                    if i + 1 < 4:
                        load_keys(i + 1, 0, 4)

            for n in range(len(items) + 4):
                for k in range(5):
                    if 0 <= n - k < len(items):
                        step(n - k, k)
            for f in er.free:
                f.extend([t for c in t_scr for side in c for t in side])
            if kind == 3:
                for t in range(NT):
                    p, pf, pi = banks.next()
                    a = mm(p[:, 0:128], xT[:, t * 128:(t + 1) * 128], wv, pf, inc=True)
                    a = acopy(ve[:, t, :, 0:8], p[:, 0:128].rearrange("p (h d) -> p h d", h=16), a, t_vi)
                    banks.free[pi] = [a]
                t_ve = [a, t_vi]
            order_keys(0)
            load_queries(1, 0, 4)
            if kind == 3:
                load_keys(1, 0, 4)

            def queries(z, q, b):
                if kind == 0:
                    o = (q % 4) * 128 + b * 32
                    return z.rearrange("p (c t) -> p c t", c=16)[:, :, o:o + 32]
                o = (q % 4) * 2048 + b * 512
                return z[:, o:o + 512]

            def keys(z, q, b):
                o = ((q % 4) * 4 + b) * 512
                return z[:, o:o + 512]

            ar, br = Ring(bank[0:3]), Ring(bank[3:6])
            av, misc = Ring([bank[6]]), Ring([bank[7]])
            for r in (ar, br, av, misc):
                for i in range(len(r.bufs)):
                    r.free[i] = [f for g in banks.free for f in g]
            nkb = 1 if kind == 0 else 4
            nmx = 16 * nkb
            mxa = [take(nmx) for _ in range(3)]
            mneg = take(nmx)
            mpt = [take(3 * nmx, BF16) for _ in range(3)]
            vq = [take(512) for _ in range(2)] if kind == 0 else None
            vqfree = [[], []]
            ot = [take(512) for _ in range(2)]
            rcs = [take(16) for _ in range(2)]
            osb = take(NT * 128).rearrange("p (t n) -> p t n", t=NT)
            otr = Ring([take(512) for _ in range(2)])
            T = {}

            def stage_a(q, u):
                qq, kk = pieces[(q // 4) % 2]
                b, half = u // 2, u % 2
                for n in range(2):
                    p, pf, pi = ar.next()
                    qt = 2 * half + n
                    l, r = (keys(kk[0:72], q, b), queries(qq[0:72], q, b)) if kind == 0 else (
                        queries(qq[0:72], q, b), keys(kk[0:72], q, b))
                    a = mm(p[:, :], l[:, qt * 128:(qt + 1) * 128], r, t_q[q], t_k[q], pf, inc=True)
                    m = mxa[q % 3][:, (b * 4 + qt) * nkb:(b * 4 + qt + 1) * nkb]
                    c = red(m, p.rearrange("p (k n) -> p k n", k=nkb), ALU.max, a, T.get(("split", q - 3)))
                    ar.free[pi] = [c]
                T["max", q, u] = c

            def split(q):
                mx_ = mxa[q % 3]
                pt = mpt[q % 3].rearrange("p (b z) -> p b z", b=16)
                p0, p1, p2 = (pt[:, :, i * nkb:(i + 1) * nkb] for i in range(3))
                v = lambda z: z.rearrange("p (b k) -> p b k", k=nkb)
                a = ts(p0, v(mx_), -1.0, None, ALU.mult, None, T["max", q, 7], T.get(("place", q - 3, 3)))
                a = stt(v(mneg), v(mx_), -1.0, p0, ALU.mult, ALU.subtract, a)
                a = vcopy(p1, v(mneg), a)
                T["split", q] = tt(p2, v(mneg), p1, ALU.subtract, a)

            def place(q, b):
                qq, kk = pieces[(q // 4) % 2]
                pt = mpt[q % 3].rearrange("p (b z) -> p b z", b=16)
                p, pf, pi = misc.next()
                for k in range(4):
                    c = mm(p[96:K, k * 128:(k + 1) * 128], pt[:, b * 4 + k, :], identb, T["split", q], pf, inc=(k == 3))
                i_ = p[96:K, :]
                if kind == 0:
                    i_ = i_.rearrange("p (c t) -> p c t", c=16)
                T["place", q, b] = c
                T["mrow", q, b] = acopy(queries(qq[96:K], q, b), i_, c)
                misc.free[pi] = [T["mrow", q, b]]

            def values(q):
                qq, kk = pieces[(q // 4) % 2]
                p, pf, pi = misc.next()
                for b in range(4):
                    for k in range(4):
                        c = mm(p[:, b * 128 + k * 32:b * 128 + (k + 1) * 32], keys(kk[0:99], q, b)[:, k * 128:(k + 1) * 128],
                               cB("sel")[0:99, :], pf, t_k[q], inc=(b == 3 and k == 3))
                T["v", q] = acopy(vq[q % 2], p[:, :], c, vqfree[q % 2])
                misc.free[pi] = [T["v", q]]

            def stage_b(q, u):
                qq, kk = pieces[(q // 4) % 2]
                half, b = u // 4, u % 4
                e, ef, ei = er.next()
                for n in range(2):
                    p, pf, pi = br.next()
                    k = 2 * half + n
                    a = mm(p[:, :], keys(kk[0:K], q, b)[:, k * 128:(k + 1) * 128],
                           queries(qq[0:K], q, b), T["mrow", q, b], pf, inc=True)
                    c = act(e[:, n * 512:(n + 1) * 512], p, ACT.Exp, a, ef, scale=scale)
                    br.free[pi] = [c]
                T["e", q, u] = (e, ei, c)
                if u == 7:
                    pfree[(q // 4) % 2] = [a]
                    if q % 4 == 3 and q // 4 + 2 < 4:
                        load_queries(q // 4 + 2, 0, 4)
                        if kind == 3:
                            load_keys(q // 4 + 2, 0, 4)

            def stage_o(q, k):
                if k == 0:
                    T["av"] = av.next()
                p, pf, pi = T["av"]
                half, n = k // 2, k % 2
                for b in range(4):
                    e, ei, te = T["e", q, half * 4 + b]
                    if kind == 0:
                        lv, tv = vq[q % 2][:, b * 128 + k * 32:b * 128 + (k + 1) * 32], T["v", q]
                    else:
                        lv, tv = ve[:, b * 4 + k, q, :], t_ve
                    a = mm(p[32 * b:32 * b + 32, :], lv, e[:, n * 512:(n + 1) * 512], te, tv, pf,
                           start=(k == 0), stop=(k == 3), inc=(n == 1 and b == 3), skip=True)
                if n == 1:
                    for b in range(4):
                        er.free[T["e", q, half * 4 + b][1]] = [a]
                if k == 3:
                    vqfree[q % 2] = [a]
                    o = ot[q % 2]
                    a = DV(lambda e_: e_.transpose(o, p[:, :]), a, T.get(("norm", q - 2)))
                    av.free[pi] = [a]
                    ov = o.rearrange("p (c m) -> p c m", m=32)
                    rc = rcs[q % 2]
                    a = DV(lambda e_: e_.reciprocal(rc, ov[:, :, 8]), a)
                    dst = osb[:, q, :].rearrange("p (c d) -> p c d", d=8) if kind == 0 else osb[:, :, q * 8:q * 8 + 8]
                    T["norm", q] = tt(dst, ov[:, :, 0:8], rc.unsqueeze(2).to_broadcast([128, 16, 8]), ALU.mult, a, eng=PO)

            def out_a(c, ring):
                oT, of, oi = otr.next()
                p, pf, pi = ring.next()
                for j in range(4):
                    a = tp(p[:, j * 128:(j + 1) * 128], osb[:, 4 * c + j, :], [T["norm", q] for q in range(16) if ("norm", q) in T],
                           pf, inc=(j == 3))
                return oT, of, oi, p, pi, a

            def project(oT, t_o, c, ring):
                p, pf, pi = ring.next()
                for j in range(4):
                    a = mm(p[:, j * 128:(j + 1) * 128], oT[:, j * 128:(j + 1) * 128], wo, t_o, pf, inc=(j == 3))
                t_p = a
                xc = x[:, 4 * c:4 * c + 4, :]
                a = tt(xc, xc, p[:, :].rearrange("p (t n) -> p t n", t=4), ALU.add, a)
                ring.free[pi] = [a]
                if kind == 0:
                    a = tt(xc, xc, bub.unsqueeze(1).to_broadcast([128, 4, 128]), ALU.add, a)
                finish(c, a, ring)
                return t_p

            def chunk_out(c, ring):
                oT, of, oi, p, pi, a = out_a(c, ring)
                a = acopy(oT, p[:, :], a, of)
                ring.free[pi] = [a]
                otr.free[oi] = [project(oT, a, c, ring)]

            prefetch()
            AHEAD = 15

            def ahead(n):
                if n < 128:
                    stage_a(n // 8, n % 8)
                    if n % 8 == 7:
                        split(n // 8)

            for n in range(AHEAD):
                ahead(n)
                if 8 <= n < 12:
                    place(0, n - 8)
            if kind == 0:
                values(0)
            for n in range(128):
                q, u = n // 8, n % 8
                if n % 32 == 16 and n // 32 + 1 < 4:
                    order_keys(n // 32 + 1)
                stage_b(q, u)
                ahead(n + AHEAD)
                if u in (0, 2) and q > 0:
                    stage_o(q - 1, 2 + (0, 2).index(u))
                if u in (1, 3, 5, 7) and q + 1 < 16:
                    place(q + 1, (1, 3, 5, 7).index(u))
                if u == 3 and kind == 0 and q >= 4 and q % 4 == 0:
                    chunk_out(q // 4 - 1, misc)
                if u in (4, 6):
                    stage_o(q, (4, 6).index(u))
                if u == 6 and q + 1 < 16 and kind == 0:
                    values(q + 1)
            stage_o(15, 2)
            stage_o(15, 3)
            rb = Ring(bank[0:4])
            for i in range(4):
                rb.free[i] = [T["norm", 15], T["e", 15, 7][2], T["max", 15, 7]]
            if kind == 0:
                chunk_out(3, rb)
            else:
                oT = ebuf[:, 0:2048]
                tt_ = []
                for c in range(CHUNKS):
                    _, _, _, p, pi, a = out_a(c, rb)
                    dst = oT.rearrange("p (b u t) -> p u b t", b=4, u=16)[:, 4 * c:4 * c + 4, :, :]
                    src = p[:, :].rearrange("p (u b t) -> p u b t", u=4, b=4)
                    a = acopy(dst, src, a)
                    rb.free[pi] = [a]
                    tt_.append(a)
                for c in range(CHUNKS):
                    project(oT[:, c * 512:(c + 1) * 512], tt_, c, rb)

        PRE = [pre_l0, lambda w: pre_attention(0, w), pre_l0, pre_l1, pre_l1_attn, pre_l1, pre_l2, pre_l2_attn, pre_l2,
               pre_l3, lambda w: pre_attention(3, w), pre_l3]
        stages = [l0_ffn, lambda: attention(0), l0_ffn, l1_ffn, l1_attn, l1_ffn, l2_ffn, l2_attn, l2_ffn,
                  l3_ffn, lambda: attention(3), l3_ffn]
        if 9 in LAYERS or 11 in LAYERS:
            zz = take(3840)
            z = mset(zz, 0.0, eng=PO)
            dma(ins["sorted_x"].rearrange("(i p) n -> p i n", p=128), zz.rearrange("p (i n) -> p i n", n=128), z)
        first = Ring(bank[4:8])
        S["feat"] = LAYERS[0] != 4
        S["next"] = LAYERS[0]
        prefetch()
        for c in range(CHUNKS):
            finish(c, t_x[c], first)
        for n in LAYERS:
            S["next"] = n + 1 if n + 1 in LAYERS else None
            S["last"] = n == LAYERS[-1]
            S["feat"] = n != 3
            stages[n]()
        SP.stop_until(S["out"])

        block = ctx.enter_context(nc.Block())

        @block.sync
        def _(e):
            SP.flush(e)

        @block.gpsimd
        def _(e):
            PO.flush(e)

        @block.scalar
        def _(e):
            AC.flush(e)

        @block.vector
        def _(e):
            DV.flush(e)

        @block.tensor
        def _(e):
            PE.flush(e)


def constants():
    f, b = {}, {}
    r = np.arange(128)
    f["ident"] = np.eye(128)
    f["iota"] = np.tile(np.arange(512), (128, 1))
    f["mhalf"] = np.full((128, 16), -0.5)
    f["ridx"] = np.tile(8 - np.arange(8), (128, 16))
    g, e = np.arange(16)[:, None] // 2, np.arange(8)[None, :]
    f["coff"] = np.tile(((e // 2) * 128 + ((e % 2) ^ (g % 2)) * 64 + 1).reshape(1, 128), (128, 1))
    f["onesrow"] = np.ones((128, 512))
    f["scanreset"] = np.tile((np.arange(128) % 16 != 0), (128, 1))
    f["k256"] = np.tile(256 * np.arange(8), (128, 8))
    f["i16"] = np.tile(np.repeat(np.arange(16), 8), (128, 1))
    f["blockdiag"] = (r[:, None] // 8 == r[None, :] // 8)
    b["ident"] = np.eye(128)
    b["tri"] = r[:, None] < r[None, :]
    b["ones"] = np.ones((128, 128))
    s = np.zeros((128, 32))
    for part in range(3):
        for d in range(8):
            s[part * 8 + d, d] = 1
    s[96, 8] = 1
    b["sel"] = s

    def pack(d):
        at, o = {}, 0
        for k, v in d.items():
            at[k] = (o, o + v.shape[1])
            o += v.shape[1]
        return np.concatenate([np.asarray(v, np.float32) for v in d.values()], 1).astype(np.float32), at

    return pack(f), pack(b)


def key_rows(blocks):
    z = np.zeros((24 + 3 * blocks, 8192), np.uint16)
    for part in range(3):
        for kb in range(blocks):
            z[24 + part * blocks + kb, (np.arange(8192) % 512) // (512 // blocks) == kb] = 0x3F80
    return z.view(np.float32)


(CONST_F, CF_AT), (CONST_B, CB_AT) = constants()

_INS = ["L0_attn_x", "L0_attn_bq", "L0_attn_bu", "L0_ffn_router_w", "L0_ffn_w0_kernel", "L0_ffn_w1_kernel",
        "L0_ffn_wo_kernel", "L1_attn_bk", "L1_attn_bka", "L1_attn_bv", "L1_attn_gamma", "L1_attn_beta",
        "L1_ffn_w3_s",
        "L2_attn_bq", "L2_attn_bk", "L2_attn_bv", "L2_attn_bo",
        "L2_ffn_Wr", "L2_ffn_br", "L2_ffn_W_up", "L2_ffn_W_down", "L2_ffn_b_down",
        "L3_attn_w_q", "L3_attn_w_k", "L3_attn_w_v", "L3_attn_w_o",
        "L3_ffn_Wr", "L3_ffn_br", "L3_ffn_W1", "L3_ffn_W2", "L3_ffn_W3", "L3_ffn_b3"]
_TRANSPOSED = {"wqT0": "L0_attn_wq", "wuT0": "L0_attn_wu", "WkT1": "L1_attn_Wk", "WkaT1": "L1_attn_Wka",
               "WvT1": "L1_attn_Wv", "w1T": "L1_ffn_w1_w", "w2T": "L1_ffn_w2_w", "h1T": "L1_ffn_h1_w",
               "h2T": "L1_ffn_h2_w", "w3T": "L1_ffn_w3_w", "WqT2": "L2_attn_Wq", "WkT2": "L2_attn_Wk",
               "WvT2": "L2_attn_Wv", "WoT2": "L2_attn_Wo"}


def kernel(**inputs):
    import concourse.bacc as _bacc
    from concourse.bass_utils import run_bass_kernel_spmd as _run

    nc = _bacc.Bacc("TRN2", target_bir_lowering=False, num_devices=1)
    arrays = {n: np.ascontiguousarray(inputs[n]) for n in _INS}
    for n, src in _TRANSPOSED.items():
        arrays[n] = np.ascontiguousarray(np.transpose(inputs[src]))
    for n in ("w1_s", "w2_s", "h1_s", "h2_s"):
        arrays[n] = np.ascontiguousarray(np.reshape(inputs["L1_ffn_" + n], (4, 128)).T)
    bup = np.zeros((128, 4, 3), np.float32)
    for f, (f0, fn) in enumerate(L2T):
        bup[0:fn, :, f] = np.transpose(inputs["L2_ffn_b_up"][:, f0:f0 + fn])
    arrays["bup"] = bup
    arrays["b12c"] = np.ascontiguousarray(np.concatenate(
        [np.transpose(np.reshape(inputs["L3_ffn_" + n], (8, -1, 128)), (0, 2, 1)) for n in ("b1", "b2")], 2))
    arrays["key_rows0"], arrays["key_rows3"] = key_rows(1), key_rows(4)
    arrays["const_f"], arrays["const_b"] = CONST_F, CONST_B
    ins = {n: nc.dram_tensor(f"in_{n}", a.shape, mybir.dt.from_np(a.dtype), kind="ExternalInput").ap()
           for n, a in arrays.items()}
    ins["scratch"] = nc.dram_tensor("scratch", (2, 16, 24, 2048), BF16, kind="Internal").ap()
    ins["sorted_x"] = nc.dram_tensor("sorted_x", (3840, 128), F32, kind="Internal").ap()
    ins["sorted_y"] = nc.dram_tensor("sorted_y", (3840, 128), F32, kind="Internal").ap()
    out = nc.dram_tensor("out_0", (4, 512, 128), F32, kind="ExternalOutput").ap()
    build(nc, ins, out)
    r = _run(nc, [{f"in_{n}": a for n, a in arrays.items()}], core_ids=[0])
    return r.results[0]["out_0"]
```
